# Optimizing a Trainium2 kernel written in Bass

```python
import numpy as np
import jax
import jax.numpy as jnp

def _softmax(x, axis=-1):
    return jax.nn.softmax(x, axis=axis)

def _gelu(x):
    return jax.nn.gelu(x, approximate=True)

def _silu(x):
    return jax.nn.silu(x)

def _sigmoid(x):
    return jax.nn.sigmoid(x)

def _layernorm(x, axis=-1, eps=1e-05):
    m = jnp.mean(x, axis=axis, keepdims=True)
    v = jnp.var(x, axis=axis, keepdims=True)
    return (x - m) / jnp.sqrt(v + eps)

def _scatter_add(tgt, idx, src, axis=0):
    return tgt.at[idx].add(src)

def _segment_sum(src, seg, n):
    return jax.ops.segment_sum(src, seg, n)
kernel_name = 'mk_sandwich_d1_jaxref_r8_2a0493'

def setup_inputs(seed: int=0):
    np.random.seed(seed)
    _w = jnp.asarray

    def _L0_attn_setup():
        import jax, jax.numpy as jnp
        import numpy as np
        B, N, E = (2, 256, 256)
        H, D = (16, 128)
        BASE = 10000.0

        def rope(t, offset=0):
            d = t.shape[-1]
            pos = jnp.arange(t.shape[1], dtype=jnp.float32) + offset
            inv = BASE ** (-jnp.arange(0, d, 2, dtype=jnp.float32) / d)
            ang = pos[:, None] * inv[None, :]
            cos = jnp.cos(ang)[None, :, None, :]
            sin = jnp.sin(ang)[None, :, None, :]
            t1, t2 = (t[..., :d // 2], t[..., d // 2:])
            return jnp.concatenate([t1 * cos - t2 * sin, t2 * cos + t1 * sin], axis=-1)
        key = jax.random.key(seed)
        ks = jax.random.split(key, 6)
        s = lambda k, shape, fan: jax.random.normal(k, shape, jnp.float32) / np.sqrt(fan)
        return {'x': jax.random.normal(ks[0], (B, N, E), jnp.float32), 'Wq': s(ks[1], (H * D, E), E), 'Wkv': s(ks[2], (2 * D, E), E), 'Wkvh': s(ks[3], (2 * H, E), E), 'Wg': s(ks[4], (2 * H, E), E), 'Wout': s(ks[5], (E, H * D), H * D)}
    _L0_attn_in = _L0_attn_setup()

    def _L0_ffn_setup():
        import jax, jax.numpy as jnp
        import numpy as np
        B, S, D = (4, 512, 256)
        E, K, I, J = (8, 2, 176, 704)
        CAP_FACTOR = 1.25
        STD = 0.02

        def _moe_routed(x_flat, router, w_up_gate, w_down):
            T, d = x_flat.shape
            logits = jnp.einsum('td,de->te', x_flat, router)
            topk_logits, sel = jax.lax.top_k(logits, K)
            cw = jax.nn.softmax(topk_logits, axis=-1).astype(x_flat.dtype)
            C = int(np.ceil(T * K / E * CAP_FACTOR))
            e_flat = sel.reshape(-1)
            oh = jax.nn.one_hot(e_flat, E, dtype=jnp.int32)
            pos_all = jnp.cumsum(oh, axis=0) - oh
            pos = jnp.take_along_axis(pos_all, e_flat[:, None], axis=1)[:, 0]
            valid = pos < C
            safe_pos = jnp.where(valid, pos, C)
            tok = jnp.repeat(jnp.arange(T), K)
            buf = jnp.zeros((E, C, d), x_flat.dtype).at[e_flat, safe_pos].set(x_flat[tok], mode='drop')
            gate_up = jnp.einsum('ecd,edm->ecm', buf, w_up_gate)
            gate, up = jnp.split(gate_up, [I], axis=-1)
            h = jax.nn.silu(gate) * up
            out_buf = jnp.einsum('eci,eid->ecd', h, w_down)
            gathered = out_buf[e_flat, jnp.minimum(safe_pos, C - 1)]
            gathered = gathered * valid[:, None].astype(x_flat.dtype)
            w = cw.reshape(-1)
            y = jnp.zeros((T, d), x_flat.dtype).at[tok].add(w[:, None] * gathered)
            return y

        def _shared_mlp(x_flat, shared_w_up_gate, shared_w_down):
            gu = jnp.einsum('td,dm->tm', x_flat, shared_w_up_gate)
            gate, up = jnp.split(gu, [J], axis=-1)
            return jnp.einsum('tm,md->td', jax.nn.silu(gate) * up, shared_w_down)
        key = jax.random.key(seed)
        kx, kr, ku, kd, ksu, ksd = jax.random.split(key, 6)
        x = jax.random.normal(kx, (B, S, D), dtype=jnp.float32)
        router = STD * jax.random.truncated_normal(kr, -3, 3, (D, E), dtype=jnp.float32)
        w_up_gate = STD * jax.random.truncated_normal(ku, -3, 3, (E, D, 2 * I), dtype=jnp.float32)
        w_down = STD * jax.random.truncated_normal(kd, -3, 3, (E, I, D), dtype=jnp.float32)
        shared_w_up_gate = STD * jax.random.truncated_normal(ksu, -3, 3, (D, 2 * J), dtype=jnp.float32)
        shared_w_down = STD * jax.random.truncated_normal(ksd, -3, 3, (J, D), dtype=jnp.float32)
        return {'x': x, 'router': router, 'w_up_gate': w_up_gate, 'w_down': w_down, 'shared_w_up_gate': shared_w_up_gate, 'shared_w_down': shared_w_down}
    _L0_ffn_in = _L0_ffn_setup()
    _d = {'L0_attn_x': _L0_attn_in['x'], 'L0_attn_Wq': _L0_attn_in['Wq'], 'L0_attn_Wkv': _L0_attn_in['Wkv'], 'L0_attn_Wkvh': _L0_attn_in['Wkvh'], 'L0_attn_Wg': _L0_attn_in['Wg'], 'L0_attn_Wout': _L0_attn_in['Wout'], 'L0_ffn_router': _L0_ffn_in['router'], 'L0_ffn_w_up_gate': _L0_ffn_in['w_up_gate'], 'L0_ffn_w_down': _L0_ffn_in['w_down'], 'L0_ffn_shared_w_up_gate': _L0_ffn_in['shared_w_up_gate'], 'L0_ffn_shared_w_down': _L0_ffn_in['shared_w_down']}
    _x0 = _d['L0_attn_x']
    _d['L0_attn_x'] = jax.random.normal(jax.random.fold_in(jax.random.key(seed), 1), (4, 512, 256), dtype=_x0.dtype)
    del _x0
    return _d

def reference(L0_attn_x, L0_attn_Wq, L0_attn_Wkv, L0_attn_Wkvh, L0_attn_Wg, L0_attn_Wout, L0_ffn_router, L0_ffn_w_up_gate, L0_ffn_w_down, L0_ffn_shared_w_up_gate, L0_ffn_shared_w_down):

    def _L0_attn_ref(x, Wq, Wkv, Wkvh, Wg, Wout):
        import jax, jax.numpy as jnp
        import numpy as np
        B, N, E = (2, 256, 256)
        H, D = (16, 128)
        BASE = 10000.0

        def rope(t, offset=0):
            d = t.shape[-1]
            pos = jnp.arange(t.shape[1], dtype=jnp.float32) + offset
            inv = BASE ** (-jnp.arange(0, d, 2, dtype=jnp.float32) / d)
            ang = pos[:, None] * inv[None, :]
            cos = jnp.cos(ang)[None, :, None, :]
            sin = jnp.sin(ang)[None, :, None, :]
            t1, t2 = (t[..., :d // 2], t[..., d // 2:])
            return jnp.concatenate([t1 * cos - t2 * sin, t2 * cos + t1 * sin], axis=-1)
        b, n, _ = x.shape
        q = (x @ Wq.T).reshape(b, n, H, D)
        kv = x @ Wkv.T
        kv_head = x @ Wkvh.T
        g = x @ Wg.T
        log_f = jnp.concatenate([jnp.zeros((b, 1, 2 * H), jnp.float32), jax.nn.log_sigmoid(g)], axis=1)
        log_f_cumsum = jnp.cumsum(log_f, axis=1)[:, :-1]
        kv_head = kv_head * jnp.exp(log_f_cumsum)
        kv_head = jnp.cumsum(kv_head, axis=1)
        kp, vp = (kv[..., :D], kv[..., D:])
        kh, vh = (kv_head[..., :H], kv_head[..., H:])
        k = jnp.einsum('bnd,bnh->bnhd', kp, kh)
        v = jnp.einsum('bnd,bnh->bnhd', vp, vh)
        q = rope(q)
        k = rope(k)
        scale = 1.0 / np.sqrt(D)
        scores = jnp.einsum('bnhd,bmhd->bhnm', q, k) * scale
        mask = jnp.tril(jnp.ones((n, n), bool))
        scores = jnp.where(mask[None, None], scores, -jnp.inf)
        p = jax.nn.softmax(scores, axis=-1)
        o = jnp.einsum('bhnm,bmhd->bnhd', p, v).reshape(b, n, H * D)
        return o @ Wout.T

    def _L0_ffn_ref(x, router, w_up_gate, w_down, shared_w_up_gate, shared_w_down):
        import jax, jax.numpy as jnp
        import numpy as np
        B, S, D = (4, 512, 256)
        E, K, I, J = (8, 2, 176, 704)
        CAP_FACTOR = 1.25
        STD = 0.02

        def _moe_routed(x_flat, router, w_up_gate, w_down):
            T, d = x_flat.shape
            logits = jnp.einsum('td,de->te', x_flat, router)
            topk_logits, sel = jax.lax.top_k(logits, K)
            cw = jax.nn.softmax(topk_logits, axis=-1).astype(x_flat.dtype)
            C = int(np.ceil(T * K / E * CAP_FACTOR))
            e_flat = sel.reshape(-1)
            oh = jax.nn.one_hot(e_flat, E, dtype=jnp.int32)
            pos_all = jnp.cumsum(oh, axis=0) - oh
            pos = jnp.take_along_axis(pos_all, e_flat[:, None], axis=1)[:, 0]
            valid = pos < C
            safe_pos = jnp.where(valid, pos, C)
            tok = jnp.repeat(jnp.arange(T), K)
            buf = jnp.zeros((E, C, d), x_flat.dtype).at[e_flat, safe_pos].set(x_flat[tok], mode='drop')
            gate_up = jnp.einsum('ecd,edm->ecm', buf, w_up_gate)
            gate, up = jnp.split(gate_up, [I], axis=-1)
            h = jax.nn.silu(gate) * up
            out_buf = jnp.einsum('eci,eid->ecd', h, w_down)
            gathered = out_buf[e_flat, jnp.minimum(safe_pos, C - 1)]
            gathered = gathered * valid[:, None].astype(x_flat.dtype)
            w = cw.reshape(-1)
            y = jnp.zeros((T, d), x_flat.dtype).at[tok].add(w[:, None] * gathered)
            return y

        def _shared_mlp(x_flat, shared_w_up_gate, shared_w_down):
            gu = jnp.einsum('td,dm->tm', x_flat, shared_w_up_gate)
            gate, up = jnp.split(gu, [J], axis=-1)
            return jnp.einsum('tm,md->td', jax.nn.silu(gate) * up, shared_w_down)
        b, s, d = x.shape
        x_flat = x.reshape(b * s, d)
        routed = _moe_routed(x_flat, router, w_up_gate, w_down)
        shared = _shared_mlp(x_flat, shared_w_up_gate, shared_w_down)
        return (routed + shared).reshape(b, s, d)
    x = L0_attn_x
    x = x + _layernorm(_L0_attn_ref(_layernorm(x, axis=-1), L0_attn_Wq, L0_attn_Wkv, L0_attn_Wkvh, L0_attn_Wg, L0_attn_Wout), axis=-1)
    x = x + _layernorm(_L0_ffn_ref(_layernorm(x, axis=-1), L0_ffn_router, L0_ffn_w_up_gate, L0_ffn_w_down, L0_ffn_shared_w_up_gate, L0_ffn_shared_w_down), axis=-1)
    return x

_drawn_inputs = setup_inputs


def setup_inputs(seed=0):
    import zlib

    import numpy as np

    out = dict(_drawn_inputs(seed))
    spreads = {}
    factors = {}
    for name, (base, spread) in spreads.items():
        noise = np.random.default_rng([zlib.crc32(name.encode()), seed]).standard_normal(out[name].shape)
        drawn = base * np.exp(spread * noise) if base else spread * noise
        out[name] = jnp.asarray(drawn.astype(out[name].dtype))
    for name, factor in factors.items():
        out[name] = (out[name] * factor).astype(out[name].dtype)
    return out
```

```python
from contextlib import ExitStack

import numpy as np

import concourse.bass as bass
from concourse import mybir

F32 = mybir.dt.float32
F32R = mybir.dt.float32r
BF16 = mybir.dt.bfloat16
U32 = mybir.dt.uint32
ALU = mybir.AluOpType
ACT = mybir.ActivationFunctionType
AX = mybir.AxisListType

P = 128
EPS = 1e-5

NT = 4
ROW_AT = [0, 128, 384, 768]
COL_AT = [0, 512, 896, 1152]
PACKED = 1280
S_BANKS = [[3], [2, 0], [1]]
PT_BANKS = [[0], [1, 3], [2]]


def s_slot(nt):
    return {3: (0, 0), 2: (1, 0), 0: (1, 384), 1: (2, 0)}[nt]


def pt_slot(mt):
    return {0: (0, 0), 1: (1, 0), 3: (1, 384), 2: (2, 0)}[mt]


def decoder_layer(nc, x, wq, w0, wout, cos_t, sin_t, ident, causal, before, iota8,
                  router, w_up, w_dn, w_dn2, out, dims):
    B, SEQ, H, D, E, NE, NPE, CAP, HID = dims
    T = B * SEQ
    TILES = T // P
    TPB = SEQ // P
    EO = E // P
    UNITS = H * B
    HG = H // 2
    H2 = HID - P
    UPW = 3 * P - (P - 64 - H2)
    SCALE = float(1.0 / np.sqrt(D))

    kvh_dram = nc.dram_tensor("kvh_rows", [B * 2 * H, SEQ], F32).ap()
    x_v = x.rearrange("(b t p) e -> b p t e", p=P, t=TPB)
    out_v = out.rearrange("(b t p) e -> b p t e", p=P, t=TPB)

    with ExitStack() as ctx:
        def sb(name, shape, dt=F32):
            return ctx.enter_context(nc.sbuf_tensor(name, shape, dt))

        def sem(name):
            return ctx.enter_context(nc.semaphore(name))

        ps = [ctx.enter_context(nc.psum_tensor(f"ps{i}", [P, 512], F32)) for i in range(8)]
        ps_q, ps_s, ps_pt, ps_o = ps[0], ps[1:4], ps[4:7], ps[7]

        x_sb = sb("x_sb", [P, TILES, E])
        xt_hi = sb("xt_hi", [P, EO, T], F32R)
        xt_lo = sb("xt_lo", [P, EO, T], F32R)
        y_sb = sb("y_sb", [P, TILES, E])
        id_f = sb("id_f", [P, P])
        stats = sb("stats", [P, TILES, 6])
        mv = sb("mv", [P, TILES, 2])
        eps_sb = sb("eps_sb", [P, 1])
        std = sb("std", [P, TILES])
        rstd = sb("rstd", [P, TILES])
        cos_sb = sb("cos_sb", [P, SEQ])
        sin_sb = sb("sin_sb", [P, SEQ])
        id_b = sb("id_b", [P, P], BF16)
        causal_b = sb("causal_b", [P, P], BF16)
        kt = sb("kt", [P, T])
        vp = sb("vp", [P, TILES, D])
        vcol = sb("vcol", [P, TPB, B * 2 * H])
        wo_sb = sb("wo_sb", [P, HG, E])
        wq_raw = sb("wq_raw", [P, EO, D])
        wq_hi = sb("wq_hi", [P, EO, D], F32R)
        wq_lo = sb("wq_lo", [P, EO, D], F32R)
        q_sw = sb("q_sw", [P, SEQ])
        q_cos = sb("q_cos", [P, SEQ])
        q_sin = sb("q_sin", [P, SEQ])
        q_rot = sb("q_rot", [P, 2, SEQ])
        kh_row = sb("kh_row", [P, 2, SEQ])
        k_h = sb("k_h", [P, 2, SEQ])
        prob = sb("prob", [P, 2, PACKED])
        prob_t = sb("prob_t", [P, PACKED])
        neg_max = sb("neg_max", [P, 2, NT])
        row_sum = sb("row_sum", [P, 2, NT])
        row_inv = sb("row_inv", [P, 2, NT])
        arena = sb("arena", [P, HG * T])
        o_t = arena[:, :].rearrange("p (h t) -> p h t", h=HG)

        cut = [0]

        def piece(n):
            cut[0] += n
            return arena[:, cut[0] - n:cut[0]]

        xn = piece(2 * TPB * E).rearrange("p (r t e) -> p r t e", r=2, t=TPB)
        f_t, kvh_t, fcum_t, hc_t, ones_t = (piece(SEQ) for _ in range(5))
        causal_f = piece(P)
        w0_raw = piece(EO * 3 * P).rearrange("p (o n) -> p o n", o=EO)
        w_hi = sb("w_hi", [P, EO, 3 * P], F32R)
        w_lo = sb("w_lo", [P, EO, 3 * P], F32R)

        cut[0] = 0
        dn_sb = piece(NPE * E).rearrange("p (n e) -> p n e", n=NPE)
        dn2_sb = piece(NPE * E).rearrange("p (n e) -> p n e", n=NPE)
        up_raw = piece(EO * UPW).rearrange("p (o n) -> p o n", o=EO)
        sg = piece(2 * SEQ).rearrange("p (r n) -> p r n", r=2)
        sg2 = piece(2 * SEQ).rearrange("p (r n) -> p r n", r=2)
        hid = piece(2 * SEQ).rearrange("p (r n) -> p r n", r=2)
        hid2 = piece(2 * SEQ).rearrange("p (r n) -> p r n", r=2)
        y_n = q_sw[:, :].rearrange("p (r e) -> p r e", r=2)
        xn2 = prob[:, 0, 0:TPB * E].rearrange("p (t e) -> p t e", t=TPB)
        up_hi, up_lo = w_hi[:, :, 0:UPW], w_lo[:, :, 0:UPW]
        rt_raw = sb("rt_raw", [P, EO, NE])
        rt_hi = sb("rt_hi", [P, EO, NE], F32R)
        rt_lo = sb("rt_lo", [P, EO, NE], F32R)
        before_f = piece(P)
        before_b = sb("before_b", [P, P], BF16)
        ones_b = sb("ones_b", [P, P], BF16)
        iota_sb = sb("iota_sb", [P, NE])
        logit = piece(TILES * NE).rearrange("p (t e) -> p t e", t=TILES)
        top = piece(TILES * 8).rearrange("p (t e) -> p t e", t=TILES)
        top_at = piece(TILES * 8).bitcast(U32).rearrange("p (t e) -> p t e", t=TILES)
        top_f = piece(TILES * 8).rearrange("p (t e) -> p t e", t=TILES)
        oh = piece(2 * TILES * NE).rearrange("p (k t e) -> p k t e", k=2, t=TILES)
        chosen = sb("chosen", [P, TILES, NE], BF16)
        fits = piece(TILES * NE).rearrange("p (t e) -> p t e", t=TILES)
        gap = sb("gap", [P, TILES])
        egap = sb("egap", [P, TILES])
        den = sb("den", [P, TILES])
        cw = sb("cw", [P, 2, TILES])
        weight = sb("weight", [P, TILES, NPE])

        consts_in, w0_in, wo_in = sem("consts_in"), sem("w0_in"), sem("wo_in")
        x_in = [sem(f"x_in{b}") for b in range(B)]
        wq_in = sem("wq_in")
        kh_row_in = [sem(f"kh_row_in{r}") for r in range(2)]
        kvh_stored = sem("kvh_stored")
        dve_c = sem("dve_c")
        w0_split, consts_made = sem("w0_split"), sem("consts_made")
        var_ready, std_ready, xn_ready = sem("var_ready"), sem("std_ready"), sem("xn_ready")
        xt_psum, xt_hi_ready, xt_lo_ready = sem("xt_psum"), sem("xt_hi_ready"), sem("xt_lo_ready")
        k_psum, k_swapped, k_cos_ready, k_sin_ready, kt_ready = (
            sem("k_psum"), sem("k_swapped"), sem("k_cos_ready"), sem("k_sin_ready"), sem("kt_ready"))
        gate_psum, gate_copied, v_psum, v_ready = sem("gate_psum"), sem("gate_copied"), sem("v_psum"), sem("v_ready")
        f_ready, hc_ready, vcol_psum, vcol_ready = sem("f_ready"), sem("hc_ready"), sem("vcol_psum"), sem("vcol_ready")
        wq_hi_ready, wq_ready = sem("wq_hi_ready"), sem("wq_ready")
        q_psum, q_swapped, q_cos_ready, q_sin_ready, q_ready = (
            sem("q_psum"), sem("q_swapped"), sem("q_cos_ready"), sem("q_sin_ready"), sem("q_ready"))
        kh_ready = sem("kh_ready")
        s_psum, max_ready, exp_ready, inv_ready, prob_ready = (
            sem("s_psum"), sem("max_ready"), sem("exp_ready"), sem("inv_ready"), sem("prob_ready"))
        pt_psum, pt_free, pt_ready = sem("pt_psum"), sem("pt_free"), sem("pt_ready")
        o_psum, o_free, o_ready = sem("o_psum"), sem("o_free"), sem("o_ready")
        proj_psum, proj_taken = sem("proj_psum"), sem("proj_taken")
        xt2_psum, xt2_hi, xt2_lo = sem("xt2_psum"), sem("xt2_hi"), sem("xt2_lo")
        var2_ready, std2_ready, xn2_ready = sem("var2_ready"), sem("std2_ready"), sem("xn2_ready")
        dn_in, up_in, up_ready, up_hi_ready = sem("dn_in"), sem("up_in"), sem("up_ready"), sem("up_hi_ready")
        logit_psum, gap_ready, egap_ready = sem("logit_psum"), sem("gap_ready"), sem("egap_ready")
        chosen_ready, pos_psum, weight_ready = sem("chosen_ready"), sem("pos_psum"), sem("weight_ready")
        gu_psum, silu_ready, gu_free, hid_ready = sem("gu_psum"), sem("silu_ready"), sem("gu_free"), sem("hid_ready")
        y_psum, y_taken = sem("y_psum"), sem("y_taken")
        out_ready, stored = sem("out_ready"), sem("stored")

        def tok(b):
            return slice(b * SEQ, (b + 1) * SEQ)

        def three_pass(pe, psum, w_hi, w_lo, m_hi, m_lo):
            for o in range(EO):
                for j, (w, m) in enumerate(((w_hi, m_hi), (w_hi, m_lo), (w_lo, m_hi))):
                    last = pe.matmul(psum, w(o), m(o), start=(o == 0 and j == 0),
                                     stop=(o == EO - 1 and j == 2))
            return last

        block = ctx.enter_context(nc.Block())

        @block.sync
        def _(sp):
            sp.dma_start(x_sb[:, 0:TPB, :], x_v[0]).then_inc(x_in[0], 16)
            sp.dma_start(id_f[:], ident).then_inc(consts_in, 16)
            sp.dma_start(w0_raw, w0).then_inc(w0_in, 16)
            for b in range(1, B):
                sp.dma_start(x_sb[:, b * TPB:(b + 1) * TPB, :], x_v[b]).then_inc(x_in[b], 16)
            sp.dma_start(causal_f, causal).then_inc(consts_in, 16)
            sp.dma_start(iota_sb[:], iota8).then_inc(consts_in, 16)
            sp.dma_start(rt_raw[:], router).then_inc(consts_in, 16)
            sp.dma_start(wo_sb[:], wout[:, 0:HG, :]).then_inc(wo_in, 16)
            sp.wait_ge(hc_ready, 1)
            sp.dma_start(kvh_dram, hc_t).then_inc(kvh_stored, 16)
            sp.wait_ge(kvh_stored, 16)
            for i in range(2):
                sp.dma_start(kh_row[:, i, :], kvh_dram[i * 2 * H:i * 2 * H + 1, :].to_broadcast([P, SEQ])) \
                    .then_inc(kh_row_in[i], 16)

            def steps(h, last):
                for b in range(B):
                    if b == 0 and not last:
                        sp.wait_ge(wq_ready, h + 1)
                        sp.dma_start(wq_raw[:], wq[bass.ds(h + 1, 1), :, :, :].rearrange("h p o d -> (h p) o d")) \
                            .then_inc(wq_in, 16)
                    if last and b + 2 >= B:
                        continue
                    b2, h2 = (b + 2) % B, h + (b + 2) // B
                    sp.wait_ge(kh_ready, h * B + b + 1)
                    sp.dma_start(kh_row[:, b % 2, :],
                                 kvh_dram[bass.ds(h2 + 2 * H * b2, 1), :].to_broadcast([P, SEQ])) \
                        .then_inc(kh_row_in[b % 2], 16)

            with sp.Fori(0, HG) as h:
                steps(h, False)
            sp.wait_ge(proj_psum, TILES)
            sp.dma_start(wo_sb[:], wout[:, HG:H, :]).then_inc(wo_in, 16)
            with sp.Fori(HG, H - 1) as h:
                steps(h, False)
            steps(H - 1, True)

            sp.wait_ge(proj_psum, 2 * TILES)
            sp.dma_start(up_raw, w_up[0]).then_inc(up_in, 16)
            sp.dma_start(before_f, before).then_inc(dn_in, 16)
            sp.dma_start(dn_sb, w_dn).then_inc(dn_in, 16)
            sp.dma_start(dn2_sb[0:H2, :, :], w_dn2).then_inc(dn_in, 16)
            with sp.Fori(0, NPE - 1) as e:
                sp.wait_ge(up_ready, e + 1)
                sp.dma_start(up_raw, w_up[bass.ds(e + 1, 1), :, :, :].rearrange("n p o c -> (n p) o c")) \
                    .then_inc(up_in, 16)
            for b in range(B):
                sp.wait_ge(out_ready, (b + 1) * TPB)
                sp.dma_start(out_v[b], y_sb[:, b * TPB:(b + 1) * TPB, :]).then_inc(stored, 16)
            sp.wait_ge(stored, 16 * B)

        @block.scalar
        def _(act):
            act.dma_start(cos_sb[:], cos_t).then_inc(consts_in, 16)
            act.dma_start(sin_sb[:], sin_t).then_inc(consts_in, 16)
            act.dma_start(wq_raw[:], wq[0]).then_inc(wq_in, 16)
            act.wait_ge(consts_in, 6 * 16)
            for b in range(B):
                act.wait_ge(var_ready, (b + 1) * TPB)
                act.activation(std[:, b * TPB:(b + 1) * TPB], mv[:, b * TPB:(b + 1) * TPB, 1], ACT.Sqrt,
                               bias=eps_sb[:, 0:1]).then_inc(std_ready, 1)
                for o in range(EO):
                    act.wait_ge(xt_psum, b * EO + o + 1)
                    act.copy(xt_hi[:, o, tok(b)], ps_pt[o][:]).then_inc(xt_hi_ready, 1)
                act.wait_ge(k_psum, b + 1)
                if b:
                    act.wait_ge(kt_ready, b)
                act.mul(q_sw[0:64, :], ps_q[64:128, :], SCALE)
                act.mul(q_sw[64:128, :], ps_q[0:64, :], SCALE).then_inc(k_swapped, 1)
                act.wait_ge(v_psum, b + 1)
                act.copy(vp[:, b * TPB:(b + 1) * TPB, :], ps_o[:]).then_inc(v_ready, 1)
            act.wait_ge(gate_copied, 2 * B)
            act.activation(f_t, f_t, ACT.Sigmoid).then_inc(f_ready, 1)
            act.wait_ge(vcol_psum, 1)
            act.copy(vcol[:], ps_s[2][:]).then_inc(vcol_ready, 1)

            def swap_q(i):
                act.wait_ge(q_psum, i + 1)
                act.copy(q_sw[0:64, :], ps_q[64:128, :])
                act.copy(q_sw[64:128, :], ps_q[0:64, :]).then_inc(q_swapped, 1)

            def exps(i, r):
                for k, tiles in enumerate(S_BANKS):
                    act.wait_ge(max_ready, 3 * i + (k + 1))
                    for nt in tiles:
                        bank, at = s_slot(nt)
                        w = P * (nt + 1)
                        ins = act.activation(prob[:, r, ROW_AT[nt]:ROW_AT[nt] + w], ps_s[bank][:, at:at + w], ACT.Exp,
                                             bias=neg_max[:, r, nt:nt + 1], accum_out=row_sum[:, r, nt:nt + 1])
                    ins.then_inc(exp_ready, 1)

            act.wait_ge(kt_ready, B)
            for i in range(3):
                if i == 1:
                    exps(0, 0)
                if i:
                    act.wait_ge(q_ready, i)
                swap_q(i)

            def steps(h, slot, last):
                for b in range(B):
                    i = h * B + b
                    if not (last and b + 1 >= B):
                        exps(i + 1, (b + 1) % 2)
                    if not (last and b + 3 >= B):
                        act.wait_ge(q_ready, i + 3)
                        swap_q(i + 3)
                    act.wait_ge(o_psum, i + 1)
                    act.copy(o_t[:, slot, tok(b)] if isinstance(slot, int) else
                             o_t[:, bass.ds(slot, 1), tok(b)].rearrange("p a t -> p (a t)"), ps_o[:]) \
                        .then_inc(o_free, 1)

            with act.Fori(0, HG) as h:
                steps(h, h, False)
            with act.Fori(HG, H - 1) as h:
                steps(h, h - HG, False)
            steps(H - 1, HG - 1, True)

            for b in range(B):
                for k in range(2):
                    act.wait_ge(var2_ready, (2 * b + k + 1) * TPB)
                    act.activation(std[:, b * TPB:(b + 1) * TPB], mv[:, b * TPB:(b + 1) * TPB, 1], ACT.Sqrt,
                                   bias=eps_sb[:, 0:1]).then_inc(std2_ready, 1)
                for o in range(EO):
                    act.wait_ge(xt2_psum, b * EO + o + 1)
                    act.copy(xt_hi[:, o, tok(b)], ps_s[o][:]).then_inc(xt2_hi, 1)
            act.wait_ge(gap_ready, 1)
            act.activation(egap[:], gap[:], ACT.Exp).then_inc(egap_ready, 1)

            with act.Fori(0, NPE) as e:
                for c in range(B):
                    r = c % 2
                    act.wait_ge(gu_psum, 2 * (e * B + c) + 1)
                    act.activation(sg[:, r, :], ps[3 * r][:], ACT.Silu).then_inc(silu_ready, 1)
                    act.wait_ge(gu_psum, 2 * (e * B + c) + 2)
                    act.activation(sg2[0:H2, r, :], ps[3 * r + 2][0:H2, :], ACT.Silu).then_inc(silu_ready, 1)
            for b in range(B):
                act.wait_ge(var2_ready, (2 * B + b + 1) * TPB)
                act.activation(std[:, b * TPB:(b + 1) * TPB], mv[:, b * TPB:(b + 1) * TPB, 1], ACT.Sqrt,
                               bias=eps_sb[:, 0:1]).then_inc(std2_ready, 1)

        @block.tensor
        def _(pe):
            pe.wait_ge(consts_in, 6 * 16)
            for b in range(B):
                pe.wait_ge(xn_ready, (b + 1) * TPB)
                if b:
                    pe.wait_ge(xt_lo_ready, b * EO)
                for o in range(EO):
                    for t in range(TPB):
                        ins = pe.transpose(ps_pt[o][:, t * P:(t + 1) * P], xn[:, b % 2, t, o * P:(o + 1) * P], id_f[:])
                    ins.then_inc(xt_psum, 1)
                pe.wait_ge(w0_split, 1)
                pe.wait_ge(xt_lo_ready, (b + 1) * EO)
                if b:
                    pe.wait_ge(k_cos_ready, b)
                three_pass(pe, ps_q[:], lambda o: w_hi[:, o, 0:P], lambda o: w_lo[:, o, 0:P],
                           lambda o: xt_hi[:, o, tok(b)], lambda o: xt_lo[:, o, tok(b)]).then_inc(k_psum, 1)
                if b:
                    pe.wait_ge(gate_copied, 2 * b)
                three_pass(pe, ps_pt[2][:], lambda o: w_hi[:, o, 2 * P:], lambda o: w_lo[:, o, 2 * P:],
                           lambda o: xt_hi[:, o, tok(b)], lambda o: xt_lo[:, o, tok(b)]).then_inc(gate_psum, 1)
                if b:
                    pe.wait_ge(v_ready, b)
                for t in range(TPB):
                    ts = slice(b * SEQ + t * P, b * SEQ + (t + 1) * P)
                    ins = three_pass(pe, ps_o[:, t * P:(t + 1) * P], lambda o: xt_hi[:, o, ts], lambda o: xt_lo[:, o, ts],
                                     lambda o: w_hi[:, o, P:2 * P], lambda o: w_lo[:, o, P:2 * P])
                ins.then_inc(v_psum, 1)

            def q_proj(i, b):
                three_pass(pe, ps_q[:], lambda o: wq_hi[:, o, :], lambda o: wq_lo[:, o, :],
                           lambda o: xt_hi[:, o, tok(b)], lambda o: xt_lo[:, o, tok(b)]).then_inc(q_psum, 1)

            def scores(i, r, first=False):
                pe.wait_ge(q_ready, i + 1)
                pe.wait_ge(kh_ready, i + 1)
                for k, tiles in enumerate(S_BANKS):
                    if not first:
                        pe.wait_ge(exp_ready, 3 * (i - 1) + (k + 1))
                    for nt in tiles:
                        bank, at = s_slot(nt)
                        w = P * (nt + 1)
                        pe.matmul(ps_s[bank][:, at:at + w], q_rot[:, r, nt * P:(nt + 1) * P], k_h[:, r, 0:w],
                                  start=True, stop=False)
                        ins = pe.matmul(ps_s[bank][:, at + w - P:at + w], id_b[:], causal_b[:],
                                        start=False, stop=True)
                    ins.then_inc(s_psum, 1)

            pe.wait_ge(consts_made, 1)
            pe.wait_ge(wq_ready, 1)
            pe.wait_ge(k_cos_ready, B)
            q_proj(0, 0)
            pe.wait_ge(hc_ready, 1)
            for mt in range(TPB):
                ins = pe.transpose(ps_s[2][:, mt * P:(mt + 1) * P], hc_t[:, mt * P:(mt + 1) * P], id_f[:])
            ins.then_inc(vcol_psum, 1)
            pe.wait_ge(q_cos_ready, 1)
            q_proj(1, 1)
            pe.wait_ge(vcol_ready, 1)
            scores(0, 0, first=True)
            pe.wait_ge(q_cos_ready, 2)
            q_proj(2, 2)

            def steps(h, last):
                for b in range(B):
                    i = h * B + b
                    pe.wait_ge(prob_ready, i + 1)
                    pe.wait_ge(pt_free, 3 * i + 3)
                    for tiles in PT_BANKS:
                        for mt in tiles:
                            bank, at = pt_slot(mt)
                            for nt in range(mt, NT):
                                src = ROW_AT[nt] + mt * P
                                dst = at + (nt - mt) * P
                                ins = pe.transpose(ps_pt[bank][:, dst:dst + P], prob[:, b % 2, src:src + P], id_f[:])
                        ins.then_inc(pt_psum, 1)
                    if not (last and b + 1 >= B):
                        scores(i + 1, (b + 1) % 2)
                    if not (last and b + 3 >= B):
                        pe.wait_ge(q_cos_ready, i + 3)
                        if b == 1:
                            pe.wait_ge(wq_ready, h + 2)
                        q_proj(i + 3, (b + 3) % B)
                    pe.wait_ge(o_free, i + 1)
                    for k, tiles in enumerate(PT_BANKS):
                        pe.wait_ge(pt_ready, 3 * i + (k + 1))
                        for mt in tiles:
                            ins = pe.matmul(ps_o[:, mt * P:SEQ], vp[:, b * TPB + mt, :],
                                            prob_t[:, COL_AT[mt]:COL_AT[mt] + SEQ - mt * P],
                                            start=(mt == 0), stop=(mt == 2))
                    ins.then_inc(o_psum, 1)

            def project(g):
                pe.wait_ge(o_free, HG * (g + 1) * B + 1)
                pe.wait_ge(pt_free, 3 * HG * (g + 1) * B + 3)
                for t in range(TILES):
                    if g == 0 and t >= 3:
                        pe.wait_ge(proj_taken, t - 2)
                    if g == 1:
                        pe.wait_ge(proj_taken, TILES + max(t - 2, 0))
                    for hh in range(HG):
                        ins = pe.matmul(ps_pt[t % 3][:, 0:E], o_t[:, hh, t * P:(t + 1) * P], wo_sb[:, hh, :],
                                        start=(hh == 0), stop=(hh == HG - 1))
                    ins.then_inc(proj_psum, 1)
                    if g == 1 and t % TPB == TPB - 1 and t >= TPB:
                        turn(t // TPB - 1)

            def turn(b):
                pe.wait_ge(xn2_ready, (b + 1) * TPB)
                for o in range(EO):
                    if b:
                        pe.wait_ge(xt2_lo, (b - 1) * EO + o + 1)
                    for t in range(TPB):
                        ins = pe.transpose(ps_s[o][:, t * P:(t + 1) * P], xn2[:, t, o * P:(o + 1) * P], id_f[:])
                    ins.then_inc(xt2_psum, 1)

            pe.wait_ge(wo_in, 16)
            with pe.Fori(0, HG) as h:
                steps(h, False)
            project(0)
            pe.wait_ge(proj_taken, TILES)
            with pe.Fori(HG, H - 1) as h:
                steps(h, False)
            steps(H - 1, True)
            pe.wait_ge(wo_in, 32)
            project(1)
            turn(B - 1)

            pe.wait_ge(xt2_lo, B * EO)
            for t in range(TILES):
                ts = slice(t * P, (t + 1) * P)
                ins = three_pass(pe, ps_q[:, t * NE:(t + 1) * NE], lambda o: xt_hi[:, o, ts], lambda o: xt_lo[:, o, ts],
                                 lambda o: rt_hi[:, o, :], lambda o: rt_lo[:, o, :])
            ins.then_inc(logit_psum, 1)
            pe.wait_ge(chosen_ready, 1)
            pe.matmul(ps_o[:, 0:TILES * NE], before_b[:], chosen[:].rearrange("p t e -> p (t e)"), start=True, stop=False)
            for j in range(TILES - 1):
                n = TILES - 1 - j
                ins = pe.matmul(ps_o[:, (j + 1) * NE:TILES * NE].rearrange("p (t e) -> p t e", e=NE), ones_b[:],
                                chosen[:, j:j + 1, :].to_broadcast([P, n, NE]), start=False, stop=(n == 1))
            ins.then_inc(pos_psum, 1)

            def up(j, c):
                r = c % 2
                pe.wait_ge(gu_free, j + 1)
                for k, (w0_, w1_) in enumerate(((0, P), (P, 2 * P), (2 * P, UPW))):
                    ins = three_pass(pe, ps[3 * r + k][0:w1_ - w0_, :], lambda o: up_hi[:, o, w0_:w1_],
                                     lambda o: up_lo[:, o, w0_:w1_],
                                     lambda o: xt_hi[:, o, tok(c)], lambda o: xt_lo[:, o, tok(c)])
                    if k:
                        ins.then_inc(gu_psum, 1)

            def down(e, j, c):
                r = c % 2
                pe.wait_ge(hid_ready, 2 * j + 2)
                for half in range(2):
                    pe.wait_ge(y_taken, 2 * j + half + 1)
                    for q in range(2):
                        t = half * 2 + q
                        dst = ps[6 + half][:, q * E:(q + 1) * E]
                        pe.matmul(dst, hid[:, r, t * P:(t + 1) * P],
                                  dn_sb[:, bass.ds(e, 1), :].rearrange("p a e -> p (a e)"), start=True, stop=False)
                        ins = pe.matmul(dst, hid2[0:H2, r, t * P:(t + 1) * P],
                                        dn2_sb[0:H2, bass.ds(e, 1), :].rearrange("p a e -> p (a e)"),
                                        start=False, stop=True)
                    ins.then_inc(y_psum, 1)

            pe.wait_ge(weight_ready, 1)
            pe.wait_ge(dn_in, 48)
            pe.wait_ge(up_ready, 1)
            up(0, 0)

            def expert_steps(e, last):
                for c in range(B):
                    j = e * B + c
                    if not (last and c + 1 >= B):
                        if c == B - 1:
                            pe.wait_ge(up_ready, e + 2)
                        up(j + 1, (c + 1) % B)
                    down(e, j, c)

            with pe.Fori(0, NPE - 1) as e:
                expert_steps(e, False)
            expert_steps(NPE - 1, True)

        @block.vector
        def _(dve):
            count = [0]

            def done(ins):
                count[0] += 1
                ins.then_inc(dve_c, 1)
                dve.wait_ge(dve_c, count[0])

            dve.memset(eps_sb[:], EPS)
            dve.memset(ones_b[:], 1.0)
            dve.memset(weight[:], 1.0)
            done(dve.memset(ones_t, 1.0))

            def mean_var(b, src, ready):
                for t in range(b * TPB, (b + 1) * TPB):
                    ins = dve.bn_stats(stats[:, t, :], src[:, t, :])
                done(ins)
                for t in range(b * TPB, (b + 1) * TPB):
                    dve.bn_aggr(mv[:, t, :], stats[:, t, :]).then_inc(ready, 1)

            def inverse_std(b, ready, n):
                dve.wait_ge(ready, n)
                done(dve.reciprocal(rstd[:, b * TPB:(b + 1) * TPB], std[:, b * TPB:(b + 1) * TPB]))

            for b in range(B):
                dve.wait_ge(x_in[b], 16)
                mean_var(b, x_sb, var_ready)
                if b == 0:
                    dve.wait_ge(w0_in, 16)
                    done(dve.tensor_copy(w_hi[:], w0_raw))
                    dve.tensor_tensor(w_lo[:], w0_raw, w_hi[:].bitcast(F32), ALU.subtract).then_inc(w0_split, 1)
                inverse_std(b, std_ready, b + 1)
                dve.wait_ge(var_ready, (b + 1) * TPB)
                for t in range(TPB):
                    g = b * TPB + t
                    dve.tensor_scalar(xn[:, b % 2, t, :], x_sb[:, g, :], mv[:, g, 0:1], rstd[:, g:g + 1],
                                      ALU.subtract, ALU.mult).then_inc(xn_ready, 1)
                for o in range(EO):
                    dve.wait_ge(xt_hi_ready, b * EO + o + 1)
                    dve.tensor_tensor(xt_lo[:, o, tok(b)], ps_pt[o][:], xt_hi[:, o, tok(b)].bitcast(F32),
                                      ALU.subtract).then_inc(xt_lo_ready, 1)
                if b == 0:
                    dve.wait_ge(consts_in, 6 * 16)
                dve.wait_ge(k_swapped, b + 1)
                dve.scalar_tensor_tensor(q_cos[:], ps_q[:], SCALE, cos_sb[:], ALU.mult, ALU.mult) \
                    .then_inc(k_cos_ready, 1)
                dve.wait_ge(gate_psum, b + 1)
                dve.tensor_copy(kvh_t[2 * H * b:2 * H * (b + 1), :], ps_pt[2][0:2 * H, :]).then_inc(gate_copied, 1)
                dve.tensor_copy(f_t[2 * H * b:2 * H * (b + 1), :], ps_pt[2][2 * H:4 * H, :]).then_inc(gate_copied, 1)
                dve.wait_ge(k_cos_ready, b + 1)
                dve.wait_ge(k_sin_ready, b + 1)
                dve.tensor_tensor(kt[:, tok(b)], q_cos[:], q_sin[:], ALU.add).then_inc(kt_ready, 1)
                if b < B - 1:
                    dve.wait_ge(kt_ready, b + 1)
            dve.tensor_copy(id_b[:], id_f[:])
            done(dve.tensor_copy(rt_hi[:], rt_raw[:]))
            dve.tensor_tensor(rt_lo[:], rt_raw[:], rt_hi[:].bitcast(F32), ALU.subtract)
            dve.tensor_copy(causal_b[:], causal_f).then_inc(consts_made, 1)

            def split_wq(h):
                dve.wait_ge(wq_in, 16 * (h + 1))
                dve.tensor_copy(wq_hi[:], wq_raw[:]).then_inc(wq_hi_ready, 1)
                dve.wait_ge(wq_hi_ready, h + 1)
                dve.tensor_tensor(wq_lo[:], wq_raw[:], wq_hi[:].bitcast(F32), ALU.subtract).then_inc(wq_ready, 1)

            split_wq(0)
            dve.memset(fcum_t[:, 0:1], 1.0)
            dve.wait_ge(f_ready, 1)
            done(dve.tensor_tensor_scan(fcum_t[:, 1:SEQ], f_t[:, 0:SEQ - 1], ones_t[:, 0:SEQ - 1], 1.0,
                                        ALU.mult, ALU.mult))
            done(dve.tensor_tensor(kvh_t, kvh_t, fcum_t, ALU.mult))
            dve.tensor_tensor_scan(hc_t, ones_t, kvh_t, 0.0, ALU.mult, ALU.add).then_inc(hc_ready, 1)

            def cos_q(i):
                dve.wait_ge(q_swapped, i + 1)
                dve.tensor_tensor(q_cos[:], ps_q[:], cos_sb[:], ALU.mult).then_inc(q_cos_ready, 1)

            def maxima(i, r):
                for k, tiles in enumerate(S_BANKS):
                    dve.wait_ge(s_psum, 3 * i + (k + 1))
                    for nt in tiles:
                        bank, at = s_slot(nt)
                        ins = dve.tensor_reduce(neg_max[:, r, nt:nt + 1], ps_s[bank][:, at:at + P * (nt + 1)],
                                                AX.X, ALU.max, negate=True)
                    ins.then_inc(max_ready, 1)

            def normalize(i, r):
                dve.wait_ge(exp_ready, 3 * i + 3)
                dve.reciprocal(row_inv[:, r, :], row_sum[:, r, :]).then_inc(inv_ready, 1)
                dve.wait_ge(inv_ready, i + 1)
                for nt in range(NT):
                    w = P * (nt + 1)
                    p_ = prob[:, r, ROW_AT[nt]:ROW_AT[nt] + w]
                    ins = dve.tensor_scalar(p_, p_, row_inv[:, r, nt:nt + 1], None, ALU.mult)
                ins.then_inc(prob_ready, 1)

            dve.wait_ge(kt_ready, B)
            for i in range(3):
                if i == 1:
                    maxima(0, 0)
                    normalize(0, 0)
                if i:
                    dve.wait_ge(q_ready, i)
                cos_q(i)
            dve.sem_inc(pt_free, 3)
            dve.sem_inc(o_free, 1)
            dve.wait_ge(vcol_ready, 1)

            def steps(h, last):
                for b in range(B):
                    i = h * B + b
                    for k, tiles in enumerate(PT_BANKS):
                        dve.wait_ge(pt_psum, 3 * i + (k + 1))
                        for mt in tiles:
                            bank, at = pt_slot(mt)
                            w = SEQ - mt * P
                            col = b * 2 * H + H
                            factor = vcol[:, mt, bass.ds(h + col, 1)]
                            ins = dve.tensor_scalar(prob_t[:, COL_AT[mt]:COL_AT[mt] + w], ps_pt[bank][:, at:at + w],
                                                    factor, None, ALU.mult)
                        ins.then_inc(pt_ready, 1)
                    dve.sem_inc(pt_free, 3)
                    if not (last and b + 1 >= B):
                        maxima(i + 1, (b + 1) % 2)
                        normalize(i + 1, (b + 1) % 2)
                    if not (last and b + 3 >= B):
                        dve.wait_ge(q_ready, i + 3)
                        cos_q(i + 3)
                    if b == 0 and not last:
                        split_wq(h + 1)

            with dve.Fori(0, HG) as h:
                steps(h, False)
            for t in range(TILES):
                dve.wait_ge(proj_psum, t + 1)
                dve.tensor_copy(y_sb[:, t, :], ps_pt[t % 3][:, 0:E]).then_inc(proj_taken, 1)
            with dve.Fori(HG, H - 1) as h:
                steps(h, False)
            steps(H - 1, True)

            def rest_of_turned(b):
                for o in range(EO):
                    dve.wait_ge(xt2_hi, b * EO + o + 1)
                    dve.tensor_tensor(xt_lo[:, o, tok(b)], ps_s[o][:], xt_hi[:, o, tok(b)].bitcast(F32),
                                      ALU.subtract).then_inc(xt2_lo, 1)

            for b in range(B):
                for t in range(b * TPB, (b + 1) * TPB):
                    dve.wait_ge(proj_psum, TILES + t + 1)
                    ins = dve.tensor_tensor(y_sb[:, t, :], ps_pt[t % 3][:, 0:E], y_sb[:, t, :], ALU.add)
                    ins.then_inc(proj_taken, 1)
                dve.wait_ge(proj_taken, TILES + (b + 1) * TPB)
                if b:
                    rest_of_turned(b - 1)
                mean_var(b, y_sb, var2_ready)
                inverse_std(b, std2_ready, 2 * b + 1)
                dve.wait_ge(var2_ready, (2 * b + 1) * TPB)
                for t in range(TPB):
                    g = b * TPB + t
                    done(dve.tensor_scalar(y_n[:, t % 2, :], y_sb[:, g, :], mv[:, g, 0:1], rstd[:, g:g + 1],
                                           ALU.subtract, ALU.mult))
                    ins = dve.tensor_tensor(x_sb[:, g, :], x_sb[:, g, :], y_n[:, t % 2, :], ALU.add)
                done(ins)
                mean_var(b, x_sb, var2_ready)
                inverse_std(b, std2_ready, 2 * b + 2)
                dve.wait_ge(var2_ready, (2 * b + 2) * TPB)
                if b:
                    dve.wait_ge(xt2_psum, b * EO)
                for t in range(TPB):
                    g = b * TPB + t
                    dve.tensor_scalar(xn2[:, t, :], x_sb[:, g, :], mv[:, g, 0:1], rstd[:, g:g + 1],
                                      ALU.subtract, ALU.mult).then_inc(xn2_ready, 1)
            dve.memset(y_sb[:], 0.0)
            rest_of_turned(B - 1)

            def split_up(e):
                dve.wait_ge(up_in, 16 * (e + 1))
                dve.tensor_copy(up_hi, up_raw).then_inc(up_hi_ready, 1)
                dve.wait_ge(up_hi_ready, e + 1)
                dve.tensor_tensor(up_lo, up_raw, up_hi.bitcast(F32), ALU.subtract).then_inc(up_ready, 1)

            split_up(0)
            dve.wait_ge(dn_in, 48)
            dve.tensor_copy(before_b[:], before_f)
            dve.wait_ge(logit_psum, 1)
            done(dve.tensor_copy(logit.rearrange("p t e -> p (t e)"), ps_q[:, 0:TILES * NE]))
            for t in range(TILES):
                ins = dve.max(top[:, t, :], logit[:, t, :])
            done(ins)
            for t in range(TILES):
                ins = dve.max_index(top_at[:, t, :], top[:, t, :], logit[:, t, :])
            done(ins)
            dve.tensor_tensor(gap[:], top[:, :, 1], top[:, :, 0], ALU.subtract).then_inc(gap_ready, 1)
            done(dve.tensor_copy(top_f, top_at))
            for k in range(2):
                ins = dve.tensor_tensor(oh[:, k, :, :], iota_sb[:].unsqueeze(1).to_broadcast([P, TILES, NE]),
                                        top_f[:, :, k:k + 1].to_broadcast([P, TILES, NE]), ALU.is_equal)
            done(ins)
            dve.tensor_tensor(chosen[:], oh[:, 0, :, :], oh[:, 1, :, :], ALU.add).then_inc(chosen_ready, 1)
            dve.wait_ge(egap_ready, 1)
            done(dve.tensor_scalar(den[:], egap[:], 1.0, None, ALU.add))
            done(dve.reciprocal(cw[:, 0, :], den[:]))
            done(dve.tensor_tensor(cw[:, 1, :], cw[:, 0, :], egap[:], ALU.mult))
            for k in range(2):
                ins = dve.tensor_tensor(oh[:, k, :, :], oh[:, k, :, :],
                                        cw[:, k, :].unsqueeze(2).to_broadcast([P, TILES, NE]), ALU.mult)
            done(ins)
            dve.wait_ge(pos_psum, 1)
            dve.tensor_scalar(fits.rearrange("p t e -> p (t e)"), ps_o[:, 0:TILES * NE], float(CAP), None, ALU.is_lt)
            done(dve.tensor_tensor(oh[:, 0, :, :], oh[:, 0, :, :], oh[:, 1, :, :], ALU.add))
            dve.tensor_tensor(weight[:, :, 0:NE], oh[:, 0, :, :], fits, ALU.mult).then_inc(weight_ready, 1)
            dve.wait_ge(weight_ready, 1)
            dve.sem_inc(gu_free, 2)
            dve.sem_inc(y_taken, 2)

            def expert_steps(e, last):
                for c in range(B):
                    j = e * B + c
                    r = c % 2
                    dve.wait_ge(silu_ready, 2 * j + 1)
                    dve.wait_ge(gu_psum, 2 * j + 2)
                    dve.tensor_tensor(hid[:, r, :], sg[:, r, :], ps[3 * r + 1][:], ALU.mult).then_inc(hid_ready, 1)
                    dve.wait_ge(silu_ready, 2 * j + 2)
                    dve.tensor_tensor(hid2[0:H2, r, :], sg2[0:H2, r, :], ps[3 * r + 2][64:64 + H2, :],
                                      ALU.mult).then_inc(hid_ready, 1)
                    dve.wait_ge(hid_ready, 2 * j + 2)
                    dve.sem_inc(gu_free, 1)
                    if c == B - 1 and not last:
                        split_up(e + 1)
                    for half in range(2):
                        dve.wait_ge(y_psum, 2 * j + half + 1)
                        for q in range(2):
                            t = c * TPB + 2 * half + q
                            ins = dve.scalar_tensor_tensor(y_sb[:, t, :], ps[6 + half][:, q * E:(q + 1) * E],
                                                           weight[:, t, bass.ds(e, 1)], y_sb[:, t, :],
                                                           ALU.mult, ALU.add)
                        ins.then_inc(y_taken, 1)

            with dve.Fori(0, NPE - 1) as e:
                expert_steps(e, False)
            expert_steps(NPE - 1, True)
            dve.wait_ge(y_taken, 2 + 2 * NPE * B)
            for b in range(B):
                mean_var(b, y_sb, var2_ready)
            for b in range(B):
                inverse_std(b, std2_ready, 2 * B + b + 1)
                dve.wait_ge(var2_ready, (2 * B + b + 1) * TPB)
                for t in range(TPB):
                    g = b * TPB + t
                    done(dve.tensor_scalar(y_sb[:, g, :], y_sb[:, g, :], mv[:, g, 0:1], rstd[:, g:g + 1],
                                           ALU.subtract, ALU.mult))
                    dve.tensor_tensor(y_sb[:, g, :], x_sb[:, g, :], y_sb[:, g, :], ALU.add).then_inc(out_ready, 1)

        @block.gpsimd
        def _(pool):
            pool.wait_ge(consts_in, 6 * 16)
            for b in range(B):
                pool.wait_ge(k_swapped, b + 1)
                if b:
                    pool.wait_ge(kt_ready, b)
                pool.tensor_tensor(q_sin[:], q_sw[:], sin_sb[:], ALU.mult).then_inc(k_sin_ready, 1)

            def rotate(i, r):
                pool.wait_ge(q_swapped, i + 1)
                pool.tensor_tensor(q_sin[:], q_sw[:], sin_sb[:], ALU.mult).then_inc(q_sin_ready, 1)
                pool.wait_ge(q_cos_ready, i + 1)
                pool.wait_ge(q_sin_ready, i + 1)
                pool.tensor_tensor(q_rot[:, r, :], q_cos[:], q_sin[:], ALU.add).then_inc(q_ready, 1)

            def scale_keys(b, nth, r):
                pool.wait_ge(kh_row_in[r], 16 * nth)
                pool.tensor_tensor(k_h[:, r, :], kt[:, tok(b)], kh_row[:, r, :], ALU.mult).then_inc(kh_ready, 1)

            pool.wait_ge(kt_ready, B)
            rotate(0, 0)
            scale_keys(0, 1, 0)
            rotate(1, 1)
            scale_keys(1, 1, 1)
            pool.wait_ge(s_psum, 3)
            rotate(2, 0)

            def steps(h, last):
                for b in range(B):
                    i = h * B + b
                    if not (last and b + 2 >= B):
                        pool.wait_ge(s_psum, 3 * i + 3)
                        scale_keys((b + 2) % B, 2 * h + (b + 2) // 2 + 1, b % 2)
                    if not (last and b + 3 >= B):
                        pool.wait_ge(s_psum, 3 * i + 6)
                        rotate(i + 3, (b + 1) % 2)

            with pool.Fori(0, H - 1) as h:
                steps(h, False)
            steps(H - 1, True)


def kernel(**inputs):
    import numpy as _np
    import concourse.bacc as _bacc
    from concourse import mybir as _mybir
    from concourse.bass_utils import run_bass_kernel_spmd as _run

    x, wq, wkv, wkvh, wg, wout, router, w_ug, w_dn, sw_ug, sw_dn = (_np.asarray(inputs[n]) for n in (
        "L0_attn_x", "L0_attn_Wq", "L0_attn_Wkv", "L0_attn_Wkvh", "L0_attn_Wg", "L0_attn_Wout", "L0_ffn_router",
        "L0_ffn_w_up_gate", "L0_ffn_w_down", "L0_ffn_shared_w_up_gate", "L0_ffn_shared_w_down"))
    B, SEQ, E = x.shape
    D = wkv.shape[0] // 2
    H = wq.shape[0] // D
    NE, HID = w_dn.shape[:2]
    J = sw_dn.shape[0]
    NS = J // HID
    NPE = NE + NS
    EO = E // 128
    CAP = int(_np.ceil(B * SEQ * 2 / NE * 1.25))
    H2 = HID - 128

    def rows(a):
        return a.reshape(EO, 128, -1).transpose(1, 0, 2)

    ug = _np.zeros((NPE, E, 2 * 128 + 64 + H2), x.dtype)
    dn = _np.zeros((NPE, HID, E), x.dtype)
    for n in range(NPE):
        if n < NE:
            gate, up = w_ug[n][:, :HID], w_ug[n][:, HID:]
            dn[n] = w_dn[n]
        else:
            s = (n - NE) * HID
            gate, up = sw_ug[:, s:s + HID], sw_ug[:, J + s:J + s + HID]
            dn[n] = sw_dn[s:s + HID]
        ug[n][:, 0:128], ug[n][:, 128:256] = gate[:, :128], up[:, :128]
        ug[n][:, 256:256 + H2], ug[n][:, 320:320 + H2] = gate[:, 128:], up[:, 128:]
    pad = _np.zeros((E, 128 - 4 * H), x.dtype)
    w0 = _np.concatenate([wkv.T, wkvh.T, wg.T, pad], axis=1)

    f32 = _np.float32
    inv = (f32(10000.0) ** (-_np.arange(0, D, 2, dtype=f32) / f32(D))).astype(f32)
    ang = _np.arange(SEQ, dtype=f32)[:, None] * inv[None, :]
    cos, sin = _np.cos(ang).T, _np.sin(ang).T
    n = _np.arange(128)
    arrays = {
        "x": x.reshape(B * SEQ, E),
        "wq": wq.reshape(H, D, EO, 128).transpose(0, 3, 2, 1),
        "w0": rows(w0),
        "wout": wout.reshape(E, H, D).transpose(2, 1, 0),
        "cos_t": _np.concatenate([cos, cos]).astype(f32),
        "sin_t": _np.concatenate([-sin, sin]).astype(f32),
        "ident": _np.eye(128, dtype=f32),
        "causal": _np.where(n[None, :] > n[:, None], f32(-1e30), f32(0)).astype(f32),
        "before": (n[:, None] < n[None, :]).astype(f32),
        "iota8": _np.tile(_np.arange(NE, dtype=f32), (128, 1)),
        "router": rows(router),
        "w_up": ug.reshape(NPE, EO, 128, -1).transpose(0, 2, 1, 3),
        "w_dn": dn[:, :128].transpose(1, 0, 2),
        "w_dn2": dn[:, 128:].transpose(1, 0, 2),
    }
    arrays = {f"in_{k}_dram": _np.ascontiguousarray(a) for k, a in arrays.items()}
    nc = _bacc.Bacc("TRN2", target_bir_lowering=False, num_devices=1)
    args = [nc.dram_tensor(k, a.shape, _mybir.dt.from_np(a.dtype), kind="ExternalInput").ap() for k, a in arrays.items()]
    out = nc.dram_tensor("out_0_dram", (B * SEQ, E), _mybir.dt.from_np(x.dtype), kind="ExternalOutput").ap()
    decoder_layer(nc, *args, out, (B, SEQ, H, D, E, NE, NPE, CAP, HID))
    r = _run(nc, [arrays], core_ids=[0])
    return r.results[0]["out_0_dram"].reshape(B, SEQ, E)
```

```python
from contextlib import ExitStack

import numpy as np

import concourse.bass as bass
from concourse import mybir

F32 = mybir.dt.float32
F32R = mybir.dt.float32r
BF16 = mybir.dt.bfloat16
U32 = mybir.dt.uint32
ALU = mybir.AluOpType
ACT = mybir.ActivationFunctionType
AX = mybir.AxisListType

P = 128
EPS = 1e-5

NT = 4
ROW_AT = [0, 128, 384, 768]
COL_AT = [0, 512, 896, 1152]
PACKED = 1280
S_BANKS = [[3], [2, 0], [1]]
PT_BANKS = [[0], [1, 3], [2]]


def s_slot(nt):
    return {3: (0, 0), 2: (1, 0), 0: (1, 384), 1: (2, 0)}[nt]


def pt_slot(mt):
    return {0: (0, 0), 1: (1, 0), 3: (1, 384), 2: (2, 0)}[mt]


def decoder_layer(nc, x, wq, w0, wout, cos_t, sin_t, ident, causal, before, iota8,
                  router, w_up, w_dn, sw_up, sw_dn, out, dims):
    B, SEQ, H, D, E, NE, NS, CAP, HID, SHID = dims
    T = B * SEQ
    TILES = T // P
    TPB = SEQ // P
    EO = E // P
    UNITS = H * B
    HG = H // 2
    H2 = HID - P
    UPW = 3 * P - (P - 64 - H2)
    SCALE = float(1.0 / np.sqrt(D))

    ST = CAP // P
    HC = CAP // 2
    SH = -(-SHID // P)
    SHW = [min(P, SHID - i * P) for i in range(SH)]
    SKIP = 8192.0

    kvh_dram = nc.dram_tensor("kvh_rows", [B * 2 * H, SEQ], F32).ap()
    xg_dram = nc.dram_tensor("slot_inputs", [NE * CAP, E], F32).ap()
    yg_dram = nc.dram_tensor("slot_outputs", [NE * CAP, E], F32).ap()
    x_v = x.rearrange("(b t p) e -> b p t e", p=P, t=TPB)
    out_v = out.rearrange("(b t p) e -> b p t e", p=P, t=TPB)

    with ExitStack() as ctx:
        def sb(name, shape, dt=F32):
            return ctx.enter_context(nc.sbuf_tensor(name, shape, dt))

        def sem(name):
            return ctx.enter_context(nc.semaphore(name))

        ps = [ctx.enter_context(nc.psum_tensor(f"ps{i}", [P, 512], F32)) for i in range(8)]
        ps_q, ps_s, ps_pt, ps_o = ps[0], ps[1:4], ps[4:7], ps[7]

        x_sb = sb("x_sb", [P, TILES, E])
        xt_hi = sb("xt_hi", [P, EO, T], F32R)
        xt_lo = sb("xt_lo", [P, EO, T], F32R)
        y_sb = sb("y_sb", [P, TILES, E])
        id_f = sb("id_f", [P, P])
        stats = sb("stats", [P, TILES, 6])
        mv = sb("mv", [P, TILES, 2])
        eps_sb = sb("eps_sb", [P, 1])
        std = sb("std", [P, TILES])
        rstd = sb("rstd", [P, TILES])
        cos_sb = sb("cos_sb", [P, SEQ])
        sin_sb = sb("sin_sb", [P, SEQ])
        id_b = sb("id_b", [P, P], BF16)
        causal_b = sb("causal_b", [P, P], BF16)
        work = sb("work", [P, T + 9 * SEQ])
        kt = work[:, 0:T]
        vp = sb("vp", [P, TILES, D])
        vcol = sb("vcol", [P, TPB, B * 2 * H])
        wo_sb = sb("wo_sb", [P, HG, E])
        wq_raw = sb("wq_raw", [P, EO, D])
        wq_hi = sb("wq_hi", [P, EO, D], F32R)
        wq_lo = sb("wq_lo", [P, EO, D], F32R)
        q_sw, q_cos, q_sin = (work[:, T + n * SEQ:T + (n + 1) * SEQ] for n in range(3))
        q_rot = work[:, T + 3 * SEQ:T + 5 * SEQ].rearrange("p (r n) -> p r n", r=2)
        kh_row = work[:, T + 5 * SEQ:T + 7 * SEQ].rearrange("p (r n) -> p r n", r=2)
        k_h = work[:, T + 7 * SEQ:T + 9 * SEQ].rearrange("p (r n) -> p r n", r=2)
        x_flat = x_sb[:, :, :].rearrange("p t e -> p (t e)")
        prob = x_flat[:, 0:2 * PACKED].rearrange("p (r n) -> p r n", r=2)
        prob_t = x_flat[:, 2 * PACKED:3 * PACKED]
        neg_max = sb("neg_max", [P, 2, NT])
        row_sum = sb("row_sum", [P, 2, NT])
        row_inv = sb("row_inv", [P, 2, NT])
        arena = sb("arena", [P, HG * T])
        o_t = arena[:, :].rearrange("p (h t) -> p h t", h=HG)

        def cutter(buffer, at=0):
            at = [at]

            def piece(shape, dt=F32):
                n = int(np.prod(shape))
                at[0] += n
                v = buffer[:, at[0] - n:at[0]]
                v = v if dt == F32 else v.bitcast(dt)
                names = "abcd"[:len(shape)]
                return v.rearrange(f"p ({' '.join(names)}) -> p {' '.join(names)}", **dict(zip(names, shape)))
            return piece

        piece = cutter(arena)
        xn = piece([2, TPB, E])
        f_t, kvh_t, fcum_t, hc_t, ones_t = (piece([SEQ]) for _ in range(5))
        causal_f = piece([P])
        before_f = piece([P])
        w0_raw = piece([EO, 3 * P])
        zeros = piece([10, E])
        WN = max(2 * EO * UPW, EO * 2 * SHID)
        w_hi = sb("w_hi", [P, WN], F32R)
        w_lo = sb("w_lo", [P, WN], F32R)

        def split_view(n, at=0):
            return [w[:, at:at + EO * n].rearrange("p (o n) -> p o n", o=EO) for w in (w_hi, w_lo)]

        w0_hi, w0_lo = split_view(3 * P)
        sw_hi, sw_lo = split_view(2 * SHID)
        up_hl = [split_view(UPW, r * EO * UPW) for r in range(2)]
        sw_raw = [piece([EO, 2 * SHID])]

        piece = cutter(arena)
        sdn_sb = piece([2, SH, E])
        s_hid = piece([2, SH, SEQ])
        s_sg = piece([SH, SEQ])
        up_raw = piece([2, EO, UPW])
        dn_sb = piece([2, 2, E])
        sw_raw.append(piece([EO, 2 * SHID]))
        xg = piece([2, ST, E])
        yo = piece([ST, E])
        logit, top, top_f, fits = (piece([TILES, NE]) for _ in range(4))
        top_at = piece([TILES, NE], U32)
        oh = piece([2, TILES, NE])
        pos_sb, pos_oh = piece([TILES, NE]), piece([2, TILES, NE])
        shared_only = cutter(arena, 2 * SH * E)
        hid, hid2 = shared_only([2, CAP]), shared_only([2, CAP])
        sg, sg2 = shared_only([2, HC]), shared_only([2, HC])
        xg_hi = sb("xg_hi", [P, EO, CAP], F32R)
        xg_lo = sb("xg_lo", [P, EO, CAP], F32R)
        xn2 = work[:, 0:T * E // P].rearrange("p (t e) -> p t e", t=TILES)
        y_n = work[:, T * E // P:T * E // P + 2 * E].rearrange("p (r e) -> p r e", r=2)
        GR = 8
        got = work[:, T * E // P + 2 * E:T * E // P + (2 + GR) * E].rearrange("p (r e) -> p r e", r=GR)
        rt_raw = sb("rt_raw", [P, EO, NE])
        rt_hi = sb("rt_hi", [P, EO, NE], F32R)
        rt_lo = sb("rt_lo", [P, EO, NE], F32R)
        before_b = sb("before_b", [P, P], BF16)
        ones_b = sb("ones_b", [P, P], BF16)
        iota_sb = sb("iota_sb", [P, NE])
        chosen = sb("chosen", [P, TILES, NE], BF16)
        gap = sb("gap", [P, TILES])
        egap = sb("egap", [P, TILES])
        den = sb("den", [P, TILES])
        cw = sb("cw", [P, 2, TILES])
        pos, keep, slot = (sb(n, [P, 2, TILES]) for n in ("pos", "keep", "slot"))
        slot_in = sb("slot_in", [P, 2, TILES])
        at_in = sb("at_in", [P, 2, TILES], U32)
        at_out = sb("at_out", [P, 2, TILES], U32)

        id_in, rope_in, consts_in, w0_in, wo_in = (
            sem("id_in"), sem("rope_in"), sem("consts_in"), sem("w0_in"), sem("wo_in"))
        x_in = [sem(f"x_in{b}") for b in range(B)]
        wq_in = sem("wq_in")
        kh_row_in = [sem(f"kh_row_in{r}") for r in range(2)]
        kvh_stored = sem("kvh_stored")
        dve_c = sem("dve_c")
        w0_split, consts_made = sem("w0_split"), sem("consts_made")
        var_ready, std_ready, xn_ready = sem("var_ready"), sem("std_ready"), sem("xn_ready")
        xt_psum, xt_hi_ready, xt_lo_ready = sem("xt_psum"), sem("xt_hi_ready"), sem("xt_lo_ready")
        k_psum, k_swapped, k_cos_ready, k_sin_ready, kt_ready = (
            sem("k_psum"), sem("k_swapped"), sem("k_cos_ready"), sem("k_sin_ready"), sem("kt_ready"))
        gate_psum, gate_copied, v_psum, v_ready = sem("gate_psum"), sem("gate_copied"), sem("v_psum"), sem("v_ready")
        f_ready, hc_ready, vcol_psum, vcol_ready = sem("f_ready"), sem("hc_ready"), sem("vcol_psum"), sem("vcol_ready")
        wq_hi_ready, wq_ready = sem("wq_hi_ready"), sem("wq_ready")
        q_psum, q_swapped, q_cos_ready, q_sin_ready, q_ready = (
            sem("q_psum"), sem("q_swapped"), sem("q_cos_ready"), sem("q_sin_ready"), sem("q_ready"))
        kh_ready = sem("kh_ready")
        s_psum, max_ready, exp_ready, inv_ready, prob_ready = (
            sem("s_psum"), sem("max_ready"), sem("exp_ready"), sem("inv_ready"), sem("prob_ready"))
        pt_psum, pt_free, pt_ready = sem("pt_psum"), sem("pt_free"), sem("pt_ready")
        o_psum, o_free, o_ready = sem("o_psum"), sem("o_free"), sem("o_ready")
        proj_psum, proj_taken = sem("proj_psum"), sem("proj_taken")
        xt2_psum, xt2_hi, xt2_lo = sem("xt2_psum"), sem("xt2_hi"), sem("xt2_lo")
        var2_ready, std2_ready, xn2_ready = sem("var2_ready"), sem("std2_ready"), sem("xn2_ready")
        x_again = [sem(f"x_again{b}") for b in range(B)]
        zeros_made, slots_cleared = sem("zeros_made"), sem("slots_cleared")
        sw_in, sdn_in, sw_split_hi, sw_split = sem("sw_in"), sem("sdn_in"), sem("sw_split_hi"), sem("sw_split")
        s_psum_g, s_silu, s_hid_ready, sy_psum, sy_taken = (
            sem("s_psum_g"), sem("s_silu"), sem("s_hid_ready"), sem("sy_psum"), sem("sy_taken"))
        logit_psum, logit_taken, gap_ready, egap_ready = (
            sem("logit_psum"), sem("logit_taken"), sem("gap_ready"), sem("egap_ready"))
        chosen_ready, pos_psum, pos_taken, slots_ready = (
            sem("chosen_ready"), sem("pos_psum"), sem("pos_taken"), sem("slots_ready"))
        scattered = sem("scattered")
        xg_in, up_in, dn_in = ([sem(f"{n}{r}") for r in range(2)] for n in ("xg_in", "up_in", "dn_in"))
        up_hi_ready, up_ready = sem("up_hi_ready"), sem("up_ready")
        xg_psum, xg_hi_ready, xg_ready = sem("xg_psum"), sem("xg_hi_ready"), sem("xg_ready")
        gu_psum, silu_ready, gu_free = sem("gu_psum"), sem("silu_ready"), sem("gu_free")
        yo_psum, yo_ready, yo_stored = sem("yo_psum"), sem("yo_ready"), sem("yo_stored")
        got_in = [sem(f"got_in{r}") for r in range(GR)]
        got_used = sem("got_used")
        out_ready, stored = sem("out_ready"), sem("stored")

        def tok(b):
            return slice(b * SEQ, (b + 1) * SEQ)

        XG_BANKS = [(0, 0), (1, 1), (2, None)]
        XG_W = 4 * P

        def xg_src(bank):
            return ps[2][:, 0:EO * P].rearrange("p (o n) -> p o n", o=EO) if bank == 2 else ps[bank][:]

        def xg_dst(buf, o):
            return buf[:, :, XG_W:CAP] if o is None else buf[:, o, 0:XG_W]

        YO_BANKS = [(0, 2), (2, 2), (4, 1)]

        def turn_bank(b, o):
            return (3 if b < B - 1 else 6) + o

        def sw_cols(i):
            g = 2 * P * i
            return (g, g + SHW[i]), (g + SHW[i], g + 2 * SHW[i])

        def three_pass(pe, psum, w_hi, w_lo, m_hi, m_lo):
            for o in range(EO):
                for j, (w, m) in enumerate(((w_hi, m_hi), (w_hi, m_lo), (w_lo, m_hi))):
                    last = pe.matmul(psum, w(o), m(o), start=(o == 0 and j == 0),
                                     stop=(o == EO - 1 and j == 2))
            return last

        block = ctx.enter_context(nc.Block())

        @block.sync
        def _(sp):
            sp.dma_start(x_sb[:, 0:TPB, :], x_v[0]).then_inc(x_in[0], 16)
            sp.dma_start(id_f[:], ident).then_inc(id_in, 16)
            sp.dma_start(w0_raw, w0).then_inc(w0_in, 16)
            for b in range(1, B):
                sp.dma_start(x_sb[:, b * TPB:(b + 1) * TPB, :], x_v[b]).then_inc(x_in[b], 16)
            sp.dma_start(causal_f, causal).then_inc(consts_in, 16)
            sp.dma_start(iota_sb[:], iota8).then_inc(consts_in, 16)
            sp.dma_start(rt_raw[:], router).then_inc(consts_in, 16)
            sp.dma_start(wo_sb[:], wout[:, 0:HG, :]).then_inc(wo_in, 16)
            sp.dma_start(before_f, before).then_inc(consts_in, 16)
            sp.dma_start(sw_raw[0], sw_up[0]).then_inc(sw_in, 16)
            sp.wait_ge(zeros_made, 1)
            for n in range(4):
                sp.dma_start(xg_dram.rearrange("(p s) e -> p s e", p=P)[:, n * 10:(n + 1) * 10, :], zeros) \
                    .then_inc(slots_cleared, 16)
            sp.wait_ge(hc_ready, 1)
            sp.dma_start(kvh_dram, hc_t).then_inc(kvh_stored, 16)
            sp.wait_ge(kvh_stored, 16)
            for i in range(2):
                sp.dma_start(kh_row[:, i, :], kvh_dram[i * 2 * H:i * 2 * H + 1, :].to_broadcast([P, SEQ])) \
                    .then_inc(kh_row_in[i], 16)

            def steps(h, last):
                for b in range(B):
                    if b == 0 and not last:
                        sp.wait_ge(wq_ready, h + 1)
                        sp.dma_start(wq_raw[:], wq[bass.ds(h + 1, 1), :, :, :].rearrange("h p o d -> (h p) o d")) \
                            .then_inc(wq_in, 16)
                    if last and b + 2 >= B:
                        continue
                    b2, h2 = (b + 2) % B, h + (b + 2) // B
                    sp.wait_ge(kh_ready, h * B + b + 1)
                    sp.dma_start(kh_row[:, b % 2, :],
                                 kvh_dram[bass.ds(h2 + 2 * H * b2, 1), :].to_broadcast([P, SEQ])) \
                        .then_inc(kh_row_in[b % 2], 16)

            with sp.Fori(0, HG) as h:
                steps(h, False)
            sp.wait_ge(proj_psum, TILES)
            sp.dma_start(wo_sb[:], wout[:, HG:H, :]).then_inc(wo_in, 16)
            with sp.Fori(HG, H - 1) as h:
                steps(h, False)
            steps(H - 1, True)

            sp.wait_ge(proj_psum, TILES + 1)
            for b in range(B):
                sp.dma_start(x_sb[:, b * TPB:(b + 1) * TPB, :], x_v[b]).then_inc(x_again[b], 16)
            sp.wait_ge(proj_psum, 2 * TILES)
            sp.dma_start(sdn_sb, sw_dn).then_inc(sdn_in, 16)

            sp.sem_inc(yo_stored, 16)

            def load_expert(e, r):
                sp.dma_start(up_raw[:, r, :, :], w_up[bass.ds(e, 1), :, :, :].rearrange("n p o c -> (n p) o c")) \
                    .then_inc(up_in[r], 16)

            def load_down(e, r):
                sp.dma_start(dn_sb[:, r, :, :], w_dn[bass.ds(e, 1), :, :, :].rearrange("n p k c -> (n p) k c")) \
                    .then_inc(dn_in[r], 16)

            def load_slots(e, r):
                sp.dma_start(xg[:, r, :, :], xg_dram[bass.ds(e * CAP, CAP), :].rearrange("(p s) e -> p s e", p=P)) \
                    .then_inc(xg_in[r], 16)

            for e in range(2):
                load_expert(e, e)
                load_down(e, e)
            sp.dma_start(sw_raw[1], sw_up[1]).then_inc(sw_in, 16)
            sp.wait_ge(scattered, 2 * TILES * 16)
            for e in range(2):
                load_slots(e, e)

            def expert_steps(e0, last):
                for r in range(2):
                    e = e0 + r
                    if not last:
                        sp.wait_ge(xg_psum, 3 * e + 3)
                        load_slots(e + 2, r)
                        sp.wait_ge(up_ready, e + 1)
                        load_expert(e + 2, r)
                    sp.wait_ge(yo_ready, 3 * e + 6)
                    sp.dma_start(yg_dram[bass.ds(e * CAP, CAP), :].rearrange("(p s) e -> p s e", p=P), yo) \
                        .then_inc(yo_stored, 16)
                    if not last:
                        load_down(e + 2, r)

            with sp.Fori(0, NE // 2 - 1) as pair:
                expert_steps(pair * 2, False)
            expert_steps(NE - 2, True)
            for b in range(B):
                sp.wait_ge(out_ready, (b + 1) * TPB)
                sp.dma_start(out_v[b], y_sb[:, b * TPB:(b + 1) * TPB, :]).then_inc(stored, 16)
            sp.wait_ge(stored, 16 * B)

        @block.scalar
        def _(act):
            act.dma_start(cos_sb[:], cos_t).then_inc(rope_in, 16)
            act.dma_start(sin_sb[:], sin_t).then_inc(rope_in, 16)
            act.dma_start(wq_raw[:], wq[0]).then_inc(wq_in, 16)
            for b in range(B):
                act.wait_ge(var_ready, (b + 1) * TPB)
                act.activation(std[:, b * TPB:(b + 1) * TPB], mv[:, b * TPB:(b + 1) * TPB, 1], ACT.Sqrt,
                               bias=eps_sb[:, 0:1]).then_inc(std_ready, 1)
                for o in range(EO):
                    act.wait_ge(xt_psum, b * EO + o + 1)
                    act.copy(xt_hi[:, o, tok(b)], ps_pt[o][:]).then_inc(xt_hi_ready, 1)
                act.wait_ge(k_psum, b + 1)
                if b:
                    act.wait_ge(kt_ready, b)
                act.mul(q_sw[0:64, :], ps_q[64:128, :], SCALE)
                act.mul(q_sw[64:128, :], ps_q[0:64, :], SCALE).then_inc(k_swapped, 1)
                act.wait_ge(v_psum, b + 1)
                act.copy(vp[:, b * TPB:(b + 1) * TPB, :], ps_o[:]).then_inc(v_ready, 1)
            act.wait_ge(gate_copied, 2 * B)
            act.activation(f_t, f_t, ACT.Sigmoid).then_inc(f_ready, 1)
            act.wait_ge(vcol_psum, 1)
            act.copy(vcol[:], ps_s[2][:]).then_inc(vcol_ready, 1)

            def swap_q(i):
                act.wait_ge(q_psum, i + 1)
                act.copy(q_sw[0:64, :], ps_q[64:128, :])
                act.copy(q_sw[64:128, :], ps_q[0:64, :]).then_inc(q_swapped, 1)

            def exps(i, r):
                for k, tiles in enumerate(S_BANKS):
                    act.wait_ge(max_ready, 3 * i + (k + 1))
                    for nt in tiles:
                        bank, at = s_slot(nt)
                        w = P * (nt + 1)
                        ins = act.activation(prob[:, r, ROW_AT[nt]:ROW_AT[nt] + w], ps_s[bank][:, at:at + w], ACT.Exp,
                                             bias=neg_max[:, r, nt:nt + 1], accum_out=row_sum[:, r, nt:nt + 1])
                    ins.then_inc(exp_ready, 1)

            act.wait_ge(kt_ready, B)
            for i in range(3):
                if i == 1:
                    exps(0, 0)
                if i:
                    act.wait_ge(q_ready, i)
                swap_q(i)

            def steps(h, slot, last):
                for b in range(B):
                    i = h * B + b
                    if not (last and b + 1 >= B):
                        exps(i + 1, (b + 1) % 2)
                    if not (last and b + 3 >= B):
                        act.wait_ge(q_ready, i + 3)
                        swap_q(i + 3)
                    act.wait_ge(o_psum, i + 1)
                    act.copy(o_t[:, slot, tok(b)] if isinstance(slot, int) else
                             o_t[:, bass.ds(slot, 1), tok(b)].rearrange("p a t -> p (a t)"), ps_o[:]) \
                        .then_inc(o_free, 1)

            with act.Fori(0, HG) as h:
                steps(h, h, False)
            with act.Fori(HG, H - 1) as h:
                steps(h, h - HG, False)
            steps(H - 1, HG - 1, True)

            def turned_head(b):
                for o in range(EO):
                    act.wait_ge(xt2_psum, b * EO + o + 1)
                    act.copy(xt_hi[:, o, tok(b)], ps[turn_bank(b, o)][:]).then_inc(xt2_hi, 1)

            def silus(j):
                for i in range(SH):
                    act.wait_ge(s_psum_g, 2 * (j * SH + i) + 1)
                    act.activation(s_sg[0:SHW[i], i, :], ps[2 * i][0:SHW[i], :], ACT.Silu).then_inc(s_silu, 1)

            for b in range(B):
                for k in range(2):
                    act.wait_ge(var2_ready, (2 * b + k + 1) * TPB)
                    act.activation(std[:, b * TPB:(b + 1) * TPB], mv[:, b * TPB:(b + 1) * TPB, 1], ACT.Sqrt,
                                   bias=eps_sb[:, 0:1]).then_inc(std2_ready, 1)
                if b < B - 1:
                    turned_head(b)
            silus(0)
            turned_head(B - 1)
            silus(1)
            act.wait_ge(gap_ready, 1)
            act.activation(egap[:], gap[:], ACT.Exp).then_inc(egap_ready, 1)
            silus(2)
            silus(3)

            def expert_head(e):
                act.wait_ge(gu_free, 4 * e + 2)
                for k, (bank, dst) in enumerate(XG_BANKS):
                    act.wait_ge(xg_psum, 3 * e + (k + 1))
                    act.copy(xg_dst(xg_hi, dst), xg_src(bank)).then_inc(xg_hi_ready, 1)

            def expert_steps(e0, last):
                for r in range(2):
                    e = e0 + r
                    for c in range(2):
                        act.wait_ge(gu_psum, 3 * (2 * e + c) + 1)
                        act.activation(sg[:, c, :], ps[3][:, 0:HC], ACT.Silu).then_inc(silu_ready, 1)
                        act.wait_ge(gu_psum, 3 * (2 * e + c) + 3)
                        act.activation(sg2[0:H2, c, :], ps[5][0:H2, 0:HC], ACT.Silu).then_inc(silu_ready, 1)
                    if not (last and r == 1):
                        expert_head(e + 1)
                    act.wait_ge(yo_stored, 16 * e + 16)
                    for k, (t0, n) in enumerate(YO_BANKS):
                        act.wait_ge(yo_psum, 3 * e + (k + 1))
                        act.copy(yo[:, t0:t0 + n, :], ps[6 + k % 2][:, 0:n * E]).then_inc(yo_ready, 1)

            act.sem_inc(yo_ready, 3)
            expert_head(0)
            with act.Fori(0, NE // 2 - 1) as pair:
                expert_steps(pair * 2, False)
            expert_steps(NE - 2, True)
            silus(B)
            for b in range(B):
                if b + 1 < B:
                    silus(B + b + 1)
                act.wait_ge(var2_ready, (2 * B + b + 1) * TPB)
                act.activation(std[:, b * TPB:(b + 1) * TPB], mv[:, b * TPB:(b + 1) * TPB, 1], ACT.Sqrt,
                               bias=eps_sb[:, 0:1]).then_inc(std2_ready, 1)

        @block.tensor
        def _(pe):
            pe.wait_ge(id_in, 16)
            for b in range(B):
                pe.wait_ge(xn_ready, (b + 1) * TPB)
                if b:
                    pe.wait_ge(xt_lo_ready, b * EO)
                for o in range(EO):
                    for t in range(TPB):
                        ins = pe.transpose(ps_pt[o][:, t * P:(t + 1) * P], xn[:, b % 2, t, o * P:(o + 1) * P], id_f[:])
                    ins.then_inc(xt_psum, 1)
                pe.wait_ge(w0_split, 1)
                pe.wait_ge(xt_lo_ready, (b + 1) * EO)
                if b:
                    pe.wait_ge(k_cos_ready, b)
                three_pass(pe, ps_q[:], lambda o: w0_hi[:, o, 0:P], lambda o: w0_lo[:, o, 0:P],
                           lambda o: xt_hi[:, o, tok(b)], lambda o: xt_lo[:, o, tok(b)]).then_inc(k_psum, 1)
                if b:
                    pe.wait_ge(gate_copied, 2 * b)
                three_pass(pe, ps_pt[2][:], lambda o: w0_hi[:, o, 2 * P:], lambda o: w0_lo[:, o, 2 * P:],
                           lambda o: xt_hi[:, o, tok(b)], lambda o: xt_lo[:, o, tok(b)]).then_inc(gate_psum, 1)
                if b:
                    pe.wait_ge(v_ready, b)
                for t in range(TPB):
                    ts = slice(b * SEQ + t * P, b * SEQ + (t + 1) * P)
                    ins = three_pass(pe, ps_o[:, t * P:(t + 1) * P], lambda o: xt_hi[:, o, ts], lambda o: xt_lo[:, o, ts],
                                     lambda o: w0_hi[:, o, P:2 * P], lambda o: w0_lo[:, o, P:2 * P])
                ins.then_inc(v_psum, 1)

            def q_proj(i, b):
                three_pass(pe, ps_q[:], lambda o: wq_hi[:, o, :], lambda o: wq_lo[:, o, :],
                           lambda o: xt_hi[:, o, tok(b)], lambda o: xt_lo[:, o, tok(b)]).then_inc(q_psum, 1)

            def scores(i, r, first=False):
                pe.wait_ge(q_ready, i + 1)
                pe.wait_ge(kh_ready, i + 1)
                for k, tiles in enumerate(S_BANKS):
                    if not first:
                        pe.wait_ge(exp_ready, 3 * (i - 1) + (k + 1))
                    for nt in tiles:
                        bank, at = s_slot(nt)
                        w = P * (nt + 1)
                        pe.matmul(ps_s[bank][:, at:at + w], q_rot[:, r, nt * P:(nt + 1) * P], k_h[:, r, 0:w],
                                  start=True, stop=False)
                        ins = pe.matmul(ps_s[bank][:, at + w - P:at + w], id_b[:], causal_b[:],
                                        start=False, stop=True)
                    ins.then_inc(s_psum, 1)

            pe.wait_ge(consts_made, 1)
            pe.wait_ge(wq_ready, 1)
            pe.wait_ge(k_cos_ready, B)
            q_proj(0, 0)
            pe.wait_ge(hc_ready, 1)
            for mt in range(TPB):
                ins = pe.transpose(ps_s[2][:, mt * P:(mt + 1) * P], hc_t[:, mt * P:(mt + 1) * P], id_f[:])
            ins.then_inc(vcol_psum, 1)
            pe.wait_ge(q_cos_ready, 1)
            q_proj(1, 1)
            pe.wait_ge(vcol_ready, 1)
            scores(0, 0, first=True)
            pe.wait_ge(q_cos_ready, 2)
            q_proj(2, 2)

            def steps(h, last):
                for b in range(B):
                    i = h * B + b
                    pe.wait_ge(prob_ready, i + 1)
                    pe.wait_ge(pt_free, 3 * i + 3)
                    for tiles in PT_BANKS:
                        for mt in tiles:
                            bank, at = pt_slot(mt)
                            for nt in range(mt, NT):
                                src = ROW_AT[nt] + mt * P
                                dst = at + (nt - mt) * P
                                ins = pe.transpose(ps_pt[bank][:, dst:dst + P], prob[:, b % 2, src:src + P], id_f[:])
                        ins.then_inc(pt_psum, 1)
                    if not (last and b + 1 >= B):
                        scores(i + 1, (b + 1) % 2)
                    if not (last and b + 3 >= B):
                        pe.wait_ge(q_cos_ready, i + 3)
                        if b == 1:
                            pe.wait_ge(wq_ready, h + 2)
                        q_proj(i + 3, (b + 3) % B)
                    pe.wait_ge(o_free, i + 1)
                    for k, tiles in enumerate(PT_BANKS):
                        pe.wait_ge(pt_ready, 3 * i + (k + 1))
                        for mt in tiles:
                            ins = pe.matmul(ps_o[:, mt * P:SEQ], vp[:, b * TPB + mt, :],
                                            prob_t[:, COL_AT[mt]:COL_AT[mt] + SEQ - mt * P],
                                            start=(mt == 0), stop=(mt == 2))
                    ins.then_inc(o_psum, 1)

            def project(g):
                banks = ps[4:7] if g == 0 else ps[5:8]
                pe.wait_ge(o_free, HG * (g + 1) * B + 1)
                pe.wait_ge(pt_free, 3 * HG * (g + 1) * B + 3)
                for t in range(TILES):
                    if t >= 3 or g == 1:
                        pe.wait_ge(proj_taken, g * TILES + max(t - 2, 0))
                    for hh in range(HG):
                        ins = pe.matmul(banks[t % 3][:, 0:E], o_t[:, hh, t * P:(t + 1) * P], wo_sb[:, hh, :],
                                        start=(hh == 0), stop=(hh == HG - 1))
                    ins.then_inc(proj_psum, 1)
                    if g == 1 and t % TPB == TPB - 1 and t >= TPB:
                        turn(t // TPB - 1)

            def turn(b):
                pe.wait_ge(xn2_ready, (b + 1) * TPB)
                for o in range(EO):
                    if 0 < b < B - 1:
                        pe.wait_ge(xt2_lo, (b - 1) * EO + o + 1)
                    for t in range(TPB):
                        ins = pe.transpose(ps[turn_bank(b, o)][:, t * P:(t + 1) * P],
                                           xn2[:, b * TPB + t, o * P:(o + 1) * P], id_f[:])
                    ins.then_inc(xt2_psum, 1)

            pe.wait_ge(wo_in, 16)
            with pe.Fori(0, HG) as h:
                steps(h, False)
            project(0)
            pe.wait_ge(proj_taken, TILES)
            with pe.Fori(HG, H - 1) as h:
                steps(h, False)
            steps(H - 1, True)
            pe.wait_ge(wo_in, 32)
            project(1)

            def shared_up(j):
                c = j % B
                for i in range(SH):
                    if j % B:
                        pe.wait_ge(s_hid_ready, (j - 1) * SH + i + 1)
                    for k, (a, z) in enumerate(sw_cols(i)):
                        three_pass(pe, ps[2 * i + k][0:z - a, :], lambda o: sw_hi[:, o, a:z], lambda o: sw_lo[:, o, a:z],
                                   lambda o: xt_hi[:, o, tok(c)], lambda o: xt_lo[:, o, tok(c)]).then_inc(s_psum_g, 1)

            def shared_down(j):
                n = j // B
                pe.wait_ge(s_hid_ready, (j + 1) * SH)
                for half in range(2):
                    if j % B:
                        pe.wait_ge(sy_taken, 2 * j - 1 + half)
                    if j == 0 and half == 0:
                        pe.wait_ge(logit_taken, 1)
                    if j == 1 and half == 1:
                        pe.wait_ge(pos_taken, 1)
                    for q in range(2):
                        t = 2 * half + q
                        for i in range(SH):
                            ins = pe.matmul(ps[6 + half][:, q * E:(q + 1) * E],
                                            s_hid[0:SHW[i], j % 2, i, t * P:(t + 1) * P], sdn_sb[0:SHW[i], n, i, :],
                                            start=(i == 0), stop=(i == SH - 1))
                    ins.then_inc(sy_psum, 1)

            def logits():
                pe.wait_ge(xt2_lo, B * EO)
                for t in range(TILES):
                    ts = slice(t * P, (t + 1) * P)
                    ins = three_pass(pe, ps[6][:, t * NE:(t + 1) * NE], lambda o: xt_hi[:, o, ts],
                                     lambda o: xt_lo[:, o, ts], lambda o: rt_hi[:, o, :], lambda o: rt_lo[:, o, :])
                ins.then_inc(logit_psum, 1)

            def positions():
                pe.wait_ge(chosen_ready, 1)
                pe.wait_ge(sy_taken, 2)
                pe.matmul(ps[7][:, 0:TILES * NE], before_b[:], chosen[:].rearrange("p t e -> p (t e)"),
                          start=True, stop=False)
                for j in range(TILES - 1):
                    n = TILES - 1 - j
                    ins = pe.matmul(ps[7][:, (j + 1) * NE:TILES * NE].rearrange("p (t e) -> p t e", e=NE), ones_b[:],
                                    chosen[:, j:j + 1, :].to_broadcast([P, n, NE]), start=False, stop=(n == 1))
                ins.then_inc(pos_psum, 1)

            pe.wait_ge(sw_split, 1)
            pe.wait_ge(xt2_lo, (B - 1) * EO)
            pe.wait_ge(proj_taken, 2 * TILES)
            shared_up(0)
            turn(B - 1)
            shared_up(1)
            logits()
            pe.wait_ge(sdn_in, 16)
            shared_down(0)
            shared_up(2)
            positions()
            shared_down(1)
            shared_up(3)
            shared_down(2)
            shared_down(3)

            def turn_slots(e, r):
                pe.wait_ge(xg_in[r], 8 * (e - r) + 16)
                for k in range(EO):
                    for t in range(4):
                        ins = pe.transpose(ps[k][:, t * P:(t + 1) * P], xg[:, r, t, k * P:(k + 1) * P], id_f[:])
                    ins.then_inc(xg_psum, 1)
                for k in range(EO):
                    ins = pe.transpose(ps[2][:, k * P:(k + 1) * P], xg[:, r, 4, k * P:(k + 1) * P], id_f[:])
                ins.then_inc(xg_psum, 1)

            def expert_up(e, r, c):
                m = 2 * e + c
                cs = slice(c * HC, (c + 1) * HC)
                w_hi_, w_lo_ = up_hl[r]
                for k, (a, z) in enumerate(((0, P), (P, 2 * P), (2 * P, UPW))):
                    if k == 0:
                        pe.wait_ge(gu_free, 2 * m + 1)
                    if k == 2:
                        pe.wait_ge(gu_free, 2 * m + 2)
                    three_pass(pe, ps[3 + k][0:z - a, 0:HC], lambda o: w_hi_[:, o, a:z], lambda o: w_lo_[:, o, a:z],
                               lambda o: xg_hi[:, o, cs], lambda o: xg_lo[:, o, cs]).then_inc(gu_psum, 1)

            def expert_down(e, r):
                pe.wait_ge(dn_in[r], 8 * (e - r) + 16)
                pe.wait_ge(gu_free, 4 * e + 6)
                for k, (t0, n) in enumerate(YO_BANKS):
                    pe.wait_ge(yo_ready, 3 * e + (3, 2, 4)[k])
                    for q in range(n):
                        t = t0 + q
                        dst = ps[6 + k % 2][:, q * E:(q + 1) * E]
                        pe.matmul(dst, hid[:, r, t * P:(t + 1) * P], dn_sb[:, r, 0, :], start=True, stop=False)
                        ins = pe.matmul(dst, hid2[0:H2, r, t * P:(t + 1) * P], dn_sb[0:H2, r, 1, :],
                                        start=False, stop=True)
                    ins.then_inc(yo_psum, 1)

            def expert_steps(e0, last):
                for r in range(2):
                    e = e0 + r
                    pe.wait_ge(xg_ready, 3 * e + 3)
                    pe.wait_ge(up_ready, e + 1)
                    expert_up(e, r, 0)
                    expert_up(e, r, 1)
                    if not (last and r == 1):
                        turn_slots(e + 1, 1 - r)
                    expert_down(e, r)

            pe.wait_ge(s_hid_ready, B * SH)
            turn_slots(0, 0)
            pe.wait_ge(sy_taken, 2 * B)
            with pe.Fori(0, NE // 2 - 1) as pair:
                expert_steps(pair * 2, False)
            expert_steps(NE - 2, True)

            pe.wait_ge(sw_split, 2)
            shared_up(B)
            pe.wait_ge(yo_ready, 3 * NE + 3)
            for j in range(B, 2 * B):
                if j + 1 < 2 * B:
                    shared_up(j + 1)
                shared_down(j)

        @block.vector
        def _(dve):
            count = [0]

            def done(ins):
                count[0] += 1
                ins.then_inc(dve_c, 1)
                dve.wait_ge(dve_c, count[0])

            dve.memset(eps_sb[:], EPS)
            dve.memset(ones_b[:], 1.0)
            done(dve.memset(ones_t, 1.0))

            def mean_var(b, src, ready):
                for t in range(b * TPB, (b + 1) * TPB):
                    ins = dve.bn_stats(stats[:, t, :], src[:, t, :])
                done(ins)
                for t in range(b * TPB, (b + 1) * TPB):
                    dve.bn_aggr(mv[:, t, :], stats[:, t, :]).then_inc(ready, 1)

            def inverse_std(b, ready, n):
                dve.wait_ge(ready, n)
                done(dve.reciprocal(rstd[:, b * TPB:(b + 1) * TPB], std[:, b * TPB:(b + 1) * TPB]))

            for b in range(B):
                dve.wait_ge(x_in[b], 16)
                mean_var(b, x_sb, var_ready)
                if b == 0:
                    dve.wait_ge(w0_in, 16)
                    done(dve.tensor_copy(w0_hi, w0_raw))
                    dve.tensor_tensor(w0_lo, w0_raw, w0_hi.bitcast(F32), ALU.subtract).then_inc(w0_split, 1)
                inverse_std(b, std_ready, b + 1)
                dve.wait_ge(var_ready, (b + 1) * TPB)
                for t in range(TPB):
                    g = b * TPB + t
                    dve.tensor_scalar(xn[:, b % 2, t, :], x_sb[:, g, :], mv[:, g, 0:1], rstd[:, g:g + 1],
                                      ALU.subtract, ALU.mult).then_inc(xn_ready, 1)
                for o in range(EO):
                    dve.wait_ge(xt_hi_ready, b * EO + o + 1)
                    dve.tensor_tensor(xt_lo[:, o, tok(b)], ps_pt[o][:], xt_hi[:, o, tok(b)].bitcast(F32),
                                      ALU.subtract).then_inc(xt_lo_ready, 1)
                if b == 0:
                    dve.wait_ge(rope_in, 32)
                dve.wait_ge(k_swapped, b + 1)
                dve.scalar_tensor_tensor(q_cos, ps_q[:], SCALE, cos_sb[:], ALU.mult, ALU.mult) \
                    .then_inc(k_cos_ready, 1)
                dve.wait_ge(gate_psum, b + 1)
                dve.tensor_copy(kvh_t[2 * H * b:2 * H * (b + 1), :], ps_pt[2][0:2 * H, :]).then_inc(gate_copied, 1)
                dve.tensor_copy(f_t[2 * H * b:2 * H * (b + 1), :], ps_pt[2][2 * H:4 * H, :]).then_inc(gate_copied, 1)
                dve.wait_ge(k_cos_ready, b + 1)
                dve.wait_ge(k_sin_ready, b + 1)
                dve.tensor_tensor(kt[:, tok(b)], q_cos, q_sin, ALU.add).then_inc(kt_ready, 1)
                if b < B - 1:
                    dve.wait_ge(kt_ready, b + 1)
            dve.wait_ge(consts_in, 4 * 16)
            dve.tensor_copy(id_b[:], id_f[:])
            dve.tensor_copy(before_b[:], before_f)
            done(dve.tensor_copy(rt_hi[:], rt_raw[:]))
            dve.tensor_tensor(rt_lo[:], rt_raw[:], rt_hi[:].bitcast(F32), ALU.subtract)
            dve.tensor_copy(causal_b[:], causal_f).then_inc(consts_made, 1)

            def split_share(n):
                dve.wait_ge(sw_in, 16 * (n + 1))
                dve.tensor_copy(sw_hi, sw_raw[n]).then_inc(sw_split_hi, 1)
                dve.wait_ge(sw_split_hi, n + 1)
                dve.tensor_tensor(sw_lo, sw_raw[n], sw_hi.bitcast(F32), ALU.subtract).then_inc(sw_split, 1)

            def split_wq(h):
                dve.wait_ge(wq_in, 16 * (h + 1))
                dve.tensor_copy(wq_hi[:], wq_raw[:]).then_inc(wq_hi_ready, 1)
                dve.wait_ge(wq_hi_ready, h + 1)
                dve.tensor_tensor(wq_lo[:], wq_raw[:], wq_hi[:].bitcast(F32), ALU.subtract).then_inc(wq_ready, 1)

            split_wq(0)
            dve.wait_ge(v_psum, B)
            split_share(0)
            dve.memset(fcum_t[:, 0:1], 1.0)
            dve.wait_ge(f_ready, 1)
            done(dve.tensor_tensor_scan(fcum_t[:, 1:SEQ], f_t[:, 0:SEQ - 1], ones_t[:, 0:SEQ - 1], 1.0,
                                        ALU.mult, ALU.mult))
            done(dve.tensor_tensor(kvh_t, kvh_t, fcum_t, ALU.mult))
            dve.tensor_tensor_scan(hc_t, ones_t, kvh_t, 0.0, ALU.mult, ALU.add).then_inc(hc_ready, 1)

            def cos_q(i):
                dve.wait_ge(q_swapped, i + 1)
                dve.tensor_tensor(q_cos, ps_q[:], cos_sb[:], ALU.mult).then_inc(q_cos_ready, 1)

            def maxima(i, r):
                for k, tiles in enumerate(S_BANKS):
                    dve.wait_ge(s_psum, 3 * i + (k + 1))
                    for nt in tiles:
                        bank, at = s_slot(nt)
                        ins = dve.tensor_reduce(neg_max[:, r, nt:nt + 1], ps_s[bank][:, at:at + P * (nt + 1)],
                                                AX.X, ALU.max, negate=True)
                    ins.then_inc(max_ready, 1)

            def normalize(i, r):
                dve.wait_ge(exp_ready, 3 * i + 3)
                dve.reciprocal(row_inv[:, r, :], row_sum[:, r, :]).then_inc(inv_ready, 1)
                dve.wait_ge(inv_ready, i + 1)
                for nt in range(NT):
                    w = P * (nt + 1)
                    p_ = prob[:, r, ROW_AT[nt]:ROW_AT[nt] + w]
                    ins = dve.tensor_scalar(p_, p_, row_inv[:, r, nt:nt + 1], None, ALU.mult)
                ins.then_inc(prob_ready, 1)

            dve.wait_ge(kt_ready, B)
            for i in range(3):
                if i == 1:
                    maxima(0, 0)
                    normalize(0, 0)
                if i:
                    dve.wait_ge(q_ready, i)
                cos_q(i)
            dve.sem_inc(pt_free, 3)
            dve.sem_inc(o_free, 1)
            dve.wait_ge(vcol_ready, 1)

            def steps(h, last):
                for b in range(B):
                    i = h * B + b
                    for k, tiles in enumerate(PT_BANKS):
                        dve.wait_ge(pt_psum, 3 * i + (k + 1))
                        for mt in tiles:
                            bank, at = pt_slot(mt)
                            w = SEQ - mt * P
                            col = b * 2 * H + H
                            factor = vcol[:, mt, bass.ds(h + col, 1)]
                            ins = dve.tensor_scalar(prob_t[:, COL_AT[mt]:COL_AT[mt] + w], ps_pt[bank][:, at:at + w],
                                                    factor, None, ALU.mult)
                        ins.then_inc(pt_ready, 1)
                    dve.sem_inc(pt_free, 3)
                    if not (last and b + 1 >= B):
                        maxima(i + 1, (b + 1) % 2)
                        normalize(i + 1, (b + 1) % 2)
                    if not (last and b + 3 >= B):
                        dve.wait_ge(q_ready, i + 3)
                        cos_q(i + 3)
                    if b == 0 and not last:
                        split_wq(h + 1)

            with dve.Fori(0, HG) as h:
                steps(h, False)
            for t in range(TILES):
                dve.wait_ge(proj_psum, t + 1)
                dve.tensor_copy(y_sb[:, t, :], ps_pt[t % 3][:, 0:E]).then_inc(proj_taken, 1)
            with dve.Fori(HG, H - 1) as h:
                steps(h, False)
            steps(H - 1, True)

            def rest_of_turned(b):
                for o in range(EO):
                    dve.wait_ge(xt2_hi, b * EO + o + 1)
                    dve.tensor_tensor(xt_lo[:, o, tok(b)], ps[turn_bank(b, o)][:], xt_hi[:, o, tok(b)].bitcast(F32),
                                      ALU.subtract).then_inc(xt2_lo, 1)

            for b in range(B):
                for t in range(b * TPB, (b + 1) * TPB):
                    dve.wait_ge(proj_psum, TILES + t + 1)
                    ins = dve.tensor_tensor(y_sb[:, t, :], ps[5 + t % 3][:, 0:E], y_sb[:, t, :], ALU.add)
                    ins.then_inc(proj_taken, 1)
                dve.wait_ge(proj_taken, TILES + (b + 1) * TPB)
                if b:
                    rest_of_turned(b - 1)
                mean_var(b, y_sb, var2_ready)
                inverse_std(b, std2_ready, 2 * b + 1)
                dve.wait_ge(var2_ready, (2 * b + 1) * TPB)
                dve.wait_ge(x_again[b], 16)
                for t in range(TPB):
                    g = b * TPB + t
                    done(dve.tensor_scalar(y_n[:, t % 2, :], y_sb[:, g, :], mv[:, g, 0:1], rstd[:, g:g + 1],
                                           ALU.subtract, ALU.mult))
                    ins = dve.tensor_tensor(x_sb[:, g, :], x_sb[:, g, :], y_n[:, t % 2, :], ALU.add)
                done(ins)
                mean_var(b, x_sb, var2_ready)
                inverse_std(b, std2_ready, 2 * b + 2)
                dve.wait_ge(var2_ready, (2 * b + 2) * TPB)
                for t in range(TPB):
                    g = b * TPB + t
                    dve.tensor_scalar(xn2[:, g, :], x_sb[:, g, :], mv[:, g, 0:1], rstd[:, g:g + 1],
                                      ALU.subtract, ALU.mult).then_inc(xn2_ready, 1)

            def shared_hidden(j):
                for i in range(SH):
                    w = SHW[i]
                    dve.wait_ge(s_silu, j * SH + i + 1)
                    dve.wait_ge(s_psum_g, 2 * (j * SH + i) + 2)
                    dve.tensor_tensor(s_hid[0:w, j % 2, i, :], s_sg[0:w, i, :], ps[2 * i + 1][0:w, :],
                                      ALU.mult).then_inc(s_hid_ready, 1)

            def shared_sum(j):
                for half in range(2):
                    dve.wait_ge(sy_psum, 2 * j + half + 1)
                    t = (j % B) * TPB + 2 * half
                    dst = y_sb[:, t:t + 2, :].rearrange("p t e -> p (t e)")
                    if j < B:
                        dve.tensor_copy(dst, ps[6 + half][:]).then_inc(sy_taken, 1)
                    else:
                        dve.tensor_tensor(dst, ps[6 + half][:], dst, ALU.add).then_inc(sy_taken, 1)

            shared_hidden(0)
            rest_of_turned(B - 1)
            shared_hidden(1)
            dve.wait_ge(logit_psum, 1)
            dve.tensor_copy(logit.rearrange("p t e -> p (t e)"), ps[6][:, 0:TILES * NE]).then_inc(logit_taken, 1)
            dve.wait_ge(logit_taken, 1)
            for t in range(TILES):
                ins = dve.max(top[:, t, :], logit[:, t, :])
            done(ins)
            for t in range(TILES):
                ins = dve.max_index(top_at[:, t, :], top[:, t, :], logit[:, t, :])
            done(ins)
            dve.tensor_tensor(gap[:], top[:, :, 1], top[:, :, 0], ALU.subtract).then_inc(gap_ready, 1)
            done(dve.tensor_copy(top_f, top_at))
            for k in range(2):
                ins = dve.tensor_tensor(oh[:, k, :, :], iota_sb[:].unsqueeze(1).to_broadcast([P, TILES, NE]),
                                        top_f[:, :, k:k + 1].to_broadcast([P, TILES, NE]), ALU.is_equal)
            done(ins)
            dve.tensor_tensor(chosen[:], oh[:, 0, :, :], oh[:, 1, :, :], ALU.add).then_inc(chosen_ready, 1)
            dve.wait_ge(egap_ready, 1)
            done(dve.tensor_scalar(den[:], egap[:], 1.0, None, ALU.add))
            done(dve.reciprocal(cw[:, 0, :], den[:]))
            dve.tensor_tensor(cw[:, 1, :], cw[:, 0, :], egap[:], ALU.mult)
            shared_sum(0)
            shared_hidden(2)
            dve.wait_ge(pos_psum, 1)
            dve.tensor_copy(pos_sb.rearrange("p t e -> p (t e)"), ps[7][:, 0:TILES * NE]).then_inc(pos_taken, 1)
            dve.wait_ge(pos_taken, 1)
            for k in range(2):
                ins = dve.tensor_tensor(pos_oh[:, k, :, :], oh[:, k, :, :], pos_sb, ALU.mult)
            done(ins)
            done(dve.tensor_reduce(pos[:], pos_oh, AX.X, ALU.add))
            expert_of = top_f[:, :, 0:2].rearrange("p t k -> p k t")
            dve.scalar_tensor_tensor(slot[:], expert_of, float(CAP), pos[:], ALU.mult, ALU.add)
            done(dve.tensor_scalar(keep[:], pos[:], float(CAP), None, ALU.is_lt))
            done(dve.scalar_tensor_tensor(slot_in[:], keep[:], -SKIP, slot[:], ALU.mult, ALU.add))
            dve.tensor_scalar(at_in[:], slot_in[:], SKIP, None, ALU.add).then_inc(slots_ready, 1)
            done(dve.tensor_scalar(pos[:], pos[:], float(CAP - 1), None, ALU.min))
            dve.scalar_tensor_tensor(at_out[:], expert_of, float(CAP), pos[:], ALU.mult, ALU.add) \
                .then_inc(slots_ready, 1)
            done(dve.tensor_tensor(cw[:], cw[:], keep[:], ALU.mult))
            shared_sum(1)
            shared_hidden(3)
            shared_sum(2)
            shared_sum(3)

            def expert_rest(e):
                for k, (bank, o) in enumerate(XG_BANKS):
                    dve.wait_ge(xg_hi_ready, 3 * e + (k + 1))
                    dve.tensor_tensor(xg_dst(xg_lo, o), xg_src(bank), xg_dst(xg_hi, o).bitcast(F32),
                                      ALU.subtract).then_inc(xg_ready, 1)

            def expert_steps(e0, last):
                for r in range(2):
                    e = e0 + r
                    for c in range(2):
                        m = 2 * e + c
                        cs = slice(c * HC, (c + 1) * HC)
                        dve.wait_ge(silu_ready, 2 * m + 1)
                        dve.wait_ge(gu_psum, 3 * m + 2)
                        dve.tensor_tensor(hid[:, r, cs], sg[:, c, :], ps[4][:, 0:HC], ALU.mult).then_inc(gu_free, 1)
                        dve.wait_ge(silu_ready, 2 * m + 2)
                        dve.tensor_tensor(hid2[0:H2, r, cs], sg2[0:H2, c, :], ps[5][64:64 + H2, 0:HC],
                                          ALU.mult).then_inc(gu_free, 1)
                    if not (last and r == 1):
                        expert_rest(e + 1)

            dve.sem_inc(gu_free, 2)
            expert_rest(0)
            with dve.Fori(0, NE // 2 - 1) as pair:
                expert_steps(pair * 2, False)
            expert_steps(NE - 2, True)
            split_share(1)

            shared_hidden(B)
            for b in range(B):
                j = B + b
                if b + 1 < B:
                    shared_hidden(j + 1)
                shared_sum(j)
                dve.wait_ge(sy_taken, 2 * j + 2)
                for k in range(2):
                    for t in range(b * TPB, (b + 1) * TPB):
                        g = 2 * (b * TPB) + k * TPB + t - b * TPB
                        dve.wait_ge(got_in[g % GR], 16 * (g // GR + 1))
                        if k == 1:
                            dve.wait_ge(got_used, g - TPB + 1)
                        dve.scalar_tensor_tensor(y_sb[:, t, :], got[:, g % GR, :], cw[:, k, t:t + 1], y_sb[:, t, :],
                                                 ALU.mult, ALU.add).then_inc(got_used, 1)
                dve.wait_ge(got_used, 2 * (b + 1) * TPB)
                mean_var(b, y_sb, var2_ready)
                inverse_std(b, std2_ready, 2 * B + b + 1)
                dve.wait_ge(var2_ready, (2 * B + b + 1) * TPB)
                for t in range(b * TPB, (b + 1) * TPB):
                    ins = dve.tensor_scalar(y_sb[:, t, :], y_sb[:, t, :], mv[:, t, 0:1], rstd[:, t:t + 1],
                                            ALU.subtract, ALU.mult)
                done(ins)
                for t in range(b * TPB, (b + 1) * TPB):
                    dve.tensor_tensor(y_sb[:, t, :], x_sb[:, t, :], y_sb[:, t, :], ALU.add).then_inc(out_ready, 1)

        @block.gpsimd
        def _(pool):
            pool.memset(zeros, 0.0).then_inc(zeros_made, 1)
            pool.wait_ge(rope_in, 32)
            for b in range(B):
                pool.wait_ge(k_swapped, b + 1)
                if b:
                    pool.wait_ge(kt_ready, b)
                pool.tensor_tensor(q_sin, q_sw, sin_sb[:], ALU.mult).then_inc(k_sin_ready, 1)

            def rotate(i, r):
                pool.wait_ge(q_swapped, i + 1)
                pool.tensor_tensor(q_sin, q_sw, sin_sb[:], ALU.mult).then_inc(q_sin_ready, 1)
                pool.wait_ge(q_cos_ready, i + 1)
                pool.wait_ge(q_sin_ready, i + 1)
                pool.tensor_tensor(q_rot[:, r, :], q_cos, q_sin, ALU.add).then_inc(q_ready, 1)

            def scale_keys(b, nth, r):
                pool.wait_ge(kh_row_in[r], 16 * nth)
                pool.tensor_tensor(k_h[:, r, :], kt[:, tok(b)], kh_row[:, r, :], ALU.mult).then_inc(kh_ready, 1)

            pool.wait_ge(kt_ready, B)
            rotate(0, 0)
            scale_keys(0, 1, 0)
            rotate(1, 1)
            scale_keys(1, 1, 1)
            pool.wait_ge(s_psum, 3)
            rotate(2, 0)

            def steps(h, last):
                for b in range(B):
                    i = h * B + b
                    if not (last and b + 2 >= B):
                        pool.wait_ge(s_psum, 3 * i + 3)
                        scale_keys((b + 2) % B, 2 * h + (b + 2) // 2 + 1, b % 2)
                    if not (last and b + 3 >= B):
                        pool.wait_ge(s_psum, 3 * i + 6)
                        rotate(i + 3, (b + 1) % 2)

            with pool.Fori(0, H - 1) as h:
                steps(h, False)
            steps(H - 1, True)

            pool.wait_ge(slots_cleared, 4 * 16)
            pool.wait_ge(slots_ready, 1)
            for t in range(TILES):
                for k in range(2):
                    pool.indirect_dma_start(
                        xg_dram[:, :], bass.IndirectOffsetOnAxis(ap=at_in[:, k, t:t + 1], axis=0), xn2[:, t, :], None,
                        bounds_check=NE * CAP - 1, oob_is_err=False).then_inc(scattered, 16)

            def split_up(e, r, first):
                hi, lo = up_hl[r]
                pool.wait_ge(up_in[r], 8 * (e - r) + 16)
                if not first:
                    pool.wait_ge(gu_free, 4 * e - 2)
                pool.tensor_copy(hi, up_raw[:, r, :, :]).then_inc(up_hi_ready, 1)
                pool.wait_ge(up_hi_ready, e + 1)
                pool.tensor_tensor(lo, up_raw[:, r, :, :], hi.bitcast(F32), ALU.subtract).then_inc(up_ready, 1)

            pool.wait_ge(s_psum_g, 2 * B * SH)
            pool.wait_ge(gu_free, 2)
            for e in range(NE):
                split_up(e, e % 2, e < 2)

            pool.wait_ge(slots_ready, 2)
            pool.wait_ge(yo_stored, 16 * NE + 16)
            for g in range(2 * TILES):
                b, k, t = g // (2 * TPB), g // TPB % 2, g % TPB + g // (2 * TPB) * TPB
                if g >= GR:
                    pool.wait_ge(got_used, g - GR + 1)
                pool.indirect_dma_start(
                    got[:, g % GR, :], None, yg_dram[:, :],
                    bass.IndirectOffsetOnAxis(ap=at_out[:, k, t:t + 1], axis=0),
                    bounds_check=NE * CAP - 1, oob_is_err=False).then_inc(got_in[g % GR], 16)


def kernel(**inputs):
    import numpy as _np
    import concourse.bacc as _bacc
    from concourse import mybir as _mybir
    from concourse.bass_utils import run_bass_kernel_spmd as _run

    x, wq, wkv, wkvh, wg, wout, router, w_ug, w_dn, sw_ug, sw_dn = (_np.asarray(inputs[n]) for n in (
        "L0_attn_x", "L0_attn_Wq", "L0_attn_Wkv", "L0_attn_Wkvh", "L0_attn_Wg", "L0_attn_Wout", "L0_ffn_router",
        "L0_ffn_w_up_gate", "L0_ffn_w_down", "L0_ffn_shared_w_up_gate", "L0_ffn_shared_w_down"))
    B, SEQ, E = x.shape
    D = wkv.shape[0] // 2
    H = wq.shape[0] // D
    NE, HID = w_dn.shape[:2]
    J = sw_dn.shape[0]
    NS = 2
    EO = E // 128
    CAP = int(_np.ceil(B * SEQ * 2 / NE * 1.25))
    H2, SHID = HID - 128, J // NS

    def rows(a):
        return a.reshape(EO, 128, -1).transpose(1, 0, 2)

    ug = _np.zeros((NE, E, 2 * 128 + 64 + H2), x.dtype)
    gate, up = w_ug[:, :, :HID], w_ug[:, :, HID:]
    ug[:, :, 0:128], ug[:, :, 128:256] = gate[:, :, :128], up[:, :, :128]
    ug[:, :, 256:256 + H2], ug[:, :, 320:320 + H2] = gate[:, :, 128:], up[:, :, 128:]
    dn = _np.zeros((NE, 128, 2, E), x.dtype)
    dn[:, :, 0], dn[:, :H2, 1] = w_dn[:, :128], w_dn[:, 128:]
    tiles = [(i, min(128, SHID - i)) for i in range(0, SHID, 128)]
    sug = _np.stack([rows(_np.concatenate([sw_ug[:, q + n * SHID + i:q + n * SHID + i + w]
                                           for i, w in tiles for q in (0, J)], axis=1)) for n in range(NS)])
    sdn = _np.zeros((128, NS, len(tiles), E), x.dtype)
    for n in range(NS):
        for a, (i, w) in enumerate(tiles):
            sdn[:w, n, a] = sw_dn[n * SHID + i:n * SHID + i + w]
    pad = _np.zeros((E, 128 - 4 * H), x.dtype)
    w0 = _np.concatenate([wkv.T, wkvh.T, wg.T, pad], axis=1)

    f32 = _np.float32
    inv = (f32(10000.0) ** (-_np.arange(0, D, 2, dtype=f32) / f32(D))).astype(f32)
    ang = _np.arange(SEQ, dtype=f32)[:, None] * inv[None, :]
    cos, sin = _np.cos(ang).T, _np.sin(ang).T
    n = _np.arange(128)
    arrays = {
        "x": x.reshape(B * SEQ, E),
        "wq": wq.reshape(H, D, EO, 128).transpose(0, 3, 2, 1),
        "w0": rows(w0),
        "wout": wout.reshape(E, H, D).transpose(2, 1, 0),
        "cos_t": _np.concatenate([cos, cos]).astype(f32),
        "sin_t": _np.concatenate([-sin, sin]).astype(f32),
        "ident": _np.eye(128, dtype=f32),
        "causal": _np.where(n[None, :] > n[:, None], f32(-1e30), f32(0)).astype(f32),
        "before": (n[:, None] < n[None, :]).astype(f32),
        "iota8": _np.tile(_np.arange(NE, dtype=f32), (128, 1)),
        "router": rows(router),
        "w_up": ug.reshape(NE, EO, 128, -1).transpose(0, 2, 1, 3),
        "w_dn": dn,
        "sw_up": sug,
        "sw_dn": sdn,
    }
    arrays = {f"in_{k}_dram": _np.ascontiguousarray(a) for k, a in arrays.items()}
    nc = _bacc.Bacc("TRN2", target_bir_lowering=False, num_devices=1)
    args = [nc.dram_tensor(k, a.shape, _mybir.dt.from_np(a.dtype), kind="ExternalInput").ap() for k, a in arrays.items()]
    out = nc.dram_tensor("out_0_dram", (B * SEQ, E), _mybir.dt.from_np(x.dtype), kind="ExternalOutput").ap()
    decoder_layer(nc, *args, out, (B, SEQ, H, D, E, NE, NS, CAP, HID, SHID))
    r = _run(nc, [arrays], core_ids=[0])
    return r.results[0]["out_0_dram"].reshape(B, SEQ, E)
```

```python
from contextlib import ExitStack

import numpy as np

import concourse.bass as bass
from concourse import mybir

F32 = mybir.dt.float32
F32R = mybir.dt.float32r
BF16 = mybir.dt.bfloat16
U32 = mybir.dt.uint32
ALU = mybir.AluOpType
ACT = mybir.ActivationFunctionType
AX = mybir.AxisListType

P = 128
EPS = 1e-5

NT = 4
ROW_AT = [0, 128, 384, 768]
COL_AT = [0, 512, 896, 1152]
PACKED = 1280
S_BANKS = [[3], [2, 0], [1]]
PT_BANKS = [[0], [1, 3], [2]]


def s_slot(nt):
    return {3: (0, 0), 2: (1, 0), 0: (1, 384), 1: (2, 0)}[nt]


def pt_slot(mt):
    return {0: (0, 0), 1: (1, 0), 3: (1, 384), 2: (2, 0)}[mt]


def decoder_layer(nc, x, wq, w0, wout, cos_t, sin_t, ident, causal, before, iota8,
                  router, w_up, w_dn, sw_up, sw_dn, out, dims):
    B, SEQ, H, D, E, NE, NS, CAP, HID, SHID = dims
    T = B * SEQ
    TILES = T // P
    TPB = SEQ // P
    EO = E // P
    UNITS = H * B
    HG = H // 2
    H2 = HID - P
    UPW = 3 * P - (P - 64 - H2)
    SCALE = float(1.0 / np.sqrt(D))

    ST = CAP // P
    HC = CAP // 2
    SH = -(-SHID // P)
    SHW = [min(P, SHID - i * P) for i in range(SH)]
    SKIP = 8192.0

    kvh_dram = nc.dram_tensor("kvh_rows", [B * 2 * H, SEQ], F32).ap()
    xg_dram = nc.dram_tensor("slot_inputs", [NE * CAP, E], F32).ap()
    yg_dram = nc.dram_tensor("slot_outputs", [NE * CAP, E], F32).ap()
    x_v = x.rearrange("(b t p) e -> b p t e", p=P, t=TPB)
    out_v = out.rearrange("(b t p) e -> b p t e", p=P, t=TPB)

    with ExitStack() as ctx:
        def sb(name, shape, dt=F32):
            return ctx.enter_context(nc.sbuf_tensor(name, shape, dt))

        def sem(name):
            return ctx.enter_context(nc.semaphore(name))

        ps = [ctx.enter_context(nc.psum_tensor(f"ps{i}", [P, 512], F32)) for i in range(8)]
        ps_q, ps_s, ps_pt, ps_o = ps[0], ps[1:4], ps[4:7], ps[7]

        x_sb = sb("x_sb", [P, TILES, E])
        xt_hi = sb("xt_hi", [P, EO, T], F32R)
        xt_lo = sb("xt_lo", [P, EO, T], F32R)
        y_sb = sb("y_sb", [P, TILES, E])
        id_f = sb("id_f", [P, P])
        stats = sb("stats", [P, TILES, 6])
        mv = sb("mv", [P, TILES, 2])
        eps_sb = sb("eps_sb", [P, 1])
        one_sb = sb("one_sb", [P, 1])
        std = sb("std", [P, TILES])
        rstd = sb("rstd", [P, TILES])
        rope_sb = sb("rope_sb", [P, 2 * SEQ])
        cos_sb, sin_sb = rope_sb[:, 0:SEQ], rope_sb[:, SEQ:2 * SEQ]
        id_b = sb("id_b", [P, P], BF16)
        causal_b = sb("causal_b", [P, 2, P], BF16)
        work = sb("work", [P, T + 8 * SEQ])
        kt = work[:, 0:T]
        vcol = sb("vcol", [P, TPB, B * H])
        wo_raw = sb("wo_raw", [P, E])
        wo_hi = sb("wo_hi", [P, HG, E], F32R)
        wo_lo = sb("wo_lo", [P, HG, E], F32R)
        wq_raw = sb("wq_raw", [P, EO, D])
        wq_hi = sb("wq_hi", [P, EO, D], F32R)
        wq_lo = sb("wq_lo", [P, EO, D], F32R)
        q_sw, q_cos = (work[:, T + n * SEQ:T + (n + 1) * SEQ] for n in range(2))
        q_rot = work[:, T + 2 * SEQ:T + 4 * SEQ].rearrange("p (r n) -> p r n", r=2)
        kh_row = work[:, T + 4 * SEQ:T + 6 * SEQ].rearrange("p (r n) -> p r n", r=2)
        k_h = work[:, T + 6 * SEQ:T + 8 * SEQ].rearrange("p (r n) -> p r n", r=2)
        x_flat = x_sb[:, :, :].rearrange("p t e -> p (t e)")
        prob = x_flat[:, 0:2 * PACKED].rearrange("p (r n) -> p r n", r=2)
        sw_raw = [x_flat[:, 2 * PACKED:2 * PACKED + EO * 2 * SHID].rearrange("p (o n) -> p o n", o=EO)]
        neg_max = sb("neg_max", [P, 2, NT])
        row_sum = sb("row_sum", [P, 2, NT])
        row_inv = sb("row_inv", [P, 2, NT])
        arena = sb("arena", [P, HG * T])
        o_t = arena[:, :].rearrange("p (h t) -> p h t", h=HG)

        def cutter(buffer, at=0):
            at = [at]

            def piece(shape, dt=F32):
                n = int(np.prod(shape))
                at[0] += n
                v = buffer[:, at[0] - n:at[0]]
                v = v if dt == F32 else v.bitcast(dt)
                names = "abcd"[:len(shape)]
                return v.rearrange(f"p ({' '.join(names)}) -> p {' '.join(names)}", **dict(zip(names, shape)))
            return piece

        piece = cutter(arena)
        xn = piece([2, TPB, E])
        f_t, kvh_t, fcum_t, hc_t, ones_t = (piece([SEQ]) for _ in range(5))
        causal_f = piece([P])
        before_f = piece([P])
        w0_raw = piece([EO, 3 * P])
        zeros = piece([10, E])
        WN = max(2 * EO * UPW, EO * 2 * SHID, T * D // P)
        w_hi = sb("w_hi", [P, WN], F32R)
        w_lo = sb("w_lo", [P, WN], F32R)

        def split_view(n, at=0):
            return [w[:, at:at + EO * n].rearrange("p (o n) -> p o n", o=EO) for w in (w_hi, w_lo)]

        vp_hi, vp_lo = (w[:, 0:T * D // P].rearrange("p (t d) -> p t d", d=D) for w in (w_hi, w_lo))
        sw_hi, sw_lo = split_view(2 * SHID)
        up_hl = [split_view(UPW, r * EO * UPW) for r in range(2)]

        piece = cutter(arena)
        sdn_sb = piece([2, SH, E])
        s_hid = piece([2, SH, SEQ])
        s_sg = piece([SH, SEQ])
        up_raw = piece([2, EO, UPW])
        dn_sb = piece([2, 2, E])
        sw_raw.append(piece([EO, 2 * SHID]))
        xg = piece([2, ST, E])
        yo = piece([ST, E])
        shared_only = cutter(arena, 2 * SH * E)
        hid, hid2, sg, sg2 = (shared_only([2, HC]) for _ in range(4))
        LO = 64
        piece = cutter(wo_hi[:, :, :].rearrange("p h e -> p (h e)"))
        hid_hi, hid2_both, dn_hi, dn2_both = piece([CAP], F32R), piece([CAP], F32R), piece([E], F32R), piece([E], F32R)
        piece = cutter(wo_lo[:, :, :].rearrange("p h e -> p (h e)"))
        hid_lo, dn_lo, dn2_lo = piece([CAP], F32R), piece([E], F32R), piece([E], F32R)
        split_hi, split_lo = (sb(n, [P, EO * CAP], F32R) for n in ("split_hi", "split_lo"))
        w0_hi, w0_lo = (s[:, 0:EO * 3 * P].rearrange("p (o n) -> p o n", o=EO) for s in (split_hi, split_lo))
        pt_hi, pt_lo = (s[:, 0:PACKED] for s in (split_hi, split_lo))
        OC = HG // 2
        oc_hi, oc_lo = (s[:, 0:HG * P].rearrange("p (c h t) -> p c h t", c=OC, h=2) for s in (split_hi, split_lo))
        xg_hi, xg_lo = (s[:, :].rearrange("p (o n) -> p o n", o=EO) for s in (split_hi, split_lo))
        xn2 = work[:, 0:T * E // P].rearrange("p (t e) -> p t e", t=TILES)
        y_n = work[:, T * E // P:T * E // P + TPB * E].rearrange("p (t e) -> p t e", t=TPB)
        GR = 24
        got = work[:, 0:GR * E].rearrange("p (r e) -> p r e", r=GR)
        piece = cutter(rope_sb)
        logit_rows = piece([SEQ])
        logit, top, top_f = (piece([TILES, NE]) for _ in range(3))
        top_at = piece([TILES, NE], U32)
        piece = cutter(work, T * E // P + TPB * E)
        shift = piece([TILES])
        oh = piece([2, TILES, NE])
        pos_sb, pos_oh = piece([TILES, NE]), piece([2, TILES, NE])
        out_shift = cutter(rope_sb)([TILES])
        rt_raw = sb("rt_raw", [P, EO, 32])
        rt_hi = sb("rt_hi", [P, EO, 32], F32R)
        rt_lo = sb("rt_lo", [P, EO, 32], F32R)
        before_b = sb("before_b", [P, P], BF16)
        ones_b = sb("ones_b", [P, P], BF16)
        iota_sb = sb("iota_sb", [P, NE])
        chosen = sb("chosen", [P, TILES, NE], BF16)
        prior = sb("prior", [P, TILES + 1, NE], BF16)
        gap = sb("gap", [P, TILES])
        egap = sb("egap", [P, TILES])
        den = sb("den", [P, TILES])
        cw = sb("cw", [P, 2, TILES])
        slot, slot_in = piece([2, TILES]), piece([2, TILES])
        pos, keep = (sb(n, [P, 2, TILES]) for n in ("pos", "keep"))
        at_in = sb("at_in", [P, 2, TILES], U32)
        at_out = sb("at_out", [P, 2, TILES], U32)

        id_in, rope_in, consts_in, w0_in, wo_in = (
            sem("id_in"), sem("rope_in"), sem("consts_in"), sem("w0_in"), sem("wo_in"))
        x_in = [sem(f"x_in{b}") for b in range(B)]
        wq_in = sem("wq_in")
        kh_row_in = [sem(f"kh_row_in{r}") for r in range(2)]
        kvh_stored = sem("kvh_stored")
        dve_c = sem("dve_c")
        w0_hi_ready, w0_split, rt_hi_ready, consts_made = (
            sem("w0_hi_ready"), sem("w0_split"), sem("rt_hi_ready"), sem("consts_made"))
        var_ready, std_ready, xn_ready = sem("var_ready"), sem("std_ready"), sem("xn_ready")
        xt_psum, xt_hi_ready, xt_lo_ready = sem("xt_psum"), sem("xt_hi_ready"), sem("xt_lo_ready")
        k_psum, k_swapped, k_cos_ready, k_sin_ready, kt_ready = (
            sem("k_psum"), sem("k_swapped"), sem("k_cos_ready"), sem("k_sin_ready"), sem("kt_ready"))
        gate_psum, gate_copied, v_psum = sem("gate_psum"), sem("gate_copied"), sem("v_psum")
        v_hi_ready, v_ready = sem("v_hi_ready"), sem("v_ready")
        f_ready, hc_ready, vcol_psum, vcol_ready = sem("f_ready"), sem("hc_ready"), sem("vcol_psum"), sem("vcol_ready")
        wq_hi_ready, wq_ready = sem("wq_hi_ready"), sem("wq_ready")
        q_psum, q_swapped, q_cos_ready, q_sin_ready, q_ready = (
            sem("q_psum"), sem("q_swapped"), sem("q_cos_ready"), sem("q_sin_ready"), sem("q_ready"))
        kh_ready = sem("kh_ready")
        s_psum, max_ready, exp_ready, inv_ready, prob_ready = (
            sem("s_psum"), sem("max_ready"), sem("exp_ready"), sem("inv_ready"), sem("prob_ready"))
        pt_psum, pt_free, pt_hi_ready, pt_ready = sem("pt_psum"), sem("pt_free"), sem("pt_hi_ready"), sem("pt_ready")
        o_psum, o_free, o_ready = sem("o_psum"), sem("o_free"), sem("o_ready")
        wo_hi_ready, wo_ready = sem("wo_hi_ready"), sem("wo_ready")
        oc_hi_ready, oc_used, proj_psum, proj_taken = (
            sem("oc_hi_ready"), sem("oc_used"), sem("proj_psum"), sem("proj_taken"))
        oc_ready = {"pool": sem("oc_ready_pool"), "dve": sem("oc_ready_dve")}
        xt2_psum, xt2_hi, xt2_lo = sem("xt2_psum"), sem("xt2_hi"), sem("xt2_lo")
        var2_ready, std2_ready, shift_ready = sem("var2_ready"), sem("std2_ready"), sem("shift_ready")
        y_n_ready, xn2_ready, out_normed = sem("y_n_ready"), sem("xn2_ready"), sem("out_normed")
        x_again = [sem(f"x_again{b}") for b in range(B)]
        zeros_made, slots_cleared = sem("zeros_made"), sem("slots_cleared")
        sw_in, sdn_in, sw_split_hi, sw_split = sem("sw_in"), sem("sdn_in"), sem("sw_split_hi"), sem("sw_split")
        s_psum_g, s_silu, s_hid_ready, sy_psum, sy_taken = (
            sem("s_psum_g"), sem("s_silu"), sem("s_hid_ready"), sem("sy_psum"), sem("sy_taken"))
        logit_psum, logit_copied, token_psum = (
            sem("logit_psum"), sem("logit_copied"), sem("token_psum"))
        gap_ready, egap_ready, rows_known = sem("gap_ready"), sem("egap_ready"), sem("rows_known")
        chosen_ready, pos_psum, pos_taken, slots_ready = (
            sem("chosen_ready"), sem("pos_psum"), sem("pos_taken"), sem("slots_ready"))
        scattered = sem("scattered")
        xg_in, up_in, dn_in = ([sem(f"{n}{r}") for r in range(2)] for n in ("xg_in", "up_in", "dn_in"))
        up_hi_ready, up_ready = sem("up_hi_ready"), sem("up_ready")
        xg_psum, xg_hi_ready, xg_ready = sem("xg_psum"), sem("xg_hi_ready"), sem("xg_ready")
        gu_psum, silu_ready, gu_free = sem("gu_psum"), sem("silu_ready"), sem("gu_free")
        pad_ready, hid_hi_ready, hid_ready = sem("pad_ready"), sem("hid_hi_ready"), sem("hid_ready")
        dn_hi_ready, dn_ready = sem("dn_hi_ready"), sem("dn_ready")
        yo_psum, yo_ready, yo_stored = sem("yo_psum"), sem("yo_ready"), sem("yo_stored")
        got_in = [sem(f"got_in{r}") for r in range(GR)]
        got_used = sem("got_used")
        out_ready = {"pool": sem("out_ready_pool"), "dve": sem("out_ready_dve")}
        stored = sem("stored")

        LAST_LN = [(b * TPB, (b + 1) * TPB) for b in range(B - 1)] + [(t, t + 2) for t in (TILES - 4, TILES - 2)]

        def tok(b):
            return slice(b * SEQ, (b + 1) * SEQ)

        XG_BANKS = [(0, 0), (1, 1), (2, None)]
        XG_W = 4 * P

        def xg_src(bank):
            return ps[2][:, 0:EO * P].rearrange("p (o n) -> p o n", o=EO) if bank == 2 else ps[bank][:]

        def xg_dst(buf, o):
            return buf[:, :, XG_W:CAP] if o is None else buf[:, o, 0:XG_W]

        YO_BANKS = [(0, 2), (2, 2), (4, 1)]

        def first_turn_bank(b, o):
            return ((4, 5), (6, 1))[b % 2][o]

        def gate_bank(b):
            return 2 + b % 2

        def turn_bank(b, o):
            return (3, 3, 6, 0)[b] + o

        GROUPS = [tuple(range(B - 2)), (B - 2,), (B - 1,)]
        LOGIT_BANKS = [(0, 2), (6,), (6,)]
        TOKEN_BANK = [6, 7, 7]
        POS_AT = 256

        def group_tiles(g):
            return slice(GROUPS[g][0] * TPB, (GROUPS[g][-1] + 1) * TPB)

        def sw_cols(i):
            g = 2 * P * i
            return (g, g + SHW[i]), (g + SHW[i], g + 2 * SHW[i])

        def three_pass(pe, psum, w_hi, w_lo, m_hi, m_lo):
            for o in range(EO):
                for j, (w, m) in enumerate(((w_hi, m_hi), (w_hi, m_lo), (w_lo, m_hi))):
                    last = pe.matmul(psum, w(o), m(o), start=(o == 0 and j == 0),
                                     stop=(o == EO - 1 and j == 2))
            return last

        block = ctx.enter_context(nc.Block())

        @block.sync
        def _(sp):
            sp.dma_start(x_sb[:, 0:TPB, :], x_v[0]).then_inc(x_in[0], 16)
            sp.dma_start(id_f[:], ident).then_inc(id_in, 16)
            sp.dma_start(w0_raw, w0).then_inc(w0_in, 16)
            for b in range(1, B):
                sp.dma_start(x_sb[:, b * TPB:(b + 1) * TPB, :], x_v[b]).then_inc(x_in[b], 16)
            sp.dma_start(causal_f, causal).then_inc(consts_in, 16)
            sp.dma_start(iota_sb[:], iota8).then_inc(consts_in, 16)
            sp.dma_start(rt_raw[:], router).then_inc(consts_in, 16)
            sp.dma_start(wo_raw[:], wout[0]).then_inc(wo_in, 16)
            sp.dma_start(before_f, before).then_inc(consts_in, 16)
            sp.wait_ge(zeros_made, 1)
            for n in range(4):
                sp.dma_start(xg_dram.rearrange("(p s) e -> p s e", p=P)[:, n * 10:(n + 1) * 10, :], zeros) \
                    .then_inc(slots_cleared, 16)
            sp.wait_ge(hc_ready, 1)
            sp.dma_start(kvh_dram, hc_t).then_inc(kvh_stored, 16)
            sp.wait_ge(kvh_stored, 16)
            for i in range(2):
                sp.dma_start(kh_row[:, i, :], kvh_dram[i * 2 * H:i * 2 * H + 1, :].to_broadcast([P, SEQ])) \
                    .then_inc(kh_row_in[i], 16)
            sp.dma_start(sw_raw[0], sw_up[0]).then_inc(sw_in, 16)

            def steps(h, last):
                for b in range(B):
                    if b == 0 and not last:
                        sp.wait_ge(wq_ready, h + 1)
                        sp.dma_start(wq_raw[:], wq[bass.ds(h + 1, 1), :, :, :].rearrange("h p o d -> (h p) o d")) \
                            .then_inc(wq_in, 16)
                    if b == 2 and not last:
                        sp.wait_ge(wo_ready, h + 1)
                        sp.dma_start(wo_raw[:], wout[bass.ds(h + 1, 1), :, :].rearrange("h d e -> (h d) e")) \
                            .then_inc(wo_in, 16)
                    if last and b + 2 >= B:
                        continue
                    b2, h2 = (b + 2) % B, h + (b + 2) // B
                    sp.wait_ge(kh_ready, h * B + b + 1)
                    sp.dma_start(kh_row[:, b % 2, :],
                                 kvh_dram[bass.ds(h2 + 2 * H * b2, 1), :].to_broadcast([P, SEQ])) \
                        .then_inc(kh_row_in[b % 2], 16)

            with sp.Fori(0, H - 1) as h:
                steps(h, False)
            steps(H - 1, True)

            sp.wait_ge(pt_psum, 3 * UNITS)
            for b in range(B):
                if b == 2:
                    sp.wait_ge(sw_split, 1)
                sp.dma_start(x_sb[:, b * TPB:(b + 1) * TPB, :], x_v[b]).then_inc(x_again[b], 16)
            sp.wait_ge(proj_psum, 2 * TILES)
            sp.dma_start(sdn_sb, sw_dn).then_inc(sdn_in, 16)

            sp.sem_inc(yo_stored, 16)

            def load_expert(e, r):
                sp.dma_start(up_raw[:, r, :, :], w_up[bass.ds(e, 1), :, :, :].rearrange("n p o c -> (n p) o c")) \
                    .then_inc(up_in[r], 16)

            def load_down(e, r):
                sp.dma_start(dn_sb[:, r, :, :], w_dn[bass.ds(e, 1), :, :, :].rearrange("n p k c -> (n p) k c")) \
                    .then_inc(dn_in[r], 16)

            def load_slots(e, r):
                sp.dma_start(xg[:, r, :, :], xg_dram[bass.ds(e * CAP, CAP), :].rearrange("(p s) e -> p s e", p=P)) \
                    .then_inc(xg_in[r], 16)

            for e in range(2):
                load_expert(e, e)
                load_down(e, e)
            sp.dma_start(sw_raw[1], sw_up[1]).then_inc(sw_in, 16)
            sp.wait_ge(scattered, 2 * TILES * 16)
            for e in range(2):
                load_slots(e, e)

            def expert_steps(e0, last):
                for r in range(2):
                    e = e0 + r
                    if not last:
                        sp.wait_ge(xg_psum, 3 * e + 3)
                        load_slots(e + 2, r)
                        sp.wait_ge(up_ready, e + 1)
                        load_expert(e + 2, r)
                    sp.wait_ge(yo_ready, 3 * e + 6)
                    sp.dma_start(yg_dram[bass.ds(e * CAP, CAP), :].rearrange("(p s) e -> p s e", p=P), yo) \
                        .then_inc(yo_stored, 16)
                    if not last:
                        load_down(e + 2, r)

            with sp.Fori(0, NE // 2 - 1) as pair:
                expert_steps(pair * 2, False)
            expert_steps(NE - 2, True)
            for t0, t1 in LAST_LN:
                b = t0 // TPB
                if b < B - 1:
                    sp.wait_ge(out_ready["pool"], t1)
                else:
                    sp.wait_ge(out_ready["dve"], t1 - (B - 1) * TPB)
                sp.dma_start(out_v[b, :, t0 - b * TPB:t1 - b * TPB, :], y_sb[:, t0:t1, :]).then_inc(stored, 16)
            sp.wait_ge(stored, 16 * len(LAST_LN))

        @block.scalar
        def _(act):
            act.dma_start(cos_sb, cos_t).then_inc(rope_in, 16)
            act.dma_start(sin_sb, sin_t).then_inc(rope_in, 16)
            act.dma_start(wq_raw[:], wq[0]).then_inc(wq_in, 16)
            def std_of(b):
                act.wait_ge(var_ready, (b + 1) * TPB)
                act.activation(std[:, b * TPB:(b + 1) * TPB], mv[:, b * TPB:(b + 1) * TPB, 1], ACT.Sqrt,
                               bias=eps_sb[:, 0:1]).then_inc(std_ready, 1)

            def head_of(b):
                for o in range(EO):
                    act.wait_ge(xt_psum, b * EO + o + 1)
                    act.copy(xt_hi[:, o, tok(b)], ps[first_turn_bank(b, o)][:]).then_inc(xt_hi_ready, 1)

            def gates_of(b):
                act.wait_ge(gate_psum, b + 1)
                rows, src = slice(2 * H * b, 2 * H * (b + 1)), ps[gate_bank(b)]
                act.copy(kvh_t[rows, :], src[0:2 * H, :])
                act.copy(f_t[rows, :], src[2 * H:4 * H, :]).then_inc(gate_copied, 1)

            def swapped_keys(b):
                act.wait_ge(k_psum, b + 1)
                if b:
                    act.wait_ge(kt_ready, b)
                act.mul(q_sw[0:64, :], ps_q[64:128, :], SCALE)
                act.mul(q_sw[64:128, :], ps_q[0:64, :], SCALE).then_inc(k_swapped, 1)

            def values_of(b):
                act.wait_ge(v_psum, b + 1)
                act.copy(vp_hi[:, b * TPB:(b + 1) * TPB, :], ps_o[:]).then_inc(v_hi_ready, 1)

            std_of(0)
            head_of(0)
            std_of(1)
            gates_of(0)
            head_of(1)
            std_of(2)
            swapped_keys(0)
            head_of(2)
            values_of(0)
            std_of(3)
            gates_of(1)
            swapped_keys(1)
            head_of(3)
            gates_of(2)
            values_of(1)
            gates_of(3)
            swapped_keys(2)
            act.wait_ge(gate_copied, B)
            act.activation(f_t, f_t, ACT.Sigmoid).then_inc(f_ready, 1)
            values_of(2)
            swapped_keys(3)

            def swap_q(i):
                act.wait_ge(q_psum, i + 1)
                act.copy(q_sw[0:64, :], ps_q[64:128, :])
                act.copy(q_sw[64:128, :], ps_q[0:64, :]).then_inc(q_swapped, 1)

            def bank_exps(i, r, k):
                act.wait_ge(max_ready, 3 * i + (k + 1))
                for nt in S_BANKS[k]:
                    bank, at = s_slot(nt)
                    w = P * (nt + 1)
                    ins = act.activation(prob[:, r, ROW_AT[nt]:ROW_AT[nt] + w], ps_s[bank][:, at:at + w], ACT.Exp,
                                         bias=neg_max[:, r, nt:nt + 1], accum_out=row_sum[:, r, nt:nt + 1])
                ins.then_inc(exp_ready, 1)

            act.wait_ge(kt_ready, B)
            swap_q(0)
            act.wait_ge(vcol_psum, 1)
            act.copy(vcol[:].rearrange("p m (b h) -> p m b h", b=B),
                     ps_s[2][:].rearrange("p (m b c) -> p m b c", m=TPB, b=B)[:, :, :, H:]).then_inc(vcol_ready, 1)
            values_of(3)
            act.wait_ge(q_ready, 1)
            swap_q(1)
            for k in range(3):
                bank_exps(0, 0, k)
            act.wait_ge(q_ready, 2)
            swap_q(2)

            def steps(h, slot, last):
                for b in range(B):
                    i = h * B + b
                    has_next = not (last and b + 1 >= B)
                    if has_next:
                        bank_exps(i + 1, (b + 1) % 2, 0)
                    for k, tiles in enumerate(PT_BANKS):
                        act.wait_ge(pt_psum, 3 * i + (k + 1))
                        for mt in tiles:
                            bank, at = pt_slot(mt)
                            w = SEQ - mt * P
                            ins = act.activation(pt_hi[:, COL_AT[mt]:COL_AT[mt] + w], ps_pt[bank][:, at:at + w],
                                                 ACT.Copy, scale=vcol[:, mt, bass.ds(h + b * H, 1)])
                        ins.then_inc(pt_hi_ready, 1)
                    if has_next:
                        bank_exps(i + 1, (b + 1) % 2, 1)
                        bank_exps(i + 1, (b + 1) % 2, 2)
                    if not (last and b + 3 >= B):
                        act.wait_ge(q_ready, i + 3)
                        swap_q(i + 3)
                    act.wait_ge(o_psum, i + 1)
                    act.copy(o_t[:, slot, tok(b)] if isinstance(slot, int) else
                             o_t[:, bass.ds(slot, 1), tok(b)].rearrange("p a t -> p (a t)"), ps_o[:]) \
                        .then_inc(o_free, 1)

            def head_of_outputs(g, t):
                for c in range(OC):
                    if c < OC - 1:
                        act.wait_ge(oc_used, (g * TILES + t) * (OC - 1) + (c + 1))
                    elif not (isinstance(t, int) and g * TILES + t == 0):
                        act.wait_ge(proj_psum, g * TILES + t)
                    act.copy(oc_hi[:, c, :, :], o_t[:, 2 * c:2 * c + 2, bass.ds(t * P, P)]).then_inc(oc_hi_ready, 1)

            with act.Fori(0, HG) as h:
                steps(h, h, False)
            act.wait_ge(o_free, HG * B + 1)
            head_of_outputs(0, 0)
            with act.Fori(1, TILES) as t:
                head_of_outputs(0, t)
            with act.Fori(HG, H - 1) as h:
                steps(h, h - HG, False)
            steps(H - 1, HG - 1, True)
            act.wait_ge(o_free, UNITS + 1)

            def turned_head(b):
                for o in range(EO):
                    act.wait_ge(xt2_psum, b * EO + o + 1)
                    act.copy(xt_hi[:, o, tok(b)], ps[turn_bank(b, o)][:]).then_inc(xt2_hi, 1)

            def silus(j, tiles=range(SH)):
                for i in tiles:
                    act.wait_ge(s_psum_g, 2 * (j * SH + i) + 1)
                    act.activation(s_sg[0:SHW[i], i, :], ps[2 * i][0:SHW[i], :], ACT.Silu).then_inc(s_silu, 1)

            def logits_copied(g):
                act.wait_ge(logit_psum, g + 1)
                for n, bank in enumerate(LOGIT_BANKS[g]):
                    ins = act.copy(logit_rows[32 * n:32 * (n + 1), :], ps[bank][0:32, :])
                ins.then_inc(logit_copied, 1)

            def deviations(b, k):
                act.wait_ge(var2_ready, 2 * b + k + 1)
                act.activation(std[:, b * TPB:(b + 1) * TPB], mv[:, b * TPB:(b + 1) * TPB, 1], ACT.Sqrt,
                               bias=eps_sb[:, 0:1]).then_inc(std2_ready, 1)

            def y_normed(b):
                act.wait_ge(shift_ready, 2 * b + 1)
                for t in range(TPB):
                    g = b * TPB + t
                    act.activation(y_n[:, t, :], y_sb[:, g, :], ACT.Identity, scale=rstd[:, g:g + 1],
                                   bias=shift[:, g:g + 1]).then_inc(y_n_ready, 1)

            def x_normed(b):
                act.wait_ge(shift_ready, 2 * b + 2)
                for t in range(TPB):
                    g = b * TPB + t
                    act.activation(xn2[:, g, :], x_sb[:, g, :], ACT.Identity, scale=rstd[:, g:g + 1],
                                   bias=shift[:, g:g + 1]).then_inc(xn2_ready, 1)

            for t in range(TILES):
                b, k = t // TPB, t % TPB
                head_of_outputs(1, t)
                if k == 0 and b >= 2:
                    deviations(b - 2, 1)
                if k == 1 and b:
                    deviations(b - 1, 0)
                if k == 1 and b >= 2:
                    x_normed(b - 2)
                if k == 2 and b:
                    y_normed(b - 1)
                if k == 3 and b >= 2:
                    turned_head(b - 2)
            logits_copied(0)
            deviations(B - 2, 1)
            deviations(B - 1, 0)
            x_normed(B - 2)
            y_normed(B - 1)
            silus(0)
            turned_head(B - 2)
            logits_copied(1)
            silus(1, [0])
            deviations(B - 1, 1)
            x_normed(B - 1)
            silus(1, range(1, SH))
            turned_head(B - 1)
            logits_copied(2)
            silus(2)
            silus(3)
            act.wait_ge(gap_ready, 1)
            act.activation(egap[:], gap[:], ACT.Exp).then_inc(egap_ready, 1)

            def expert_head(e):
                for k, (bank, dst) in enumerate(XG_BANKS):
                    act.wait_ge(xg_psum, 3 * e + (k + 1))
                    act.copy(xg_dst(xg_hi, dst), xg_src(bank)).then_inc(xg_hi_ready, 1)

            def expert_steps(e0, last):
                for r in range(2):
                    e = e0 + r
                    for c in range(2):
                        act.wait_ge(gu_psum, 3 * (2 * e + c) + 1)
                        act.activation(sg[:, c, :], ps[3][:, 0:HC], ACT.Silu).then_inc(silu_ready, 1)
                        act.wait_ge(gu_psum, 3 * (2 * e + c) + 3)
                        act.activation(sg2[0:H2, c, :], ps[5][0:H2, 0:HC], ACT.Silu).then_inc(silu_ready, 1)
                        if c == 0:
                            down_head(e, r)
                    if not (last and r == 1):
                        expert_head(e + 1)
                    act.wait_ge(yo_stored, 16 * e + 16)
                    for k, (t0, n) in enumerate(YO_BANKS):
                        act.wait_ge(yo_psum, 3 * e + (k + 1))
                        act.copy(yo[:, t0:t0 + n, :], ps[6 + k % 2][:, 0:n * E]).then_inc(yo_ready, 1)

            def down_head(e, r):
                act.wait_ge(dn_in[r], 8 * (e - r) + 16)
                act.copy(dn_hi, dn_sb[:, r, 0, :])
                act.copy(dn2_both[0:LO, :], dn_sb[0:LO, r, 1, :])
                act.copy(dn2_both[LO:LO + H2, :], dn_sb[0:H2, r, 1, :]).then_inc(dn_hi_ready, 1)

            act.sem_inc(yo_ready, 3)
            expert_head(0)
            with act.Fori(0, NE // 2 - 1) as pair:
                expert_steps(pair * 2, False)
            expert_steps(NE - 2, True)
            silus(B)
            for n, (t0, t1) in enumerate(LAST_LN):
                if n + 1 < B:
                    silus(B + n + 1)
                act.wait_ge(var2_ready, 2 * B + n + 1)
                act.activation(std[:, t0:t1], mv[:, t0:t1, 1], ACT.Sqrt, bias=eps_sb[:, 0:1]).then_inc(std2_ready, 1)
                act.wait_ge(shift_ready, 2 * B + n + 1)
                for t in range(t0, t1):
                    act.activation(y_sb[:, t, :], y_sb[:, t, :], ACT.Identity, scale=rstd[:, t:t + 1],
                                   bias=out_shift[:, t:t + 1]).then_inc(out_normed, 1)

        @block.tensor
        def _(pe):
            pe.wait_ge(id_in, 16)

            def turn_x(b):
                pe.wait_ge(xn_ready, (b + 1) * TPB)
                if b >= 2:
                    pe.wait_ge(xt_lo_ready, (b - 1) * EO)
                for o in range(EO):
                    for t in range(TPB):
                        ins = pe.transpose(ps[first_turn_bank(b, o)][:, t * P:(t + 1) * P],
                                           xn[:, b % 2, t, o * P:(o + 1) * P], id_f[:])
                    ins.then_inc(xt_psum, 1)

            def project_rows(psum, cols, b):
                return three_pass(pe, psum, lambda o: w0_hi[:, o, cols], lambda o: w0_lo[:, o, cols],
                                  lambda o: xt_hi[:, o, tok(b)], lambda o: xt_lo[:, o, tok(b)])

            def gates(b):
                pe.wait_ge(w0_split, 1)
                pe.wait_ge(xt_lo_ready, (b + 1) * EO)
                if b >= 2:
                    pe.wait_ge(gate_copied, b - 1)
                project_rows(ps[gate_bank(b)][:], slice(2 * P, 3 * P), b).then_inc(gate_psum, 1)

            def keys(b):
                if b:
                    pe.wait_ge(k_cos_ready, b)
                project_rows(ps_q[:], slice(0, P), b).then_inc(k_psum, 1)

            def values(b):
                if b:
                    pe.wait_ge(v_ready, b)
                for t in range(TPB):
                    ts = slice(b * SEQ + t * P, b * SEQ + (t + 1) * P)
                    ins = three_pass(pe, ps_o[:, t * P:(t + 1) * P], lambda o: xt_hi[:, o, ts], lambda o: xt_lo[:, o, ts],
                                     lambda o: w0_hi[:, o, P:2 * P], lambda o: w0_lo[:, o, P:2 * P])
                ins.then_inc(v_psum, 1)

            turn_x(0)
            gates(0)
            turn_x(1)
            keys(0)
            values(0)
            turn_x(2)
            gates(1)
            keys(1)
            turn_x(3)
            gates(2)
            values(1)
            gates(3)
            keys(2)
            values(2)
            keys(3)

            def q_proj(i, b):
                three_pass(pe, ps_q[:], lambda o: wq_hi[:, o, :], lambda o: wq_lo[:, o, :],
                           lambda o: xt_hi[:, o, tok(b)], lambda o: xt_lo[:, o, tok(b)]).then_inc(q_psum, 1)

            def scores(i, r, first=False):
                pe.wait_ge(q_ready, i + 1)
                pe.wait_ge(kh_ready, i + 1)
                for k, tiles in enumerate(S_BANKS):
                    if not first:
                        pe.wait_ge(exp_ready, 3 * (i - 1) + (k + 1))
                    for nt in tiles:
                        bank, at = s_slot(nt)
                        w = P * (nt + 1)
                        pe.matmul(ps_s[bank][:, at:at + w], q_rot[:, r, nt * P:(nt + 1) * P], k_h[:, r, 0:w],
                                  start=(nt == tiles[0]), stop=False)
                    at, w = s_slot(tiles[0])[1] + P * tiles[0], P * len(tiles)
                    pe.matmul(ps_s[bank][:, at:at + w], id_b[:], causal_b[:, 0:len(tiles), :],
                              start=False, stop=True).then_inc(s_psum, 1)

            pe.wait_ge(consts_made, 1)
            pe.wait_ge(wq_ready, 1)
            pe.wait_ge(k_cos_ready, B)
            q_proj(0, 0)
            pe.wait_ge(hc_ready, 1)
            for mt in range(TPB):
                ins = pe.transpose(ps_s[2][:, mt * P:(mt + 1) * P], hc_t[:, mt * P:(mt + 1) * P], id_f[:])
            ins.then_inc(vcol_psum, 1)
            values(3)
            pe.wait_ge(q_cos_ready, 1)
            q_proj(1, 1)
            pe.wait_ge(vcol_ready, 1)
            scores(0, 0, first=True)
            pe.wait_ge(q_cos_ready, 2)
            q_proj(2, 2)

            def steps(h, last):
                for b in range(B):
                    i = h * B + b
                    if not (last and b + 1 >= B):
                        scores(i + 1, (b + 1) % 2)
                    pe.wait_ge(prob_ready, i + 1)
                    pe.wait_ge(pt_free, 3 * i + 3)
                    for tiles in PT_BANKS:
                        for mt in tiles:
                            bank, at = pt_slot(mt)
                            for nt in range(mt, NT):
                                src = ROW_AT[nt] + mt * P
                                dst = at + (nt - mt) * P
                                ins = pe.transpose(ps_pt[bank][:, dst:dst + P], prob[:, b % 2, src:src + P], id_f[:])
                        ins.then_inc(pt_psum, 1)
                    if not (last and b + 3 >= B):
                        pe.wait_ge(q_cos_ready, i + 3)
                        if b == 1:
                            pe.wait_ge(wq_ready, h + 2)
                        q_proj(i + 3, (b + 3) % B)
                    pe.wait_ge(o_free, i + 1)
                    for k, tiles in enumerate(PT_BANKS):
                        pe.wait_ge(pt_ready, 3 * i + (k + 1))
                        for mt in tiles:
                            cols = slice(COL_AT[mt], COL_AT[mt] + SEQ - mt * P)
                            for j, (v, p_) in enumerate(((vp_hi, pt_hi), (vp_lo, pt_hi), (vp_hi, pt_lo))):
                                ins = pe.matmul(ps_o[:, mt * P:SEQ], v[:, b * TPB + mt, :], p_[:, cols],
                                                start=(mt == 0 and j == 0),
                                                stop=(mt == PT_BANKS[-1][-1] and j == 2))
                    ins.then_inc(o_psum, 1)

            def project(g, t, bank):
                pe.wait_ge(proj_taken, g * TILES + t + 1)
                for c in range(OC):
                    if g == 0 or t < TPB:
                        pe.wait_ge(oc_ready[("pool", "dve")[c % 2]], (g * TILES + t) * (OC // 2) + (c // 2 + 1))
                    else:
                        pe.wait_ge(oc_ready["pool"], (TILES + TPB) * OC // 2 + (t - TPB) * OC + (c + 1))
                    for hh in range(2):
                        for j, (o_, w) in enumerate(((oc_hi, wo_hi), (oc_hi, wo_lo), (oc_lo, wo_hi))):
                            ins = pe.matmul(bank[:, 0:E], o_[:, c, hh, :], w[:, 2 * c + hh, :],
                                            start=(c == 0 and hh == 0 and j == 0),
                                            stop=(c == OC - 1 and hh == 1 and j == 2))
                    ins.then_inc(oc_used if c < OC - 1 else proj_psum, 1)

            def logits(g):
                for n, b in enumerate(GROUPS[g]):
                    pe.wait_ge(xt2_lo, (b + 1) * EO)
                    ins = three_pass(pe, ps[LOGIT_BANKS[g][n]][0:32, :], lambda o: rt_hi[:, o, :],
                                     lambda o: rt_lo[:, o, :], lambda o: xt_hi[:, o, tok(b)], lambda o: xt_lo[:, o, tok(b)])
                ins.then_inc(logit_psum, 1)

            def turn_logits(g):
                pe.wait_ge(logit_copied, g + 1)
                n = 32 * len(GROUPS[g])
                for t in range(TPB):
                    ins = pe.transpose(ps[TOKEN_BANK[g]][:, t * n:(t + 1) * n], logit_rows[0:n, t * P:(t + 1) * P],
                                       id_f[0:n, 0:n])
                ins.then_inc(token_psum, 1)

            def positions(g):
                pe.wait_ge(chosen_ready, g + 1)
                ts = group_tiles(g)
                dst = ps[TOKEN_BANK[g]][:, POS_AT:POS_AT + (ts.stop - ts.start) * NE]
                pe.matmul(dst, before_b[:], chosen[:, ts, :].rearrange("p t e -> p (t e)"), start=True, stop=False)
                pe.matmul(dst, ones_b[:], prior[:, ts, :].rearrange("p t e -> p (t e)"), start=False, stop=True) \
                    .then_inc(pos_psum, 1)

            def turn(b):
                pe.wait_ge(xn2_ready, (b + 1) * TPB)
                for o in range(EO):
                    if 0 < b < B - 1:
                        pe.wait_ge(xt2_lo, (b - 1) * EO + o + 1)
                    for t in range(TPB):
                        ins = pe.transpose(ps[turn_bank(b, o)][:, t * P:(t + 1) * P],
                                           xn2[:, b * TPB + t, o * P:(o + 1) * P], id_f[:])
                    ins.then_inc(xt2_psum, 1)

            with pe.Fori(0, HG) as h:
                steps(h, False)
            pe.sem_inc(oc_used, OC - 1)
            pe.wait_ge(wo_ready, HG)
            pe.wait_ge(pt_free, 3 * HG * B + 3)
            with pe.Fori(0, TILES // 2) as pair:
                for r in range(2):
                    project(0, pair * 2 + r, ps_pt[r])
            pe.wait_ge(proj_taken, TILES + 2)
            with pe.Fori(HG, H - 1) as h:
                steps(h, False)
            steps(H - 1, True)
            pe.wait_ge(wo_ready, H)
            pe.wait_ge(o_free, UNITS + 1)
            for t in range(TILES):
                project(1, t, ps[5 + t % 2 * 2])
                if t % TPB == 2 and t >= 2 * TPB:
                    turn(t // TPB - 2)
            logits(0)

            def shared_up(j, tiles=range(SH)):
                c = j % B
                for i in tiles:
                    if j % B:
                        pe.wait_ge(s_hid_ready, (j - 1) * SH + i + 1)
                    for k, (a, z) in enumerate(sw_cols(i)):
                        three_pass(pe, ps[2 * i + k][0:z - a, :], lambda o: sw_hi[:, o, a:z], lambda o: sw_lo[:, o, a:z],
                                   lambda o: xt_hi[:, o, tok(c)], lambda o: xt_lo[:, o, tok(c)]).then_inc(s_psum_g, 1)

            def shared_down(j):
                n = j // B
                pe.wait_ge(s_hid_ready, (j + 1) * SH)
                for half in range(2):
                    if j % B:
                        pe.wait_ge(sy_taken, 2 * j - 1 + half)
                    if j in (0, 2) and half == 1:
                        pe.wait_ge(pos_taken, 2 + j // 2)
                    for q in range(2):
                        t = 2 * half + q
                        for i in range(SH):
                            ins = pe.matmul(ps[6 + half][:, q * E:(q + 1) * E],
                                            s_hid[0:SHW[i], j % 2, i, t * P:(t + 1) * P], sdn_sb[0:SHW[i], n, i, :],
                                            start=(i == 0), stop=(i == SH - 1))
                    ins.then_inc(sy_psum, 1)

            pe.wait_ge(sw_split, 1)
            pe.wait_ge(proj_taken, 2 * TILES + 2)
            turn_logits(0)
            shared_up(0, [0, 1])
            positions(0)
            shared_up(0, range(2, SH))
            pe.wait_ge(pos_taken, 1)
            turn(B - 2)
            shared_up(1, [0])
            logits(1)
            shared_up(1, [1])
            turn_logits(1)
            shared_up(1, range(2, SH))
            positions(1)
            pe.wait_ge(sdn_in, 16)
            shared_down(0)
            pe.wait_ge(s_hid_ready, SH + 1)
            turn(B - 1)
            shared_down(1)
            pe.wait_ge(sy_taken, 4)
            logits(2)
            shared_up(2, [0])
            turn_logits(2)
            shared_up(2, range(1, SH))
            positions(2)
            shared_up(3)
            shared_down(2)
            shared_down(3)

            def turn_slots(e, r):
                pe.wait_ge(xg_in[r], 8 * (e - r) + 16)
                for k in range(EO):
                    for t in range(4):
                        ins = pe.transpose(ps[k][:, t * P:(t + 1) * P], xg[:, r, t, k * P:(k + 1) * P], id_f[:])
                    ins.then_inc(xg_psum, 1)
                for k in range(EO):
                    ins = pe.transpose(ps[2][:, k * P:(k + 1) * P], xg[:, r, 4, k * P:(k + 1) * P], id_f[:])
                ins.then_inc(xg_psum, 1)

            def expert_up(e, r, c):
                m = 2 * e + c
                cs = slice(c * HC, (c + 1) * HC)
                w_hi_, w_lo_ = up_hl[r]
                for k, (a, z) in enumerate(((0, P), (P, 2 * P), (2 * P, UPW))):
                    if k == 0:
                        pe.wait_ge(gu_free, 2 * m + 1)
                    if k == 2:
                        pe.wait_ge(gu_free, 2 * m + 2)
                    three_pass(pe, ps[3 + k][0:z - a, 0:HC], lambda o: w_hi_[:, o, a:z], lambda o: w_lo_[:, o, a:z],
                               lambda o: xg_hi[:, o, cs], lambda o: xg_lo[:, o, cs]).then_inc(gu_psum, 1)

            def expert_down(e):
                pe.wait_ge(dn_ready, e + 1)
                for k, (t0, n) in enumerate(YO_BANKS):
                    if k < 2:
                        pe.wait_ge(hid_ready, 4 * e + 2 * k + 2)
                    pe.wait_ge(yo_ready, 3 * e + (3, 2, 4)[k])
                    for q in range(n):
                        ts = slice((t0 + q) * P, (t0 + q + 1) * P)
                        dst = ps[6 + k % 2][:, q * E:(q + 1) * E]
                        pe.matmul(dst, hid_hi[:, ts], dn_hi, start=True, stop=False)
                        pe.matmul(dst, hid_hi[:, ts], dn_lo, start=False, stop=False)
                        pe.matmul(dst, hid_lo[:, ts], dn_hi, start=False, stop=False)
                        pe.matmul(dst, hid2_both[0:LO + H2, ts], dn2_both[0:LO + H2, :], start=False, stop=False)
                        ins = pe.matmul(dst, hid2_both[0:H2, ts], dn2_lo[0:H2, :], start=False, stop=True)
                    ins.then_inc(yo_psum, 1)

            def expert_steps(e0, last):
                for r in range(2):
                    e = e0 + r
                    pe.wait_ge(xg_ready, 3 * e + 2)
                    pe.wait_ge(up_ready, e + 1)
                    expert_up(e, r, 0)
                    pe.wait_ge(xg_ready, 3 * e + 3)
                    expert_up(e, r, 1)
                    if not (last and r == 1):
                        turn_slots(e + 1, 1 - r)
                    expert_down(e)

            pe.wait_ge(s_hid_ready, B * SH)
            turn_slots(0, 0)
            pe.wait_ge(sy_taken, 2 * B)
            with pe.Fori(0, NE // 2 - 1) as pair:
                expert_steps(pair * 2, False)
            expert_steps(NE - 2, True)

            pe.wait_ge(sw_split, 2)
            shared_up(B)
            pe.wait_ge(yo_ready, 3 * NE + 3)
            for j in range(B, 2 * B):
                if j + 1 < 2 * B:
                    shared_up(j + 1)
                shared_down(j)

        @block.vector
        def _(dve):
            count = [0]

            def done(ins):
                count[0] += 1
                ins.then_inc(dve_c, 1)
                dve.wait_ge(dve_c, count[0])

            dve.memset(eps_sb[:], EPS)
            dve.memset(ones_b[:], 1.0)
            dve.memset(prior[:, 0, :], 0.0)
            done(dve.memset(ones_t, 1.0))

            def mean_var(b, src, ready):
                for t in range(b * TPB, (b + 1) * TPB):
                    ins = dve.bn_stats(stats[:, t, :], src[:, t, :])
                done(ins)
                for t in range(b * TPB, (b + 1) * TPB):
                    dve.bn_aggr(mv[:, t, :], stats[:, t, :]).then_inc(ready, 1)

            def inverse_std(b, ready, n):
                dve.wait_ge(ready, n)
                done(dve.reciprocal(rstd[:, b * TPB:(b + 1) * TPB], std[:, b * TPB:(b + 1) * TPB]))

            def normalize_x(b):
                inverse_std(b, std_ready, b + 1)
                dve.wait_ge(var_ready, (b + 1) * TPB)
                for t in range(TPB):
                    g = b * TPB + t
                    dve.tensor_scalar(xn[:, b % 2, t, :], x_sb[:, g, :], mv[:, g, 0:1], rstd[:, g:g + 1],
                                      ALU.subtract, ALU.mult).then_inc(xn_ready, 1)

            def rest_of(b):
                for o in range(EO):
                    dve.wait_ge(xt_hi_ready, b * EO + o + 1)
                    dve.tensor_tensor(xt_lo[:, o, tok(b)], ps[first_turn_bank(b, o)][:],
                                      xt_hi[:, o, tok(b)].bitcast(F32), ALU.subtract).then_inc(xt_lo_ready, 1)

            def cos_of_keys(b):
                if b:
                    dve.wait_ge(kt_ready, b)
                dve.wait_ge(k_swapped, b + 1)
                dve.scalar_tensor_tensor(q_cos, ps_q[:], SCALE, cos_sb, ALU.mult, ALU.mult) \
                    .then_inc(k_cos_ready, 1)

            def roped_keys(b):
                dve.wait_ge(k_cos_ready, b + 1)
                dve.wait_ge(k_sin_ready, b + 1)
                dve.tensor_tensor(kt[:, tok(b)], q_cos, q_sw, ALU.add).then_inc(kt_ready, 1)

            def rest_of_values(b):
                dve.wait_ge(v_hi_ready, b + 1)
                vs = slice(b * TPB, (b + 1) * TPB)
                dve.tensor_tensor(vp_lo[:, vs, :].rearrange("p t d -> p (t d)"), ps_o[:],
                                  vp_hi[:, vs, :].rearrange("p t d -> p (t d)").bitcast(F32),
                                  ALU.subtract).then_inc(v_ready, 1)

            def stats_of_x(b):
                dve.wait_ge(x_in[b], 16)
                mean_var(b, x_sb, var_ready)

            def split_wq(h):
                dve.wait_ge(wq_in, 16 * (h + 1))
                dve.tensor_copy(wq_hi[:], wq_raw[:]).then_inc(wq_hi_ready, 1)
                dve.wait_ge(wq_hi_ready, h + 1)
                dve.tensor_tensor(wq_lo[:], wq_raw[:], wq_hi[:].bitcast(F32), ALU.subtract).then_inc(wq_ready, 1)

            def factors():
                dve.memset(fcum_t[:, 0:1], 1.0)
                dve.wait_ge(f_ready, 1)
                done(dve.tensor_tensor_scan(fcum_t[:, 1:SEQ], f_t[:, 0:SEQ - 1], ones_t[:, 0:SEQ - 1], 1.0,
                                            ALU.mult, ALU.mult))
                done(dve.tensor_tensor(kvh_t, kvh_t, fcum_t, ALU.mult))
                dve.tensor_tensor_scan(hc_t, ones_t, kvh_t, 0.0, ALU.mult, ALU.add).then_inc(hc_ready, 1)

            stats_of_x(0)
            normalize_x(0)
            stats_of_x(1)
            rest_of(0)
            normalize_x(1)
            stats_of_x(2)
            rest_of(1)
            normalize_x(2)
            stats_of_x(3)
            dve.wait_ge(rope_in, 32)
            cos_of_keys(0)
            rest_of(2)
            roped_keys(0)
            rest_of_values(0)
            normalize_x(3)
            cos_of_keys(1)
            rest_of(3)
            roped_keys(1)
            rest_of_values(1)
            cos_of_keys(2)
            split_wq(0)
            roped_keys(2)
            factors()
            rest_of_values(2)
            cos_of_keys(3)
            roped_keys(3)

            def cos_q(i):
                dve.wait_ge(q_swapped, i + 1)
                dve.tensor_tensor(q_cos, ps_q[:], cos_sb, ALU.mult).then_inc(q_cos_ready, 1)

            def bank_maxima(i, r, k):
                dve.wait_ge(s_psum, 3 * i + (k + 1))
                for nt in S_BANKS[k]:
                    bank, at = s_slot(nt)
                    ins = dve.tensor_reduce(neg_max[:, r, nt:nt + 1], ps_s[bank][:, at:at + P * (nt + 1)],
                                            AX.X, ALU.max, negate=True)
                ins.then_inc(max_ready, 1)

            def rest_of_probs(h, b, k):
                dve.wait_ge(pt_hi_ready, 3 * (h * B + b) + (k + 1))
                for mt in PT_BANKS[k]:
                    bank, at = pt_slot(mt)
                    w = SEQ - mt * P
                    cols = slice(COL_AT[mt], COL_AT[mt] + w)
                    ins = dve.scalar_tensor_tensor(pt_lo[:, cols], ps_pt[bank][:, at:at + w],
                                                   vcol[:, mt, bass.ds(h + b * H, 1)],
                                                   pt_hi[:, cols].bitcast(F32), ALU.mult, ALU.subtract)
                ins.then_inc(pt_ready, 1)

            def bank_normalize(i, r, k):
                dve.wait_ge(exp_ready, 3 * i + (k + 1))
                tiles = S_BANKS[k]
                of_bank = slice(min(tiles), max(tiles) + 1, 2)
                dve.reciprocal(row_inv[:, r, of_bank], row_sum[:, r, of_bank]).then_inc(inv_ready, 1)
                dve.wait_ge(inv_ready, 3 * i + (k + 1))
                for nt in tiles:
                    w = P * (nt + 1)
                    p_ = prob[:, r, ROW_AT[nt]:ROW_AT[nt] + w]
                    ins = dve.tensor_scalar(p_, p_, row_inv[:, r, nt:nt + 1], None, ALU.mult)
                if k == len(S_BANKS) - 1:
                    ins.then_inc(prob_ready, 1)

            dve.wait_ge(kt_ready, B)
            cos_q(0)
            rest_of_values(3)
            dve.wait_ge(q_ready, 1)
            cos_q(1)
            for k in range(3):
                bank_maxima(0, 0, k)
            for k in range(3):
                bank_normalize(0, 0, k)
            dve.wait_ge(q_ready, 2)
            cos_q(2)
            dve.sem_inc(pt_free, 3)
            dve.sem_inc(o_free, 1)
            dve.wait_ge(vcol_ready, 1)

            def steps(h, last):
                for b in range(B):
                    i = h * B + b
                    has_next = not (last and b + 1 >= B)
                    if has_next:
                        for k in range(3):
                            bank_maxima(i + 1, (b + 1) % 2, k)
                        bank_normalize(i + 1, (b + 1) % 2, 0)
                    for k in range(3):
                        rest_of_probs(h, b, k)
                    dve.sem_inc(pt_free, 3)
                    if has_next:
                        for k in (1, 2):
                            bank_normalize(i + 1, (b + 1) % 2, k)
                    if not (last and b + 3 >= B):
                        dve.wait_ge(q_ready, i + 3)
                        cos_q(i + 3)
                    if b == 0 and not last:
                        split_wq(h + 1)

            with dve.Fori(0, HG) as h:
                steps(h, False)

            def rest_of_outputs(g, t):
                for c in range(1, OC, 2):
                    dve.wait_ge(oc_hi_ready, (g * TILES + t) * OC + (c + 1))
                    dve.tensor_tensor(oc_lo[:, c, :, :], o_t[:, 2 * c:2 * c + 2, bass.ds(t * P, P)],
                                      oc_hi[:, c, :, :].bitcast(F32), ALU.subtract).then_inc(oc_ready["dve"], 1)

            def projected(t, r):
                dve.wait_ge(proj_psum, t + 1)
                dve.tensor_copy(y_sb[:, bass.ds(t, 1), :].rearrange("p t e -> p (t e)"), ps_pt[r][:, 0:E]) \
                    .then_inc(proj_taken, 1)

            dve.sem_inc(proj_taken, 2)
            rest_of_outputs(0, 0)
            rest_of_outputs(0, 1)
            with dve.Fori(0, TILES // 2 - 1) as pair:
                for r in range(2):
                    projected(pair * 2 + r, r)
                    rest_of_outputs(0, pair * 2 + (r + 2))
            projected(TILES - 2, 0)
            projected(TILES - 1, 1)
            with dve.Fori(HG, H - 1) as h:
                steps(h, False)
            steps(H - 1, True)

            def rest_of_turned(b):
                for o in range(EO):
                    dve.wait_ge(xt2_hi, b * EO + o + 1)
                    dve.tensor_tensor(xt_lo[:, o, tok(b)], ps[turn_bank(b, o)][:], xt_hi[:, o, tok(b)].bitcast(F32),
                                      ALU.subtract).then_inc(xt2_lo, 1)

            def choose(g):
                ts = group_tiles(g)
                n = len(GROUPS[g])
                dve.wait_ge(token_psum, g + 1)
                turned = ps[TOKEN_BANK[g]][:, 0:TPB * n * 32].rearrange("p (t b c) -> p t b c", t=TPB, b=n)
                done(dve.tensor_copy(logit[:, ts, :].rearrange("p (b t) e -> p t b e", b=n), turned[:, :, :, 0:NE]))
                for t in range(ts.start, ts.stop):
                    ins = dve.max(top[:, t, :], logit[:, t, :])
                done(ins)
                for t in range(ts.start, ts.stop):
                    ins = dve.max_index(top_at[:, t, :], top[:, t, :], logit[:, t, :])
                done(ins)
                ins = dve.tensor_tensor(gap[:, ts], top[:, ts, 1], top[:, ts, 0], ALU.subtract)
                if g == len(GROUPS) - 1:
                    ins.then_inc(gap_ready, 1)
                done(dve.tensor_copy(top_f[:, ts, :], top_at[:, ts, :]))
                nt = ts.stop - ts.start
                for k in range(2):
                    ins = dve.tensor_tensor(oh[:, k, ts, :], iota_sb[:].unsqueeze(1).to_broadcast([P, nt, NE]),
                                            top_f[:, ts, k:k + 1].to_broadcast([P, nt, NE]), ALU.is_equal)
                done(ins)
                done(dve.tensor_tensor(chosen[:, ts, :], oh[:, 0, ts, :], oh[:, 1, ts, :], ALU.add))
                for t in range(ts.start, ts.stop):
                    ins = dve.tensor_tensor(prior[:, t + 1, :], prior[:, t, :], chosen[:, t, :], ALU.add)
                    if t < ts.stop - 1:
                        done(ins)
                done(ins)
                dve.sem_inc(chosen_ready, 1)

            def find_slots(g):
                ts = group_tiles(g)
                nt = ts.stop - ts.start
                dve.wait_ge(pos_psum, g + 1)
                done(dve.tensor_copy(pos_sb[:, ts, :].rearrange("p t e -> p (t e)"),
                                     ps[TOKEN_BANK[g]][:, POS_AT:POS_AT + nt * NE]))
                dve.sem_inc(pos_taken, 1)
                for k in range(2):
                    ins = dve.tensor_tensor(pos_oh[:, k, ts, :], oh[:, k, ts, :], pos_sb[:, ts, :], ALU.mult)
                done(ins)
                done(dve.tensor_reduce(pos[:, :, ts], pos_oh[:, :, ts, :], AX.X, ALU.add))
                expert_of = top_f[:, ts, 0:2].rearrange("p t k -> p k t")
                dve.scalar_tensor_tensor(slot[:, :, ts], expert_of, float(CAP), pos[:, :, ts], ALU.mult, ALU.add)
                done(dve.tensor_scalar(keep[:, :, ts], pos[:, :, ts], float(CAP), None, ALU.is_lt))
                done(dve.scalar_tensor_tensor(slot_in[:, :, ts], keep[:, :, ts], -SKIP, slot[:, :, ts],
                                              ALU.mult, ALU.add))
                dve.tensor_scalar(at_in[:, :, ts], slot_in[:, :, ts], SKIP, None, ALU.add).then_inc(slots_ready, 1)
                done(dve.tensor_scalar(pos[:, :, ts], pos[:, :, ts], float(CAP - 1), None, ALU.min))
                dve.scalar_tensor_tensor(at_out[:, :, ts], expert_of, float(CAP), pos[:, :, ts], ALU.mult, ALU.add) \
                    .then_inc(rows_known, 1)

            def add_projected(t):
                dve.wait_ge(proj_psum, TILES + t + 1)
                dve.tensor_tensor(y_sb[:, t, :], ps[5 + t % 2 * 2][:, 0:E], y_sb[:, t, :], ALU.add) \
                    .then_inc(proj_taken, 1)

            def stats_for_ln(t0, t1, src):
                for t in range(t0, t1):
                    ins = dve.bn_stats(stats[:, t, :], src[:, t, :])
                done(ins)
                for t in range(t0, t1):
                    ins = dve.bn_aggr(mv[:, t, :], stats[:, t, :])
                ins.then_inc(var2_ready, 1)

            def y_stats(b):
                dve.wait_ge(proj_taken, TILES + 2 + (b + 1) * TPB)
                stats_for_ln(b * TPB, (b + 1) * TPB, y_sb)

            def scale_and_shift(b, k):
                invert(slice(b * TPB, (b + 1) * TPB), shift, 2 * b + k + 1)

            def invert(ts, shift, nth):
                dve.wait_ge(std2_ready, nth)
                done(dve.reciprocal(rstd[:, ts], std[:, ts]))
                dve.scalar_tensor_tensor(shift[:, ts], mv[:, ts, 0], -1.0, rstd[:, ts], ALU.mult, ALU.mult) \
                    .then_inc(shift_ready, 1)

            def add_y(b):
                dve.wait_ge(x_again[b], 16)
                for t in range(TPB):
                    g = b * TPB + t
                    dve.wait_ge(y_n_ready, g + 1)
                    ins = dve.tensor_tensor(x_sb[:, g, :], x_sb[:, g, :], y_n[:, t, :], ALU.add)
                done(ins)
                stats_for_ln(b * TPB, (b + 1) * TPB, x_sb)

            dve.wait_ge(sw_in, 16)
            dve.wait_ge(o_psum, UNITS)
            dve.tensor_copy(sw_hi, sw_raw[0]).then_inc(sw_split_hi, 1)
            rest_of_outputs(1, 0)
            dve.wait_ge(sw_split_hi, 1)
            dve.tensor_tensor(sw_lo, sw_raw[0], sw_hi.bitcast(F32), ALU.subtract).then_inc(sw_split, 1)

            for t in range(TILES):
                b, k = t // TPB, t % TPB
                if t + 1 < TPB:
                    rest_of_outputs(1, t + 1)
                if k == 0 and b:
                    y_stats(b - 1)
                add_projected(t)
                if k == 0 and b >= 2:
                    scale_and_shift(b - 2, 1)
                if k == 1 and b:
                    scale_and_shift(b - 1, 0)
                if k == 2 and b:
                    add_y(b - 1)
                if k == 3 and b >= 2:
                    rest_of_turned(b - 2)
            scale_and_shift(B - 2, 1)
            y_stats(B - 1)
            choose(0)
            scale_and_shift(B - 1, 0)
            find_slots(0)

            def shared_hidden(j):
                for i in range(SH):
                    w = SHW[i]
                    dve.wait_ge(s_silu, j * SH + i + 1)
                    dve.wait_ge(s_psum_g, 2 * (j * SH + i) + 2)
                    dve.tensor_tensor(s_hid[0:w, j % 2, i, :], s_sg[0:w, i, :], ps[2 * i + 1][0:w, :],
                                      ALU.mult).then_inc(s_hid_ready, 1)

            def shared_sum(j, halves=range(2)):
                for half in halves:
                    dve.wait_ge(sy_psum, 2 * j + half + 1)
                    t = (j % B) * TPB + 2 * half
                    dst = y_sb[:, t:t + 2, :].rearrange("p t e -> p (t e)")
                    if j < B:
                        dve.tensor_copy(dst, ps[6 + half][:]).then_inc(sy_taken, 1)
                    else:
                        dve.tensor_tensor(dst, ps[6 + half][:], dst, ALU.add).then_inc(sy_taken, 1)

            shared_hidden(0)
            rest_of_turned(B - 2)
            add_y(B - 1)
            scale_and_shift(B - 1, 1)
            choose(1)
            shared_hidden(1)
            find_slots(1)
            shared_sum(0)
            rest_of_turned(B - 1)
            shared_sum(1)
            choose(2)
            shared_hidden(2)
            find_slots(2)
            shared_hidden(3)
            shared_sum(2)
            dve.wait_ge(egap_ready, 1)
            done(dve.tensor_scalar(den[:], egap[:], 1.0, None, ALU.add))
            done(dve.reciprocal(cw[:, 0, :], den[:]))
            done(dve.tensor_tensor(cw[:, 1, :], cw[:, 0, :], egap[:], ALU.mult))
            done(dve.tensor_tensor(cw[:], cw[:], keep[:], ALU.mult))
            shared_sum(3)

            def expert_rest(e):
                for k, (bank, o) in enumerate(XG_BANKS):
                    dve.wait_ge(xg_hi_ready, 3 * e + (k + 1))
                    dve.tensor_tensor(xg_dst(xg_lo, o), xg_src(bank), xg_dst(xg_hi, o).bitcast(F32),
                                      ALU.subtract).then_inc(xg_ready, 1)

            def expert_steps(e0, last):
                for r in range(2):
                    e = e0 + r
                    for c in range(2):
                        m = 2 * e + c
                        cs = slice(c * HC, (c + 1) * HC)
                        dve.wait_ge(silu_ready, 2 * m + 1)
                        dve.wait_ge(gu_psum, 3 * m + 2)
                        dve.tensor_tensor(hid[:, c, :], sg[:, c, :], ps[4][:, 0:HC], ALU.mult).then_inc(gu_free, 1)
                        dve.wait_ge(gu_free, 2 * m + 3)
                        dve.tensor_copy(hid_hi[:, cs], hid[:, c, :]).then_inc(hid_hi_ready, 1)
                        dve.wait_ge(hid_hi_ready, 2 * m + 1)
                        dve.tensor_tensor(hid_lo[:, cs], hid[:, c, :], hid_hi[:, cs].bitcast(F32),
                                          ALU.subtract).then_inc(hid_ready, 1)
                        dve.wait_ge(silu_ready, 2 * m + 2)
                        dve.tensor_tensor(hid2[0:H2, c, :], sg2[0:H2, c, :], ps[5][64:64 + H2, 0:HC],
                                          ALU.mult).then_inc(gu_free, 1)
                        dve.wait_ge(gu_free, 2 * m + 4)
                        dve.tensor_copy(hid2_both[0:H2, cs], hid2[0:H2, c, :]).then_inc(hid_hi_ready, 1)
                        dve.wait_ge(hid_hi_ready, 2 * m + 2)
                        dve.tensor_tensor(hid2_both[LO:LO + H2, cs], hid2[0:H2, c, :],
                                          hid2_both[0:H2, cs].bitcast(F32), ALU.subtract).then_inc(hid_ready, 1)
                    if not (last and r == 1):
                        expert_rest(e + 1)

            dve.sem_inc(gu_free, 2)
            dve.memset(hid2_both[32:LO, :].bitcast(F32), 0.0).then_inc(pad_ready, 1)
            dve.wait_ge(pad_ready, 1)
            expert_rest(0)
            with dve.Fori(0, NE // 2 - 1) as pair:
                expert_steps(pair * 2, False)
            expert_steps(NE - 2, True)
            dve.wait_ge(sw_in, 2 * 16)
            dve.tensor_copy(sw_hi, sw_raw[1]).then_inc(sw_split_hi, 1)
            dve.wait_ge(sw_split_hi, 2)
            dve.tensor_tensor(sw_lo, sw_raw[1], sw_hi.bitcast(F32), ALU.subtract).then_inc(sw_split, 1)

            def routed_sum(b):
                for k in range(2):
                    for t in range(b * TPB, (b + 1) * TPB):
                        g = 2 * (b * TPB) + k * TPB + t - b * TPB
                        dve.wait_ge(got_in[g % GR], 16 * (g // GR + 1))
                        if k == 1:
                            dve.wait_ge(got_used, g - TPB + 1)
                        dve.scalar_tensor_tensor(y_sb[:, t, :], got[:, g % GR, :], cw[:, k, t:t + 1], y_sb[:, t, :],
                                                 ALU.mult, ALU.add).then_inc(got_used, 1)
                dve.wait_ge(got_used, 2 * (b + 1) * TPB)

            def piece_stats(n):
                t0, t1 = LAST_LN[n]
                dve.wait_ge(sy_taken, 2 * B + t1 // 2)
                stats_for_ln(t0, t1, y_sb)

            def piece_scale(n):
                invert(slice(*LAST_LN[n]), out_shift, 2 * B + n + 1)

            shared_hidden(B)
            for b in range(B - 2):
                shared_hidden(B + b + 1)
                routed_sum(b)
                shared_sum(B + b)
                piece_stats(b)
                piece_scale(b)
            routed_sum(B - 2)
            shared_hidden(2 * B - 1)
            routed_sum(B - 1)
            shared_sum(2 * B - 2)
            piece_stats(B - 2)
            piece_scale(B - 2)
            shared_sum(2 * B - 1, [0])
            piece_stats(B - 1)
            shared_sum(2 * B - 1, [1])
            piece_stats(B)
            piece_scale(B - 1)
            piece_scale(B)
            for t in range((B - 1) * TPB, TILES):
                dve.wait_ge(out_normed, t + 1)
                dve.tensor_tensor(y_sb[:, t, :], x_sb[:, t, :], y_sb[:, t, :], ALU.add).then_inc(out_ready["dve"], 1)

        @block.gpsimd
        def _(pool):
            pool.memset(one_sb[:], 1.0)
            pool.memset(zeros, 0.0).then_inc(zeros_made, 1)
            pool.wait_ge(w0_in, 16)
            pool.tensor_copy(w0_hi, w0_raw).then_inc(w0_hi_ready, 1)
            pool.wait_ge(w0_hi_ready, 1)
            pool.tensor_tensor(w0_lo, w0_raw, w0_hi.bitcast(F32), ALU.subtract).then_inc(w0_split, 1)
            pool.wait_ge(rope_in, 32)
            for b in range(B):
                pool.wait_ge(k_swapped, b + 1)
                pool.tensor_tensor(q_sw, q_sw, sin_sb, ALU.mult).then_inc(k_sin_ready, 1)
                if b == 0:
                    pool.wait_ge(consts_in, 4 * 16)
                    pool.wait_ge(id_in, 16)
                    pool.tensor_copy(id_b[:], id_f[:])
                    pool.tensor_copy(before_b[:], before_f)
                    pool.tensor_copy(rt_hi[:], rt_raw[:]).then_inc(rt_hi_ready, 1)
                    pool.wait_ge(rt_hi_ready, 1)
                    pool.tensor_tensor(rt_lo[:], rt_raw[:], rt_hi[:].bitcast(F32), ALU.subtract)
                    for n in range(2):
                        ins = pool.tensor_copy(causal_b[:, n, :], causal_f)
                    ins.then_inc(consts_made, 1)

            def rotate(i, r):
                pool.wait_ge(q_swapped, i + 1)
                pool.tensor_tensor(q_sw, q_sw, sin_sb, ALU.mult).then_inc(q_sin_ready, 1)
                pool.wait_ge(q_cos_ready, i + 1)
                pool.wait_ge(q_sin_ready, i + 1)
                pool.tensor_tensor(q_rot[:, r, :], q_cos, q_sw, ALU.add).then_inc(q_ready, 1)

            def scale_keys(b, nth, r):
                pool.wait_ge(kh_row_in[r], 16 * nth)
                pool.tensor_tensor(k_h[:, r, :], kt[:, tok(b)], kh_row[:, r, :], ALU.mult).then_inc(kh_ready, 1)

            pool.wait_ge(kt_ready, B)
            rotate(0, 0)
            scale_keys(0, 1, 0)
            rotate(1, 1)
            scale_keys(1, 1, 1)
            pool.wait_ge(s_psum, 3)
            rotate(2, 0)

            def split_wo(h, slot):
                pool.wait_ge(wo_in, 16 * h + 16)
                at = bass.ds(slot, 1)
                pool.tensor_tensor(wo_hi[:, at, :].rearrange("p a e -> p (a e)"), wo_raw[:],
                                   one_sb[:].to_broadcast([P, E]), ALU.mult).then_inc(wo_hi_ready, 1)
                pool.wait_ge(wo_hi_ready, h + 1)
                pool.tensor_tensor(wo_lo[:, at, :].rearrange("p a e -> p (a e)"), wo_raw[:],
                                   wo_hi[:, at, :].bitcast(F32).rearrange("p a e -> p (a e)"), ALU.subtract) \
                    .then_inc(wo_ready, 1)

            def steps(h, slot, last):
                for b in range(B):
                    i = h * B + b
                    if not (last and b + 2 >= B):
                        pool.wait_ge(s_psum, 3 * i + 3)
                        scale_keys((b + 2) % B, 2 * h + (b + 2) // 2 + 1, b % 2)
                    if not (last and b + 3 >= B):
                        pool.wait_ge(s_psum, 3 * i + 6)
                        rotate(i + 3, (b + 1) % 2)
                    if b == 0:
                        split_wo(h, slot)

            def rest_of_outputs(g, t):
                for c in range(0, OC, 2 if g == 0 or (isinstance(t, int) and t < TPB) else 1):
                    pool.wait_ge(oc_hi_ready, (g * TILES + t) * OC + (c + 1))
                    pool.tensor_tensor(oc_lo[:, c, :, :], o_t[:, 2 * c:2 * c + 2, bass.ds(t * P, P)],
                                       oc_hi[:, c, :, :].bitcast(F32), ALU.subtract).then_inc(oc_ready["pool"], 1)

            with pool.Fori(0, HG) as h:
                steps(h, h, False)
            with pool.Fori(0, TILES) as t:
                rest_of_outputs(0, t)
            pool.wait_ge(proj_psum, TILES)
            with pool.Fori(HG, H - 1) as h:
                steps(h, h - HG, False)
            steps(H - 1, HG - 1, True)

            for t in range(TILES):
                rest_of_outputs(1, t)

            pool.wait_ge(slots_cleared, 4 * 16)
            for g in range(len(GROUPS)):
                ts = group_tiles(g)
                pool.wait_ge(slots_ready, g + 1)
                for t in range(ts.start, ts.stop):
                    for k in range(2):
                        pool.indirect_dma_start(
                            xg_dram[:, :], bass.IndirectOffsetOnAxis(ap=at_in[:, k, t:t + 1], axis=0), xn2[:, t, :],
                            None, bounds_check=NE * CAP - 1, oob_is_err=False).then_inc(scattered, 16)

            def split_up(e, r, first):
                hi, lo = up_hl[r]
                pool.wait_ge(up_in[r], 8 * (e - r) + 16)
                if not first:
                    pool.wait_ge(gu_free, 4 * e - 2)
                pool.tensor_copy(hi, up_raw[:, r, :, :]).then_inc(up_hi_ready, 1)
                pool.wait_ge(up_hi_ready, e + 1)
                pool.tensor_tensor(lo, up_raw[:, r, :, :], hi.bitcast(F32), ALU.subtract).then_inc(up_ready, 1)

            def rest_of_down(e, r):
                pool.wait_ge(dn_hi_ready, e + 1)
                pool.tensor_tensor(dn_lo, dn_sb[:, r, 0, :], dn_hi.bitcast(F32), ALU.subtract)
                pool.tensor_tensor(dn2_lo[0:H2, :], dn_sb[0:H2, r, 1, :], dn2_both[0:H2, :].bitcast(F32),
                                   ALU.subtract).then_inc(dn_ready, 1)

            pool.wait_ge(s_psum_g, 2 * B * SH)
            for e in range(NE + 1):
                if e < NE:
                    split_up(e, e % 2, e < 2)
                if e:
                    rest_of_down(e - 1, (e - 1) % 2)

            pool.wait_ge(scattered, 2 * TILES * 16)
            pool.wait_ge(rows_known, len(GROUPS))
            pool.wait_ge(yo_stored, 16 * NE + 16)
            for g in range(2 * TILES):
                b, k, t = g // (2 * TPB), g // TPB % 2, g % TPB + g // (2 * TPB) * TPB
                if g >= GR:
                    pool.wait_ge(got_used, g - GR + 1)
                pool.indirect_dma_start(
                    got[:, g % GR, :], None, yg_dram[:, :],
                    bass.IndirectOffsetOnAxis(ap=at_out[:, k, t:t + 1], axis=0),
                    bounds_check=NE * CAP - 1, oob_is_err=False).then_inc(got_in[g % GR], 16)

            for t in range((B - 1) * TPB):
                pool.wait_ge(out_normed, t + 1)
                pool.tensor_tensor(y_sb[:, t, :], x_sb[:, t, :], y_sb[:, t, :], ALU.add).then_inc(out_ready["pool"], 1)


def kernel(**inputs):
    import numpy as _np
    import concourse.bacc as _bacc
    from concourse import mybir as _mybir
    from concourse.bass_utils import run_bass_kernel_spmd as _run

    x, wq, wkv, wkvh, wg, wout, router, w_ug, w_dn, sw_ug, sw_dn = (_np.asarray(inputs[n]) for n in (
        "L0_attn_x", "L0_attn_Wq", "L0_attn_Wkv", "L0_attn_Wkvh", "L0_attn_Wg", "L0_attn_Wout", "L0_ffn_router",
        "L0_ffn_w_up_gate", "L0_ffn_w_down", "L0_ffn_shared_w_up_gate", "L0_ffn_shared_w_down"))
    B, SEQ, E = x.shape
    D = wkv.shape[0] // 2
    H = wq.shape[0] // D
    NE, HID = w_dn.shape[:2]
    J = sw_dn.shape[0]
    NS = 2
    EO = E // 128
    CAP = int(_np.ceil(B * SEQ * 2 / NE * 1.25))
    H2, SHID = HID - 128, J // NS

    def rows(a):
        return a.reshape(EO, 128, -1).transpose(1, 0, 2)

    ug = _np.zeros((NE, E, 2 * 128 + 64 + H2), x.dtype)
    gate, up = w_ug[:, :, :HID], w_ug[:, :, HID:]
    ug[:, :, 0:128], ug[:, :, 128:256] = gate[:, :, :128], up[:, :, :128]
    ug[:, :, 256:256 + H2], ug[:, :, 320:320 + H2] = gate[:, :, 128:], up[:, :, 128:]
    dn = _np.zeros((NE, 128, 2, E), x.dtype)
    dn[:, :, 0], dn[:, :H2, 1] = w_dn[:, :128], w_dn[:, 128:]
    tiles = [(i, min(128, SHID - i)) for i in range(0, SHID, 128)]
    sug = _np.stack([rows(_np.concatenate([sw_ug[:, q + n * SHID + i:q + n * SHID + i + w]
                                           for i, w in tiles for q in (0, J)], axis=1)) for n in range(NS)])
    sdn = _np.zeros((128, NS, len(tiles), E), x.dtype)
    for n in range(NS):
        for a, (i, w) in enumerate(tiles):
            sdn[:w, n, a] = sw_dn[n * SHID + i:n * SHID + i + w]
    pad = _np.zeros((E, 128 - 4 * H), x.dtype)
    w0 = _np.concatenate([wkv.T, wkvh.T, wg.T, pad], axis=1)

    f32 = _np.float32
    inv = (f32(10000.0) ** (-_np.arange(0, D, 2, dtype=f32) / f32(D))).astype(f32)
    ang = _np.arange(SEQ, dtype=f32)[:, None] * inv[None, :]
    cos, sin = _np.cos(ang).T, _np.sin(ang).T
    n = _np.arange(128)
    arrays = {
        "x": x.reshape(B * SEQ, E),
        "wq": wq.reshape(H, D, EO, 128).transpose(0, 3, 2, 1),
        "w0": rows(w0),
        "wout": wout.reshape(E, H, D).transpose(1, 2, 0),
        "cos_t": _np.concatenate([cos, cos]).astype(f32),
        "sin_t": _np.concatenate([-sin, sin]).astype(f32),
        "ident": _np.eye(128, dtype=f32),
        "causal": _np.where(n[None, :] > n[:, None], f32(-1e30), f32(0)).astype(f32),
        "before": (n[:, None] < n[None, :]).astype(f32),
        "iota8": _np.tile(_np.arange(NE, dtype=f32), (128, 1)),
        "router": rows(_np.concatenate([router, _np.zeros((E, 32 - NE), router.dtype)], axis=1)),
        "w_up": ug.reshape(NE, EO, 128, -1).transpose(0, 2, 1, 3),
        "w_dn": dn,
        "sw_up": sug,
        "sw_dn": sdn,
    }
    arrays = {f"in_{k}_dram": _np.ascontiguousarray(a) for k, a in arrays.items()}
    nc = _bacc.Bacc("TRN2", target_bir_lowering=False, num_devices=1)
    args = [nc.dram_tensor(k, a.shape, _mybir.dt.from_np(a.dtype), kind="ExternalInput").ap() for k, a in arrays.items()]
    out = nc.dram_tensor("out_0_dram", (B * SEQ, E), _mybir.dt.from_np(x.dtype), kind="ExternalOutput").ap()
    decoder_layer(nc, *args, out, (B, SEQ, H, D, E, NE, NS, CAP, HID, SHID))
    r = _run(nc, [arrays], core_ids=[0])
    return r.results[0]["out_0_dram"].reshape(B, SEQ, E)
```
